# Optimizing a Trainium2 kernel written in Bass

```python
import numpy as np
import jax
import jax.numpy as jnp

def _softmax(x, axis=-1):
    return jax.nn.softmax(x, axis=axis)

def _gelu(x):
    return jax.nn.gelu(x, approximate=True)

def _silu(x):
    return jax.nn.silu(x)

def _sigmoid(x):
    return jax.nn.sigmoid(x)

def _layernorm(x, axis=-1, eps=1e-05):
    m = jnp.mean(x, axis=axis, keepdims=True)
    v = jnp.var(x, axis=axis, keepdims=True)
    return (x - m) / jnp.sqrt(v + eps)

def _scatter_add(tgt, idx, src, axis=0):
    return tgt.at[idx].add(src)

def _segment_sum(src, seg, n):
    return jax.ops.segment_sum(src, seg, n)
kernel_name = 'mk_hybrid_d1_jaxref_r8_468b15'

def setup_inputs(seed: int=0):
    np.random.seed(seed)
    _w = jnp.asarray

    def _L0_attn_a_setup():
        import jax, jax.numpy as jnp
        import numpy as np
        B, S, E = (2, 256, 128)
        N_HEADS = 16
        HEAD_DIM = E // N_HEADS
        ATTN_SCALE = 1.0 / np.sqrt(E)
        ROPE_BASE = 10000.0

        def _rope(t):
            d = t.shape[-1]
            s = t.shape[-2]
            inv_freq = 1.0 / ROPE_BASE ** (jnp.arange(0, d, 2, dtype=jnp.float32) / d)
            ang = jnp.arange(s, dtype=jnp.float32)[:, None] * inv_freq[None, :]
            cos, sin = (jnp.cos(ang), jnp.sin(ang))
            tp = t.reshape(t.shape[:-1] + (d // 2, 2))
            te, to = (tp[..., 0], tp[..., 1])
            oe = te * cos - to * sin
            oo = te * sin + to * cos
            return jnp.stack([oe, oo], axis=-1).reshape(t.shape)
        key = jax.random.key(seed)
        ks = jax.random.split(key, 5)
        std = 0.02
        return {'x': jax.random.normal(ks[0], (B, S, E), dtype=jnp.float32), 'W_q': jax.random.normal(ks[1], (E, E), dtype=jnp.float32) * std, 'W_k': jax.random.normal(ks[2], (E, E), dtype=jnp.float32) * std, 'W_v': jax.random.normal(ks[3], (E, E), dtype=jnp.float32) * std, 'W_o': jax.random.normal(ks[4], (E, E), dtype=jnp.float32) * std}
    _L0_attn_a_in = _L0_attn_a_setup()

    def _L0_attn_b_setup():
        import math
        import jax, jax.numpy as jnp
        import numpy as np
        NUM_HEADS = 16
        HEAD_SIZE = 64
        HIDDEN = 128
        ROPE_BASE = 10000.0

        def _rope_cos_sin(seq_len, dim, dtype):
            inv_freq = 1.0 / ROPE_BASE ** (jnp.arange(0, dim, 2, dtype=jnp.float32) / dim)
            t = jnp.arange(seq_len, dtype=jnp.float32)
            freqs = jnp.einsum('s,d->sd', t, inv_freq)
            emb = jnp.concatenate([freqs, freqs], axis=-1)
            return (jnp.cos(emb).astype(dtype), jnp.sin(emb).astype(dtype))

        def _rotate_half(x):
            half = x.shape[-1] // 2
            return jnp.concatenate([-x[..., half:], x[..., :half]], axis=-1)

        def _apply_rope(q, k):
            cos, sin = _rope_cos_sin(q.shape[-2], q.shape[-1], q.dtype)
            q = q * cos + _rotate_half(q) * sin
            k = k * cos + _rotate_half(k) * sin
            return (q, k)
        key = jax.random.key(seed)
        ks = jax.random.split(key, 9)
        B, S = (2, 512)
        dt = jnp.bfloat16
        lim_in = 1.0 / math.sqrt(HIDDEN)
        inp = {'input_embeds': jax.random.normal(ks[0], (B, S, HIDDEN), dtype=dt), 'Wq': jax.random.uniform(ks[1], (NUM_HEADS * HEAD_SIZE, HIDDEN), dtype=dt, minval=-lim_in, maxval=lim_in), 'bq': jnp.zeros((NUM_HEADS * HEAD_SIZE,), dtype=dt), 'Wk': jax.random.uniform(ks[2], (NUM_HEADS * HEAD_SIZE, HIDDEN), dtype=dt, minval=-lim_in, maxval=lim_in), 'bk': jnp.zeros((NUM_HEADS * HEAD_SIZE,), dtype=dt), 'Wv': jax.random.uniform(ks[3], (NUM_HEADS * HEAD_SIZE, HIDDEN), dtype=dt, minval=-lim_in, maxval=lim_in), 'bv': jnp.zeros((NUM_HEADS * HEAD_SIZE,), dtype=dt), 'Wo': jax.random.uniform(ks[4], (HIDDEN, NUM_HEADS * HEAD_SIZE), dtype=dt, minval=-lim_in, maxval=lim_in), 'bo': jnp.zeros((HIDDEN,), dtype=dt)}
        return inp
    _L0_attn_b_in = _L0_attn_b_setup()

    def _L0_ffn_setup():
        import jax, jax.numpy as jnp
        import numpy as np
        B, S, DIM = (2, 256, 128)
        HID = 256
        E, NSH, TOPK = (8, 2, 2)

        def _ffn(x, w1, w2, w3):
            return jax.nn.silu(x @ w1.T) * (x @ w3.T) @ w2.T
        key = jax.random.key(seed)
        ks = jax.random.split(key, 8)
        sc = 0.02
        return {'x': jax.random.normal(ks[0], (B, S, DIM), jnp.float32), 'router_w': jax.random.normal(ks[1], (E, DIM), jnp.float32) * sc, 'expert_bias': jnp.zeros((E,), jnp.float32), 'w1': jax.random.normal(ks[2], (E, HID, DIM), jnp.float32) * sc, 'w3': jax.random.normal(ks[3], (E, HID, DIM), jnp.float32) * sc, 'w2': jax.random.normal(ks[4], (E, DIM, HID), jnp.float32) * sc, 'sw1': jax.random.normal(ks[5], (NSH, HID, DIM), jnp.float32) * sc, 'sw3': jax.random.normal(ks[6], (NSH, HID, DIM), jnp.float32) * sc, 'sw2': jax.random.normal(ks[7], (NSH, DIM, HID), jnp.float32) * sc}
    _L0_ffn_in = _L0_ffn_setup()
    _d = {'L0_attn_a_x': _L0_attn_a_in['x'], 'L0_attn_a_W_q': _L0_attn_a_in['W_q'], 'L0_attn_a_W_k': _L0_attn_a_in['W_k'], 'L0_attn_a_W_v': _L0_attn_a_in['W_v'], 'L0_attn_a_W_o': _L0_attn_a_in['W_o'], 'L0_attn_b_Wq': _L0_attn_b_in['Wq'], 'L0_attn_b_bq': _L0_attn_b_in['bq'], 'L0_attn_b_Wk': _L0_attn_b_in['Wk'], 'L0_attn_b_bk': _L0_attn_b_in['bk'], 'L0_attn_b_Wv': _L0_attn_b_in['Wv'], 'L0_attn_b_bv': _L0_attn_b_in['bv'], 'L0_attn_b_Wo': _L0_attn_b_in['Wo'], 'L0_attn_b_bo': _L0_attn_b_in['bo'], 'L0_ffn_router_w': _L0_ffn_in['router_w'], 'L0_ffn_expert_bias': _L0_ffn_in['expert_bias'], 'L0_ffn_w1': _L0_ffn_in['w1'], 'L0_ffn_w3': _L0_ffn_in['w3'], 'L0_ffn_w2': _L0_ffn_in['w2'], 'L0_ffn_sw1': _L0_ffn_in['sw1'], 'L0_ffn_sw3': _L0_ffn_in['sw3'], 'L0_ffn_sw2': _L0_ffn_in['sw2']}
    _x0 = _d['L0_attn_a_x']
    _d['L0_attn_a_x'] = jax.random.normal(jax.random.fold_in(jax.random.key(seed), 1), (2, 1024, 128), dtype=_x0.dtype)
    del _x0
    return _d

def reference(L0_attn_a_x, L0_attn_a_W_q, L0_attn_a_W_k, L0_attn_a_W_v, L0_attn_a_W_o, L0_attn_b_Wq, L0_attn_b_bq, L0_attn_b_Wk, L0_attn_b_bk, L0_attn_b_Wv, L0_attn_b_bv, L0_attn_b_Wo, L0_attn_b_bo, L0_ffn_router_w, L0_ffn_expert_bias, L0_ffn_w1, L0_ffn_w3, L0_ffn_w2, L0_ffn_sw1, L0_ffn_sw3, L0_ffn_sw2):

    def _L0_attn_a_ref(x, W_q, W_k, W_v, W_o):
        import jax, jax.numpy as jnp
        import numpy as np
        B, S, E = (2, 256, 128)
        N_HEADS = 16
        HEAD_DIM = E // N_HEADS
        ATTN_SCALE = 1.0 / np.sqrt(E)
        ROPE_BASE = 10000.0

        def _rope(t):
            d = t.shape[-1]
            s = t.shape[-2]
            inv_freq = 1.0 / ROPE_BASE ** (jnp.arange(0, d, 2, dtype=jnp.float32) / d)
            ang = jnp.arange(s, dtype=jnp.float32)[:, None] * inv_freq[None, :]
            cos, sin = (jnp.cos(ang), jnp.sin(ang))
            tp = t.reshape(t.shape[:-1] + (d // 2, 2))
            te, to = (tp[..., 0], tp[..., 1])
            oe = te * cos - to * sin
            oo = te * sin + to * cos
            return jnp.stack([oe, oo], axis=-1).reshape(t.shape)
        b, s, e = x.shape
        hd = e // N_HEADS

        def proj(w):
            return (x @ w).reshape(b, s, N_HEADS, hd).transpose(0, 2, 1, 3)
        q = _rope(proj(W_q))
        k = _rope(proj(W_k))
        v = proj(W_v)
        scores = jnp.einsum('bhsd,bhtd->bhst', q, k) * ATTN_SCALE
        causal = jnp.triu(jnp.ones((s, s), dtype=bool), k=1)
        scores = jnp.where(causal, -jnp.inf, scores)
        probs = jax.nn.softmax(scores, axis=-1)
        out = jnp.einsum('bhst,bhtd->bhsd', probs, v)
        out = out.transpose(0, 2, 1, 3).reshape(b, s, e)
        return out @ W_o

    def _L0_attn_b_ref(input_embeds, Wq, bq, Wk, bk, Wv, bv, Wo, bo):
        import math
        import jax, jax.numpy as jnp
        import numpy as np
        NUM_HEADS = 16
        HEAD_SIZE = 64
        HIDDEN = 128
        ROPE_BASE = 10000.0

        def _rope_cos_sin(seq_len, dim, dtype):
            inv_freq = 1.0 / ROPE_BASE ** (jnp.arange(0, dim, 2, dtype=jnp.float32) / dim)
            t = jnp.arange(seq_len, dtype=jnp.float32)
            freqs = jnp.einsum('s,d->sd', t, inv_freq)
            emb = jnp.concatenate([freqs, freqs], axis=-1)
            return (jnp.cos(emb).astype(dtype), jnp.sin(emb).astype(dtype))

        def _rotate_half(x):
            half = x.shape[-1] // 2
            return jnp.concatenate([-x[..., half:], x[..., :half]], axis=-1)

        def _apply_rope(q, k):
            cos, sin = _rope_cos_sin(q.shape[-2], q.shape[-1], q.dtype)
            q = q * cos + _rotate_half(q) * sin
            k = k * cos + _rotate_half(k) * sin
            return (q, k)
        B, S, _ = input_embeds.shape
        q = input_embeds @ Wq.T + bq
        k = input_embeds @ Wk.T + bk
        v = input_embeds @ Wv.T + bv

        def split_heads(x):
            return x.reshape(B, S, NUM_HEADS, HEAD_SIZE).transpose(0, 2, 1, 3)
        q, k, v = (split_heads(q), split_heads(k), split_heads(v))
        q, k = _apply_rope(q, k)
        scale = 1.0 / math.sqrt(HEAD_SIZE)
        scores = jnp.einsum('bhqd,bhkd->bhqk', q, k) * scale
        attn = jax.nn.softmax(scores, axis=-1)
        out = jnp.einsum('bhqk,bhkd->bhqd', attn, v)
        out = out.transpose(0, 2, 1, 3).reshape(B, S, NUM_HEADS * HEAD_SIZE)
        return out @ Wo.T + bo

    def _L0_ffn_ref(x, router_w, expert_bias, w1, w3, w2, sw1, sw3, sw2):
        import jax, jax.numpy as jnp
        import numpy as np
        B, S, DIM = (2, 256, 128)
        HID = 256
        E, NSH, TOPK = (8, 2, 2)

        def _ffn(x, w1, w2, w3):
            return jax.nn.silu(x @ w1.T) * (x @ w3.T) @ w2.T
        bs, sl, d = x.shape
        xf = x.reshape(-1, d)
        shared = jnp.zeros_like(xf)
        for i in range(sw1.shape[0]):
            shared = shared + _ffn(xf, sw1[i], sw2[i], sw3[i])
        logits = xf @ router_w.T + expert_bias
        rw, sel = jax.lax.top_k(logits, TOPK)
        rw = jax.nn.softmax(rw.astype(jnp.float32), axis=-1).astype(x.dtype)
        onehot = jax.nn.one_hot(sel, E, dtype=x.dtype)
        combine = jnp.einsum('tk,tke->te', rw, onehot)

        def body(acc, ew):
            e1, e3, e2, cw = ew
            acc = acc + cw[:, None] * _ffn(xf, e1, e2, e3)
            return (acc, None)
        out, _ = jax.lax.scan(body, jnp.zeros_like(xf), (w1, w3, w2, combine.T))
        out = out + shared
        return out.reshape(bs, sl, -1)
    x = L0_attn_a_x
    x = x + _L0_attn_a_ref(_layernorm(x, axis=-1), L0_attn_a_W_q, L0_attn_a_W_k, L0_attn_a_W_v, L0_attn_a_W_o)
    x = x + _L0_ffn_ref(_layernorm(x, axis=-1), L0_ffn_router_w, L0_ffn_expert_bias, L0_ffn_w1, L0_ffn_w3, L0_ffn_w2, L0_ffn_sw1, L0_ffn_sw3, L0_ffn_sw2)
    x = x + _L0_attn_b_ref(_layernorm(x, axis=-1), L0_attn_b_Wq, L0_attn_b_bq, L0_attn_b_Wk, L0_attn_b_bk, L0_attn_b_Wv, L0_attn_b_bv, L0_attn_b_Wo, L0_attn_b_bo)
    x = x + _L0_ffn_ref(_layernorm(x, axis=-1), L0_ffn_router_w, L0_ffn_expert_bias, L0_ffn_w1, L0_ffn_w3, L0_ffn_w2, L0_ffn_sw1, L0_ffn_sw3, L0_ffn_sw2)
    return x

_drawn_inputs = setup_inputs


def setup_inputs(seed=0):
    import zlib

    import numpy as np

    out = dict(_drawn_inputs(seed))
    spreads = {'L0_attn_b_bq': (0.0, 0.8),
     'L0_attn_b_bk': (0.0, 0.8),
     'L0_attn_b_bv': (0.0, 0.1),
     'L0_attn_b_bo': (0.0, 0.1),
     'L0_ffn_expert_bias': (0.0, 0.8)}
    factors = {'L0_attn_a_W_q': 8.0,
     'L0_attn_a_W_k': 8.0,
     'L0_attn_a_W_v': 8.0,
     'L0_attn_a_W_o': 8.0,
     'L0_attn_b_Wq': 3.021,
     'L0_attn_b_Wk': 3.011,
     'L0_ffn_router_w': 6.076,
     'L0_ffn_w1': 5.05,
     'L0_ffn_w3': 5.041,
     'L0_ffn_w2': 5.05}
    for name, (base, spread) in spreads.items():
        noise = np.random.default_rng([zlib.crc32(name.encode()), seed]).standard_normal(out[name].shape)
        drawn = base * np.exp(spread * noise) if base else spread * noise
        out[name] = jnp.asarray(drawn.astype(out[name].dtype))
    for name, factor in factors.items():
        out[name] = (out[name] * factor).astype(out[name].dtype)
    return out
```

```python
import concourse.bass as bass
from concourse import mybir
from contextlib import ExitStack

P = 128
B, S, E = 2, 1024, 128
N = B * S
NT = N // P
QT = S // P
EPS = 1e-5
HA, DA = 16, 8
HB, DB = 16, 64
U = B * HA
VA = 2 * DA + 1
NE, NX, HID = 8, 10, 256
MASKED = -1.0e30
BIG = 3.0e38
C = 512

f32 = mybir.dt.float32
f32r = mybir.dt.float32r
bf16 = mybir.dt.bfloat16
ALU = mybir.AluOpType
ACT = mybir.ActivationFunctionType
AX = mybir.AxisListType


def before(it, k):
    return (it, k - 1) if k else (it - 1, 15)


def words(ap):
    return ap.bitcast(f32)


def hold(eng, tally):
    eng.sem_inc(tally, 1)


def flat(ap):
    return ap.rearrange("p a b -> p (a b)")


class Chain:

    def __init__(self, eng, sem):
        self.eng, self.sem, self.n = eng, sem, 0

    def step(self, ins):
        self.n += 1
        ins.then_inc(self.sem, 1)

    def wait(self):
        self.eng.wait_ge(self.sem, self.n)

    def then(self, ins):
        self.step(ins)
        self.wait()


def layernorm_transposed(nc, tag, X, xh, xl, ident, PS, XN=None):
    with ExitStack() as c:
        sb = lambda n, s, d: c.enter_context(nc.sbuf_tensor(f"{tag}_{n}", s, d))
        sem = lambda n: c.enter_context(nc.semaphore(f"{tag}_{n}"))
        cen = sb("cen", [P, NT, E], f32)
        sq = sb("sq", [P, NT, E], f32)
        st = sb("st", [P, 8, NT], f32)
        eps = sb("eps", [P, 1], f32)
        dve_done, var_ready, root_ready, norm_ready, tr_ready, hi_ready = (
            sem(n) for n in ("dve_done", "var_ready", "root_ready", "norm_ready", "tr_ready", "hi_ready"))
        block = c.enter_context(nc.Block())
        wide = lambda a: a.unsqueeze(2).broadcast_to([P, NT, E])

        @block.vector
        def _(dve):
            ch = Chain(dve, dve_done)
            tot, mean, var, root, half, rstd, t = (st[:, i, :] for i in range(7))
            ch.step(nc.vector.memset(eps[:, :], EPS))
            ch.then(nc.vector.tensor_reduce(tot, X[:, :, :], AX.X, ALU.add))
            ch.then(nc.vector.tensor_scalar(mean, tot, 1.0 / E, None, ALU.mult))
            ch.then(nc.vector.tensor_tensor(cen[:, :, :], X[:, :, :], wide(mean), ALU.subtract))
            ch.then(nc.vector.tensor_tensor(sq[:, :, :], cen[:, :, :], cen[:, :, :], ALU.mult))
            ch.then(nc.vector.tensor_reduce(tot, sq[:, :, :], AX.X, ALU.add))
            nc.vector.tensor_scalar(var, tot, 1.0 / E, EPS, ALU.mult, ALU.add).then_inc(var_ready, 1)
            dve.wait_ge(root_ready, 1)
            ch.then(nc.vector.reciprocal(rstd, root))
            ch.then(nc.vector.tensor_tensor(t, rstd, rstd, ALU.mult))
            ch.then(nc.vector.tensor_tensor(half, t, var, ALU.mult))
            ch.then(nc.vector.tensor_scalar(t, half, -0.5, 1.5, ALU.mult, ALU.add))
            ch.then(nc.vector.tensor_tensor(half, t, rstd, ALU.mult))
            nc.vector.tensor_tensor(sq[:, :, :], cen[:, :, :], wide(half), ALU.mult).then_inc(norm_ready, 1)
            for g in range(4):
                dve.wait_ge(hi_ready, g + 1)
                nc.vector.tensor_tensor(xl[:, g * C:(g + 1) * C], PS[:, g, :], xh[:, g * C:(g + 1) * C], ALU.subtract)

        @block.scalar
        def _(act):
            act.wait_ge(var_ready, 1)
            nc.scalar.activation(st[:, 3, :], st[:, 2, :], ACT.Sqrt).then_inc(root_ready, 1)
            for g in range(4):
                act.wait_ge(tr_ready, g + 1)
                nc.scalar.activation(xh[:, g * C:(g + 1) * C], PS[:, g, :], ACT.Copy).then_inc(hi_ready, 1)

        @block.tensor
        def _(pe):
            pe.wait_ge(norm_ready, 1)
            for g in range(4):
                for a in range(4):
                    ins = nc.tensor.transpose(PS[:, g, a * P:(a + 1) * P], sq[:, g * 4 + a, :], ident[:, :])
                ins.then_inc(tr_ready, 1)


def attention_core(nc, tag, c, PS, ident, causal, DQK):
    class A: pass
    A = A()
    sb = lambda n, s, d: c.enter_context(nc.sbuf_tensor(f"{tag}_{n}", s, d))
    sem = lambda n: c.enter_context(nc.semaphore(f"{tag}_{n}"))
    vm = VA if causal else P
    QS = A.QS = [sb(f"QS{j}", [P, S], f32r) for j in range(2)]
    K1 = A.K1 = [sb(f"K1{j}", [P, S], f32r) for j in range(2)]
    K2 = A.K2 = None if causal else [sb(f"K2{j}", [P, S], f32r) for j in range(2)]
    V = A.V = [sb(f"V{j}", [P, QT, vm], f32r) for j in range(2)]
    prob = [sb(f"prob{j}", [P, S], f32) for j in range(2)]
    PTh = sb("PTh", [P, QT, C], f32r)
    PTl = sb("PTl", [P, QT, C], f32r)
    nmax = sb("nmax", [P, 4], f32)
    A.rsum = sb("rsum", [P, 2, QT], f32)
    A.OT = [sb(f"OT{j}", [vm, S], f32) for j in range(2)]
    A.s_ready, A.max_ready, A.p_ready, A.t_ready, A.ph_ready, A.pl_ready, A.pv_ready, A.o_ready = (
        sem(n) for n in ("s_ready", "max_ready", "p_ready", "t_ready", "ph_ready", "pl_ready", "pv_ready", "o_ready"))
    PL0, O0 = 2, 1
    halves = [[(4 * h, min(4 * h + 4, qt + 1 if causal else QT)) for h in range(2) if not causal or 4 * h <= qt]
              for qt in range(QT)]
    halves_before = [sum(len(halves[k % QT]) for k in range(n)) for n in range(2 * QT + 1)]
    HP = halves_before[2 * QT]
    width = lambda qt: (qt + 1) * P if causal else S
    bank = lambda k: PS[:, 2 * (k % 2):2 * (k % 2) + 2, :]
    A.credits = (PL0, O0)

    def scores(it, k, maskr=None, identr=None, loaded=None):
        if k % QT == 0 and loaded:
            loaded(it, k)
        j, qt = (k // QT) % 2, k % QT
        q = QS[j][:, qt * P:(qt + 1) * P]
        w = width(qt)
        for h in range((w + C - 1) // C):
            n = min(C, w - h * C)
            out = PS[:, 2 * (k % 2) + h, 0:n]
            last = h == (w + C - 1) // C - 1
            ins = nc.tensor.matmul(out, q, K1[j][:, h * C:h * C + n], start=True, stop=causal and not last)
            if not causal:
                ins = nc.tensor.matmul(out, q, K2[j][:, h * C:h * C + n], start=False, stop=True)
            elif last:
                ins = nc.tensor.matmul(PS[:, 2 * (k % 2) + h, n - P:n], identr[:, :], maskr[:, :], start=False, stop=True)
        ins.then_inc(A.s_ready, 1)

    def transposes(pe, it, k):
        pe.wait_ge(A.p_ready, it * 16 + k + 1)
        for i, (a, b) in enumerate(halves[k % QT]):
            m = halves_before[k] + i
            pe.wait_ge(A.pl_ready, it * HP + m + PL0 - 1)
            for kt in range(a, b):
                ins = nc.tensor.transpose(PS[:, 4 + m % 2, (kt - a) * P:(kt - a + 1) * P],
                                          prob[k % 2][:, kt * P:(kt + 1) * P], ident[:, :])
            ins.then_inc(A.t_ready, 1)

    def values(pe, it, k):
        j, g = k // QT, (k % QT) // 4
        pe.wait_ge(A.pl_ready, it * HP + halves_before[k + 1] + PL0)
        pe.wait_ge(A.o_ready, it * 4 + 2 * j + g + O0)
        nk = 4 * g + 4 if causal else QT
        for kt in range(nk):
            q0 = max(0, kt - 4 * g) * P if causal else 0
            for part in (PTh, PTl):
                ins = nc.tensor.matmul(PS[0:vm, 6, q0:C], V[j][:, kt, :], part[:, kt, q0:C],
                                       start=kt == 0 and part is PTh, stop=kt == nk - 1 and part is PTl)
        ins.then_inc(A.pv_ready, 1)

    def maximum(dve, it, k):
        dve.wait_ge(A.s_ready, it * 16 + k + 1)
        w = width(k % QT)
        src = flat(bank(k))[:, 0:w]
        nc.vector.tensor_reduce(nmax[:, k % 4:k % 4 + 1], src, AX.X, ALU.max, negate=True).then_inc(A.max_ready, 1)

    def exponent(act, it, k):
        act.wait_ge(A.max_ready, it * 16 + k + 1)
        w = width(k % QT)
        kw = {} if causal else {"accum_out": A.rsum[:, (k // QT) % 2, k % QT:k % QT + 1]}
        nc.scalar.activation(prob[k % 2][:, 0:w], flat(bank(k))[:, 0:w], ACT.Exp,
                             bias=nmax[:, k % 4:k % 4 + 1], scale=1.0, **kw).then_inc(A.p_ready, 1)

    def part(k, buf, a, b):
        return buf[:, a:b, (k % 4) * P:(k % 4 + 1) * P]

    def src(m, a, b):
        return PS[:, 4 + m % 2, 0:(b - a) * P].rearrange("p (a q) -> p a q", q=P)

    def high_parts(act, it, k):
        for i, (a, b) in enumerate(halves[k % QT]):
            m = halves_before[k] + i
            act.wait_ge(A.t_ready, it * HP + m + 1)
            nc.scalar.activation(part(k, PTh, a, b), src(m, a, b), ACT.Copy).then_inc(A.ph_ready, 1)

    def low_parts(dve, it, k):
        for i, (a, b) in enumerate(halves[k % QT]):
            m = halves_before[k] + i
            dve.wait_ge(A.ph_ready, it * HP + m + 1)
            nc.vector.tensor_tensor(part(k, PTl, a, b), src(m, a, b), part(k, PTh, a, b),
                                    ALU.subtract).then_inc(A.pl_ready, 1)

    def output(act, it, k, free=None):
        j, g = k // QT, (k % QT) // 4
        act.wait_ge(A.pv_ready, it * 4 + 2 * j + g + 1)
        if free and g == 0:
            free(it, j)
        nc.scalar.activation(A.OT[j][:, g * C:(g + 1) * C], PS[0:vm, 6, :], ACT.Copy).then_inc(A.o_ready, 1)

    A.scores, A.transposes, A.values, A.maximum, A.exponent = scores, transposes, values, maximum, exponent
    A.high_parts, A.low_parts, A.output = high_parts, low_parts, output
    return A


def attention_a(nc, X, xh, xl, ident, identr, maskr, PS, d):
    qk_dram = nc.dram_tensor("qk_a", [2, U, 2, DA, S], f32r, kind="Internal").ap()
    o_dram = nc.dram_tensor("o_a", [U, VA, S], f32, kind="Internal").ap()
    outer = ExitStack()
    with outer:
        Va = outer.enter_context(nc.sbuf_tensor("Va", [P, U, QT, VA], f32r))
        with ExitStack() as c:
            sb = lambda n, s, t: c.enter_context(nc.sbuf_tensor(f"pa_{n}", s, t))
            sem = lambda n: c.enter_context(nc.semaphore(f"pa_{n}"))
            W = sb("W", [P, 5, P], f32)
            Wh = sb("Wh", [P, 5, P], f32r)
            Wl = sb("Wl", [P, 5, P], f32r)
            tab = sb("tab", [P, 4, S], f32)
            T = [sb(f"T{i}", [P, C], f32) for i in range(2)]
            rot = [sb(f"rot{i}", [P, C], f32) for i in range(2)]
            qkh = sb("qkh", [P, 2, N], f32r)
            qkl = sb("qkl", [P, 2, N], f32r)
            ld, split, mm, dve_done, mid, va_hi, qk_done, st = (
                sem(n) for n in ("ld", "split", "mm", "dve_done", "mid", "va_hi", "qk_done", "st"))
            block = c.enter_context(nc.Block())

            @block.sync
            def _(sp):
                sp.dma_start(W[:, :, :], d["a_w"].rearrange("k e f -> e k f")).then_inc(ld, 16)
                sp.dma_start(tab[:, :, :], d["a_tab"].rearrange("k f s -> f k s")).then_inc(ld, 16)
                for w in range(2):
                    sp.wait_ge(qk_done, 4 * (w + 1))
                    for prt, src in enumerate((qkh, qkl)):
                        for b in range(B):
                            sp.dma_start(words(qk_dram[w, b * HA:(b + 1) * HA, prt]),
                                         words(src[:, w, b * S:(b + 1) * S])).then_inc(st, 16)
                sp.wait_ge(st, 16 * 8)

            @block.tensor
            def _(pe):
                pe.wait_ge(split, 2)
                n = 0
                for w in range(2):
                    for t in range(4):
                        for r in range(2):
                            if n >= 4:
                                pe.wait_ge(mid, n // 2 - 1)
                            bk = PS[:, (n % 4), :]
                            i = 2 * w + r
                            x = slice(t * C, (t + 1) * C)
                            nc.tensor.matmul(bk, Wh[:, i, :], xl[:, x], start=True, stop=False)
                            nc.tensor.matmul(bk, Wl[:, i, :], xh[:, x], start=False, stop=False)
                            nc.tensor.matmul(bk, Wh[:, i, :], xh[:, x], start=False, stop=True).then_inc(mm, 1)
                            n += 1
                for t in range(NT):
                    bk = PS[:, 4 + t // 4, (t % 4) * P:(t % 4 + 1) * P]
                    x = slice(t * P, (t + 1) * P)
                    nc.tensor.matmul(bk, xl[:, x], Wh[:, 4, :], start=True, stop=False)
                    nc.tensor.matmul(bk, xh[:, x], Wl[:, 4, :], start=False, stop=False)
                    ins = nc.tensor.matmul(bk, xh[:, x], Wh[:, 4, :], start=False, stop=True)
                    if t % 4 == 3:
                        ins.then_inc(mm, 1)

            @block.vector
            def _(dve):
                ch = Chain(dve, dve_done)
                dve.wait_ge(ld, 32)
                nc.vector.tensor_copy(Wh[:, :, :], W[:, :, :]).then_inc(split, 1)
                dve.wait_ge(split, 1)
                nc.vector.tensor_tensor(Wl[:, :, :], W[:, :, :], Wh[:, :, :], ALU.subtract).then_inc(split, 1)
                ch.step(nc.vector.memset(Va[:, :, :, 2 * DA:VA].bitcast(f32), 1.0))
                for w in range(2):
                    for t in range(4):
                        n = 8 * w + 2 * t
                        dve.wait_ge(mm, n + 2)
                        s0 = (t % 2) * C
                        ch.step(nc.vector.tensor_tensor(T[0][:, :], PS[:, n % 4, :], tab[:, 2 * w, s0:s0 + C], ALU.mult))
                        nc.vector.tensor_tensor(T[1][:, :], PS[:, n % 4 + 1, :], tab[:, 2 * w + 1, s0:s0 + C],
                                                ALU.mult).then_inc(mid, 1)
                        ch.wait()
                        dve.wait_ge(mid, 4 * w + t + 1)
                        x = slice(t * C, (t + 1) * C)
                        ch.then(nc.vector.tensor_tensor(rot[0][:, :], T[0][:, :], T[1][:, :], ALU.add))
                        ch.then(nc.vector.tensor_copy(qkh[:, w, x], rot[0][:, :]))
                        nc.vector.tensor_tensor(qkl[:, w, x], rot[0][:, :], qkh[:, w, x], ALU.subtract).then_inc(qk_done, 1)
                        dve.wait_ge(qk_done, 4 * w + t + 1)
                for g in range(4):
                    dve.wait_ge(va_hi, 4 * (g + 1))
                    for a in range(4):
                        t = 4 * g + a
                        b, kt = t // QT, t % QT
                        v = Va[:, b * HA:(b + 1) * HA, kt, :]
                        nc.vector.tensor_tensor(v[:, :, DA:2 * DA],
                                                PS[:, 4 + g, a * P:(a + 1) * P].rearrange("p (h d) -> p h d", d=DA),
                                                v[:, :, 0:DA], ALU.subtract)

            @block.scalar
            def _(act):
                for g in range(4):
                    act.wait_ge(mm, 16 + g + 1)
                    for a in range(4):
                        t = 4 * g + a
                        b, kt = t // QT, t % QT
                        nc.scalar.activation(Va[:, b * HA:(b + 1) * HA, kt, 0:DA],
                                             PS[:, 4 + g, a * P:(a + 1) * P].rearrange("p (h d) -> p h d", d=DA),
                                             ACT.Copy).then_inc(va_hi, 1)

        with ExitStack() as c:
            sem = lambda n: c.enter_context(nc.semaphore(f"aa_{n}"))
            A = attention_core(nc, "aa", c, PS, ident, True, DA)
            PL0, O0 = A.credits
            zero_ready, st = sem("zero_ready"), sem("st")
            qk_ld = [sem(f"qk_ld{j}") for j in range(2)]
            v_ld = [sem(f"v_ld{j}") for j in range(2)]
            o_st = [sem(f"o_st{j}") for j in range(2)]
            NP = U // 2

            def load_qk(sp, u, j):
                for r in range(2):
                    sp.dma_start(words(A.QS[j][16 * r:16 * r + 16, :]),
                                 words(qk_dram[0, u].rearrange("r d s -> (r d) s"))).then_inc(qk_ld[j], 16)
                for r in range(4):
                    sp.dma_start(words(A.K1[j][8 * r:8 * r + 8, :]), words(qk_dram[1, u, r // 2])).then_inc(qk_ld[j], 16)

            def load_v(sp, u, j):
                sp.dma_start(words(A.V[j][:, :, :]), words(Va[:, u, :, :])).then_inc(v_ld[j], 16)

            block = c.enter_context(nc.Block())

            def each_pair(eng, body):
                body(0, True, False)
                with eng.Fori(1, NP - 1) as it:
                    body(it, False, False)
                body(NP - 1, False, True)

            @block.sync
            def _(sp):
                sp.wait_ge(zero_ready, 4)
                for j in range(2):
                    load_qk(sp, j, j)
                    load_v(sp, j, j)

                def body(it, first, last):
                    for j in range(2):
                        u = it * 2 + j
                        if not last:
                            sp.wait_ge(A.s_ready, it * 16 + 8 * j + 8)
                            load_qk(sp, u + 2, j)
                            sp.wait_ge(A.pv_ready, it * 4 + 2 * j + 2)
                            load_v(sp, u + 2, j)
                        sp.wait_ge(A.o_ready, it * 4 + 2 * j + 2 + O0)
                        sp.dma_start(o_dram[u], A.OT[j][:, :]).then_inc(o_st[j], 16)
                each_pair(sp, body)
                for j in range(2):
                    sp.wait_ge(o_st[j], 16 * (NP + 1))

            @block.gpsimd
            def _(pool):
                for j in range(2):
                    nc.gpsimd.memset(A.QS[j][:, :].bitcast(f32), 0.0).then_inc(zero_ready, 1)
                    nc.gpsimd.memset(A.K1[j][:, :].bitcast(f32), 0.0).then_inc(zero_ready, 1)

            @block.tensor
            def _(pe):
                def loaded(it, k):
                    j = (k // QT) % 2
                    pe.wait_ge(qk_ld[j], 96 * (it + k // 16 + 1))

                def values(it, k):
                    if k % 8 == 3:
                        pe.wait_ge(v_ld[k // QT], 16 * (it + 1))
                    A.values(pe, it, k)

                sc = lambda it, k: A.scores(it, k, maskr, identr, loaded)
                sc(0, 0)
                sc(0, 1)

                def body(it, first, last):
                    for k in range(16):
                        if not last or k < 14:
                            pe.wait_ge(A.p_ready, it * 16 + k + 1)
                            sc(it, k + 2)
                        if k % 4 == 0 and not (first and k == 0):
                            values(*before(it, k))
                        A.transposes(pe, it, k)
                each_pair(pe, body)
                values(NP - 1, 15)

            @block.scalar
            def _(act):
                def free(it, j):
                    act.wait_ge(o_st[j], 16 * (it + 1))

                A.exponent(act, 0, 0)

                def body(it, first, last):
                    for k in range(16):
                        if not last or k < 15:
                            A.exponent(act, it, k + 1)
                        if k % 4 == 0 and not (first and k == 0):
                            A.output(act, *before(it, k), free)
                        A.high_parts(act, it, k)
                each_pair(act, body)
                A.output(act, NP - 1, 15, free)

            @block.vector
            def _(dve):
                nc.vector.memset(A.rsum[:, 0, 0:1], 0.0).then_inc(A.pl_ready, PL0)
                nc.vector.memset(A.rsum[:, 0, 1:2], 0.0).then_inc(A.o_ready, O0)
                for j in range(2):
                    nc.vector.memset(A.rsum[:, 1, j:j + 1], 0.0).then_inc(o_st[j], 16)
                A.maximum(dve, 0, 0)
                A.maximum(dve, 0, 1)

                def body(it, first, last):
                    for k in range(16):
                        if not last or k < 14:
                            A.maximum(dve, it, k + 2)
                        A.low_parts(dve, it, k)
                each_pair(dve, body)

    with ExitStack() as c:
        sb = lambda n, s, t: c.enter_context(nc.sbuf_tensor(f"oa_{n}", s, t))
        sem = lambda n: c.enter_context(nc.semaphore(f"oa_{n}"))
        oh = sb("oh", [P, B, S], f32)
        ol = sb("ol", [P, B, S], f32)
        den = sb("den", [P, B, S], f32)
        Wo = sb("Wo", [P, P], f32)
        ld, dve_done, o_norm, mm = (sem(n) for n in ("ld", "dve_done", "o_norm", "mm"))
        block = c.enter_context(nc.Block())

        @block.sync
        def _(sp):
            sp.dma_start(Wo[:, :], d["a_wo"]).then_inc(ld, 16)
            for b in range(B):
                us = slice(b * HA, (b + 1) * HA)
                heads = lambda tile: tile[:, b, :]
                sp.dma_start(heads(oh), o_dram[us, 0:DA]).then_inc(ld, 16)
                sp.dma_start(heads(ol), o_dram[us, DA:2 * DA]).then_inc(ld, 16)
                sp.dma_start(heads(den), o_dram[us, 2 * DA:VA].broadcast_to([HA, DA, S])).then_inc(ld, 16)

        @block.vector
        def _(dve):
            ch = Chain(dve, dve_done)
            dve.wait_ge(ld, 16 * (1 + 3 * B))
            ch.step(nc.vector.reciprocal(flat(den[:, :, :]), flat(den[:, :, :])))
            ch.then(nc.vector.tensor_tensor(flat(oh[:, :, :]), flat(oh[:, :, :]), flat(ol[:, :, :]), ALU.add))
            nc.vector.tensor_tensor(flat(ol[:, :, :]), flat(oh[:, :, :]), flat(den[:, :, :]), ALU.mult).then_inc(o_norm, 1)
            for g in range(4):
                dve.wait_ge(mm, g + 1)
                x = flat(X[:, 4 * g:4 * g + 4, :])
                nc.vector.tensor_tensor(x, x, PS[:, g, :], ALU.add)

        @block.tensor
        def _(pe):
            pe.wait_ge(o_norm, 1)
            for t in range(NT):
                ins = nc.tensor.matmul(PS[:, t // 4, (t % 4) * P:(t % 4 + 1) * P],
                                       flat(ol[:, :, :])[:, t * P:(t + 1) * P], Wo[:, :], start=True, stop=True)
                if t % 4 == 3:
                    ins.then_inc(mm, 1)


def router(nc, tag, xh, xl, PS, d, ident, cw_dram):
    with ExitStack() as c:
        sb = lambda n, s, t: c.enter_context(nc.sbuf_tensor(f"{tag}_{n}", s, t))
        sem = lambda n: c.enter_context(nc.semaphore(f"{tag}_{n}"))
        rw = sb("rw", [P, NE], f32)
        rwh = sb("rwh", [P, NE], f32r)
        rwl = sb("rwl", [P, NE], f32r)
        bias = sb("bias", [P, NE], f32)
        rank = sb("rank", [P, NE], f32)
        W = {n: sb(n, [P, NT, NE], f32) for n in ("lg", "lg2", "eq", "cand", "one1", "one2", "cmb")}
        v = sb("v", [P, 8, NT], f32)
        cT = sb("cT", [P, P], f32)
        ones = sb("ones", [NX - NE, N], f32)
        ld, split, mm, dve_done, dif_ready, exp_ready, cmb_ready, tr, cT_ready, ones_ready, st = (
            sem(n) for n in ("ld", "split", "mm", "dve_done", "dif_ready", "exp_ready", "cmb_ready", "tr", "cT_ready", "ones_ready", "st"))
        block = c.enter_context(nc.Block())
        wide = lambda a: a.unsqueeze(2).broadcast_to([P, NT, NE])
        rows = lambda a: a.unsqueeze(1).broadcast_to([P, NT, NE])

        @block.sync
        def _(sp):
            sp.dma_start(rw[:, :], d["router"]).then_inc(ld, 16)
            sp.dma_start(bias[:, :], d["ebias"].broadcast_to([P, NE])).then_inc(ld, 16)
            sp.dma_start(rank[:, :], d["rank"].broadcast_to([P, NE])).then_inc(ld, 16)
            sp.wait_ge(ones_ready, 1)
            sp.dma_start(cw_dram[NE:NX, :], ones[:, :]).then_inc(st, 16)
            sp.wait_ge(cT_ready, 1)
            for t in range(NT):
                sp.dma_start(cw_dram[0:NE, t * P:(t + 1) * P], cT[t * NE:(t + 1) * NE, :]).then_inc(st, 16)
            sp.wait_ge(st, 16 * (NT + 1))

        @block.gpsimd
        def _(pool):
            nc.gpsimd.memset(ones[:, :], 1.0).then_inc(ones_ready, 1)

        @block.tensor
        def _(pe):
            pe.wait_ge(split, 2)
            for t in range(NT):
                o = PS[:, 0, t * NE:(t + 1) * NE]
                x = slice(t * P, (t + 1) * P)
                nc.tensor.matmul(o, xl[:, x], rwl[:, :], start=True, stop=False)
                nc.tensor.matmul(o, xl[:, x], rwh[:, :], start=False, stop=False)
                nc.tensor.matmul(o, xh[:, x], rwl[:, :], start=False, stop=False)
                ins = nc.tensor.matmul(o, xh[:, x], rwh[:, :], start=False, stop=True)
            ins.then_inc(mm, 1)
            pe.wait_ge(cmb_ready, 1)
            nc.tensor.transpose(PS[:, 1, 0:P], flat(W["cmb"][:, :, :]), ident[:, :]).then_inc(tr, 1)

        @block.scalar
        def _(act):
            act.wait_ge(dif_ready, 1)
            nc.scalar.activation(v[:, 3, :], v[:, 2, :], ACT.Exp).then_inc(exp_ready, 1)

        @block.vector
        def _(dve):
            ch = Chain(dve, dve_done)
            lg, lg2, eq, cand, one1, one2, cmb = (W[n][:, :, :] for n in ("lg", "lg2", "eq", "cand", "one1", "one2", "cmb"))
            m1, m2, dif, e, den, w1, w2, top = (v[:, i, :] for i in range(8))
            tt = nc.vector.tensor_tensor
            dve.wait_ge(ld, 48)
            nc.vector.tensor_copy(rwh[:, :], rw[:, :]).then_inc(split, 1)
            dve.wait_ge(split, 1)
            tt(rwl[:, :], rw[:, :], rwh[:, :], ALU.subtract).then_inc(split, 1)
            dve.wait_ge(mm, 1)
            ch.then(tt(lg, PS[:, 0, 0:NT * NE].rearrange("p (t e) -> p t e", e=NE), rows(bias[:, :]), ALU.add))

            def pick(scores, mx, one):
                ch.then(nc.vector.tensor_reduce(mx, scores, AX.X, ALU.max))
                ch.then(tt(eq, scores, wide(mx), ALU.is_equal))
                ch.then(tt(cand, eq, rows(rank[:, :]), ALU.mult))
                ch.then(nc.vector.tensor_reduce(top, cand, AX.X, ALU.max))
                ch.then(tt(one, rows(rank[:, :]), wide(top), ALU.is_equal))

            pick(lg, m1, one1)
            ch.then(nc.vector.scalar_tensor_tensor(lg2, one1, -BIG, lg, ALU.mult, ALU.add))
            pick(lg2, m2, one2)
            tt(dif, m2, m1, ALU.subtract).then_inc(dif_ready, 1)
            dve.wait_ge(exp_ready, 1)
            ch.then(nc.vector.tensor_scalar(den, e, 1.0, None, ALU.add))
            ch.then(nc.vector.reciprocal(w1, den))
            ch.then(tt(w2, e, w1, ALU.mult))
            ch.then(tt(cand, one1, wide(w1), ALU.mult))
            ch.then(tt(eq, one2, wide(w2), ALU.mult))
            tt(cmb, cand, eq, ALU.add).then_inc(cmb_ready, 1)
            dve.wait_ge(tr, 1)
            nc.vector.tensor_copy(cT[:, :], PS[:, 1, 0:P]).then_inc(cT_ready, 1)


def experts(nc, tag, X, xh, xl, PS, d, ident, cw_dram):
    WC = 3 * HID
    with ExitStack() as c:
        sb = lambda n, s, t: c.enter_context(nc.sbuf_tensor(f"{tag}_{n}", s, t))
        sem = lambda n: c.enter_context(nc.semaphore(f"{tag}_{n}"))
        raw = [sb(f"raw{j}", [P, WC], f32) for j in range(2)]
        wh = [sb(f"wh{j}", [P, WC], f32r) for j in range(2)]
        wl = [sb(f"wl{j}", [P, WC], f32r) for j in range(2)]
        cw = [sb(f"cw{j}", [P, N], f32) for j in range(2)]
        sl = [sb(f"sl{i}", [P, C], f32) for i in range(4)]
        G = [sb(f"G{i}", [P, C], f32) for i in range(4)]
        Gh = [sb(f"Gh{i}", [P, C], f32r) for i in range(4)]
        Gl = [sb(f"Gl{i}", [P, C], f32r) for i in range(4)]
        tmp = [sb(f"tmp{i}", [P, C], f32) for i in range(2)]
        acc = sb("acc", [P, N], f32)
        h_ready, silu_ready, g_ready, gh_ready, gl_ready, y_ready, tmp_ready, acc_ready, w_hi, w_ready, tr, held = (
            sem(n) for n in ("h_ready", "silu_ready", "g_ready", "gh_ready", "gl_ready", "y_ready", "tmp_ready",
                             "acc_ready", "w_hi", "w_ready", "tr", "held"))
        w_ld = [sem(f"w_ld{j}") for j in range(2)]
        cw_ld = [sem(f"cw_ld{j}") for j in range(2)]
        block = c.enter_context(nc.Block())
        NI = NX // 2

        def each_pair(eng, body):
            body(0, True, False)
            with eng.Fori(1, NI - 1) as i:
                body(i, False, False)
            body(NI - 1, False, True)

        @block.sync
        def _(sp):
            for j in range(2):
                sp.dma_start(raw[j][:, :], d["f_w"][j]).then_inc(w_ld[j], 16)
                sp.dma_start(cw[j][:, :], cw_dram[j:j + 1, :].broadcast_to([P, N])).then_inc(cw_ld[j], 16)

            def body(i, first, last):
                for j in range(2):
                    if not last:
                        e = i * 2 + j
                        sp.wait_ge(w_ready, e + 1)
                        sp.dma_start(raw[j][:, :], d["f_w"][e + 2]).then_inc(w_ld[j], 16)
                        sp.wait_ge(tmp_ready, e * 4 + 4)
                        sp.dma_start(cw[j][:, :], cw_dram[e + 2].unsqueeze(0).broadcast_to([P, N])).then_inc(cw_ld[j], 16)
            each_pair(sp, body)

        @block.gpsimd
        def _(pool):
            def split(e, i, j):
                pool.wait_ge(w_ld[j], 16 * (i + 1))
                hold(pool, held)
                nc.gpsimd.tensor_copy(wh[j][:, :], raw[j][:, :]).then_inc(w_hi, 1)
                pool.wait_ge(w_hi, e + 1)
                nc.gpsimd.tensor_tensor(wl[j][:, :], raw[j][:, :], wh[j][:, :], ALU.subtract).then_inc(w_ready, 1)

            split(0, 0, 0)
            split(1, 0, 1)

            def body(i, first, last):
                for j in range(2):
                    for t in range(4):
                        n = i * 8 + j * 4 + t
                        a = acc[:, t * C:(t + 1) * C]
                        pool.wait_ge(tmp_ready, n + 1)
                        if first and j == 0:
                            nc.gpsimd.tensor_copy(a, tmp[t % 2][:, :]).then_inc(acc_ready, 1)
                        else:
                            pool.wait_ge(acc_ready, n - 3)
                            nc.gpsimd.tensor_tensor(a, a, tmp[t % 2][:, :], ALU.add).then_inc(acc_ready, 1)
                    if not last:
                        split(i * 2 + j + 2, i + 1, j)
            each_pair(pool, body)

        @block.tensor
        def _(pe):
            def up(i, w):
                j, t, hh = (w // 8) % 2, (w // 2) % 4, w % 2
                if w % 8 == 0:
                    pe.wait_ge(w_ready, i * 2 + w // 8 + 1)
                if not (isinstance(i, int) and i == 0 and w < 2):
                    pe.wait_ge(g_ready, i * 16 + w - 1)
                x = slice(t * C, (t + 1) * C)
                for bk, col in ((hh, hh * P), (2 + hh, HID + hh * P)):
                    cs = slice(col, col + P)
                    nc.tensor.matmul(PS[:, bk, :], wh[j][:, cs], xl[:, x], start=True, stop=False)
                    nc.tensor.matmul(PS[:, bk, :], wl[j][:, cs], xh[:, x], start=False, stop=False)
                    ins = nc.tensor.matmul(PS[:, bk, :], wh[j][:, cs], xh[:, x], start=False, stop=True)
                ins.then_inc(h_ready, 1)

            def down(i, first, n):
                j, t = n // 4, n % 4
                pe.wait_ge(gl_ready, i * 16 + 2 * n + 2)
                if not first or n >= 2:
                    pe.wait_ge(tmp_ready, i * 8 + n - 1)
                for hh in range(2):
                    cs = slice(2 * HID + hh * P, 2 * HID + hh * P + P)
                    s = (2 * n + hh) % 4
                    nc.tensor.matmul(PS[:, 4 + n % 2, :], wh[j][:, cs], Gl[s][:, :], start=hh == 0, stop=False)
                    nc.tensor.matmul(PS[:, 4 + n % 2, :], wl[j][:, cs], Gh[s][:, :], start=False, stop=False)
                    ins = nc.tensor.matmul(PS[:, 4 + n % 2, :], wh[j][:, cs], Gh[s][:, :], start=False, stop=hh == 1)
                ins.then_inc(y_ready, 1)

            up(0, 0)
            up(0, 1)

            def body(i, first, last):
                for n in range(8):
                    if not last or n < 7:
                        up(i, 2 * n + 2)
                        up(i, 2 * n + 3)
                    down(i, first, n)
            each_pair(pe, body)
            pe.wait_ge(acc_ready, 4 * NX)
            for t in range(NT):
                ins = nc.tensor.transpose(PS[:, t // 4, (t % 4) * P:(t % 4 + 1) * P], acc[:, t * P:(t + 1) * P], ident[:, :])
                if t % 4 == 3:
                    ins.then_inc(tr, 1)

        @block.scalar
        def _(act):
            def silu(i, w):
                act.wait_ge(h_ready, i * 16 + w + 1)
                nc.scalar.activation(sl[w % 4][:, :], PS[:, w % 2, :], ACT.Silu).then_inc(silu_ready, 1)

            def high(i, w):
                act.wait_ge(g_ready, i * 16 + w + 1)
                nc.scalar.activation(Gh[w % 4][:, :], G[w % 4][:, :], ACT.Copy).then_inc(gh_ready, 1)

            silu(0, 0)

            def body(i, first, last):
                for w in range(16):
                    if not last or w < 15:
                        silu(i, w + 1)
                    high(i, w)
            each_pair(act, body)

        @block.vector
        def _(dve):
            def gate(i, w):
                dve.wait_ge(silu_ready, i * 16 + w + 1)
                nc.vector.tensor_tensor(G[w % 4][:, :], sl[w % 4][:, :], PS[:, 2 + w % 2, :], ALU.mult).then_inc(g_ready, 1)

            def low(i, w):
                dve.wait_ge(gh_ready, i * 16 + w + 1)
                nc.vector.tensor_tensor(Gl[w % 4][:, :], G[w % 4][:, :], Gh[w % 4][:, :], ALU.subtract).then_inc(gl_ready, 1)

            def weigh(i, n, skip_free):
                j, t = (n // 4) % 2, n % 4
                if t == 0:
                    dve.wait_ge(cw_ld[j], 16 * (i + 1))
                dve.wait_ge(y_ready, i * 8 + n + 1)
                if not skip_free:
                    dve.wait_ge(acc_ready, i * 8 + n - 1)
                nc.vector.tensor_tensor(tmp[n % 2][:, :], PS[:, 4 + n % 2, :], cw[j][:, t * C:(t + 1) * C],
                                        ALU.mult).then_inc(tmp_ready, 1)

            gate(0, 0)

            def body(i, first, last):
                for w in range(16):
                    if not last or w < 15:
                        gate(i, w + 1)
                    low(i, w)
                    if w % 2 == 0 and w >= 2:
                        weigh(i, w // 2 - 1, first and w <= 4)
                    elif w == 0 and not first:
                        weigh(i - 1, 7, False)
                if last:
                    weigh(i, 7, False)
            each_pair(dve, body)
            for g in range(4):
                dve.wait_ge(tr, g + 1)
                x = flat(X[:, 4 * g:4 * g + 4, :])
                nc.vector.tensor_tensor(x, x, PS[:, g, :], ALU.add)


def attention_b(nc, X, xh, xl, ident, PS, d):
    v_dram = nc.dram_tensor("v_b", [U, P, QT, 2 * DB], f32r, kind="Internal").ap()
    with ExitStack() as c:
        sb = lambda n, s, t: c.enter_context(nc.sbuf_tensor(f"vb_{n}", s, t))
        sem = lambda n: c.enter_context(nc.semaphore(f"vb_{n}"))
        HF = HB * DB
        Wb = sb("Wb", [P, HF], bf16)
        W = sb("W", [P, HF], f32r)
        bb = sb("bb", [1, HF], bf16)
        bob = sb("bob", [P, E], bf16)
        brow = sb("brow", [P, HF], f32r)
        one = sb("one", [P, P], f32r)
        NS = 4
        vp = [sb(f"vp{i}", [P, HB, 2 * DB], f32r) for i in range(NS)]
        ld, zero, w_ready, mm, hi, lo = (sem(n) for n in ("ld", "zero", "w_ready", "mm", "hi", "lo"))
        st = [sem(f"st{i}") for i in range(NS)]
        block = c.enter_context(nc.Block())

        @block.sync
        def _(sp):
            sp.dma_start(Wb[:, :], d["b_wv"]).then_inc(ld, 16)
            sp.dma_start(bb[:, :], d["b_bv"]).then_inc(ld, 16)
            sp.dma_start(bob[:, :], d["b_bo"].broadcast_to([P, E])).then_inc(ld, 16)
            for t in range(NT):
                b, kt = t // QT, t % QT
                sp.wait_ge(lo, t + 1)
                sp.dma_start(words(v_dram[b * HB:(b + 1) * HB, :, kt, :].rearrange("h p c -> p h c")),
                             words(vp[t % NS][:, :, :])).then_inc(st[t % NS], 16)
            for i in range(NS):
                sp.wait_ge(st[i], 16 * (NT // NS))

        @block.gpsimd
        def _(pool):
            nc.gpsimd.memset(brow[:, :].bitcast(f32), 0.0).then_inc(zero, 1)
            nc.gpsimd.memset(one[:, :].bitcast(f32), 0.0).then_inc(zero, 1)
            pool.wait_ge(zero, 2)
            nc.gpsimd.memset(one[0:1, :].bitcast(f32), 1.0).then_inc(w_ready, 1)
            pool.wait_ge(ld, 48)
            nc.gpsimd.tensor_copy(brow[0:1, :], bb[:, :]).then_inc(w_ready, 1)
            nc.gpsimd.tensor_copy(W[:, :], Wb[:, :]).then_inc(w_ready, 1)

        @block.tensor
        def _(pe):
            pe.wait_ge(w_ready, 3)
            for t in range(NT):
                if t >= NS:
                    pe.wait_ge(lo, t - NS + 1)
                x = slice(t * P, (t + 1) * P)
                for h in range(2):
                    o, cs = PS[:, 2 * (t % NS) + h, :], slice(h * C, (h + 1) * C)
                    nc.tensor.matmul(o, one[:, :], brow[:, cs], start=True, stop=False)
                    nc.tensor.matmul(o, xl[:, x], W[:, cs], start=False, stop=False)
                    ins = nc.tensor.matmul(o, xh[:, x], W[:, cs], start=False, stop=True)
                ins.then_inc(mm, 1)

        @block.scalar
        def _(act):
            for t in range(NT):
                act.wait_ge(mm, t + 1)
                if t >= NS:
                    act.wait_ge(st[t % NS], 16 * (t // NS))
                src = flat(PS[:, 2 * (t % NS):2 * (t % NS) + 2, :]).rearrange("p (h d) -> p h d", d=DB)
                nc.scalar.activation(vp[t % NS][:, :, 0:DB], src, ACT.Copy).then_inc(hi, 1)

        @block.vector
        def _(dve):
            dve.wait_ge(ld, 48)
            for t in range(NT):
                dve.wait_ge(hi, t + 1)
                v = vp[t % NS]
                src = flat(PS[:, 2 * (t % NS):2 * (t % NS) + 2, :]).rearrange("p (h d) -> p h d", d=DB)
                nc.vector.tensor_tensor(v[:, :, DB:2 * DB], src, v[:, :, 0:DB], ALU.subtract).then_inc(lo, 1)
            nc.vector.tensor_tensor(X[:, :, :], X[:, :, :], bob[:, :].unsqueeze(1).broadcast_to([P, NT, E]), ALU.add)

    with ExitStack() as c:
        sb = lambda n, s, t: c.enter_context(nc.sbuf_tensor(f"ab_{n}", s, t))
        sem = lambda n: c.enter_context(nc.semaphore(f"ab_{n}"))
        A = attention_core(nc, "ab", c, PS, ident, False, DB)
        PL0, O0 = A.credits
        NP = U // 2
        HPB = HB // 2
        tab = sb("tab", [P, 4, S], f32)
        Wall = sb("Wall", [P, HPB, 4, P], bf16)
        ball = sb("ball", [P, HPB, 4], bf16)
        Wo = sb("Wo", [P, HB, E], bf16)
        Wst = sb("Wst", [P, 4, P], f32r)
        bst = sb("bst", [P, 4], f32)
        Wo32 = sb("Wo32", [P, HB, E], f32)
        T1 = [sb(f"T1{w}", [P, S], f32) for w in range(2)]
        T2 = [sb(f"T2{w}", [P, S], f32) for w in range(2)]
        rh = [sb(f"rh{w}", [P, S], f32r) for w in range(2)]
        rl = [sb(f"rl{w}", [P, S], f32r) for w in range(2)]
        rden = sb("rden", [P, 2, QT], f32)
        ld, wst_ready, r_full, r_free, parts_done, parts_ready, den_ready, proj_ready, proj_add, wo_ready, held = (
            sem(n) for n in ("ld", "wst_ready", "r_full", "r_free", "parts_done", "parts_ready", "den_ready",
                             "proj_ready", "proj_add", "wo_ready", "held"))
        qk_ld = [sem(f"qk_ld{j}") for j in range(2)]
        v_ld = [sem(f"v_ld{j}") for j in range(2)]
        block = c.enter_context(nc.Block())

        def each_pair(eng, body):
            body(0, True, False)
            with eng.Fori(1, NP - 1) as it:
                body(it, False, False)
            body(NP - 1, False, True)

        def load_qk(sp, j, pair):
            rows = slice(j * DB, (j + 1) * DB)
            sp.wait_ge(parts_ready, 2 * pair + 2)
            for dst, top, bot in ((A.QS[j], rh[0], rl[0]), (A.K1[j], rh[1], rh[1]), (A.K2[j], rl[1], rl[1])):
                sp.dma_start(words(dst[0:DB, :]), words(top[rows, :])).then_inc(qk_ld[j], 16)
                sp.dma_start(words(dst[DB:P, :]), words(bot[rows, :])).then_inc(qk_ld[j], 16)

        @block.sync
        def _(sp):
            sp.dma_start(tab[:, :, :], d["b_tab"].rearrange("k f s -> f k s")).then_inc(ld, 16)
            sp.dma_start(Wall[:, :, :, :], d["b_wqk"]).then_inc(ld, 16)
            sp.dma_start(ball[:, :, :], d["b_bqk"]).then_inc(ld, 16)
            sp.dma_start(Wo[:, :, :], d["b_wo"]).then_inc(ld, 16)
            for j in range(2):
                sp.dma_start(words(A.V[j][:, :, :]), words(v_dram[j])).then_inc(v_ld[j], 16)
                load_qk(sp, j, 0)

            def body(it, first, last):
                if last:
                    return
                sp.wait_ge(A.pv_ready, it * 4 + 2)
                sp.dma_start(words(A.V[0][:, :, :]), words(v_dram[it * 2 + 2])).then_inc(v_ld[0], 16)
                sp.wait_ge(A.s_ready, it * 16 + 8)
                load_qk(sp, 0, it + 1)
                sp.wait_ge(A.s_ready, it * 16 + 16)
                load_qk(sp, 1, it + 1)
                sp.wait_ge(A.pv_ready, it * 4 + 4)
                sp.dma_start(words(A.V[1][:, :, :]), words(v_dram[it * 2 + 3])).then_inc(v_ld[1], 16)
            each_pair(sp, body)

        def stage_weights(pool, pair):
            p = pair % HPB
            nc.gpsimd.tensor_copy(Wst[:, :, :], Wall[:, p, :, :]).then_inc(wst_ready, 1)
            nc.gpsimd.tensor_copy(bst[:, :], ball[:, p, :]).then_inc(wst_ready, 1)

        def make_parts(pool, w, pair):
            pool.wait_ge(r_free, pair * 8 + 4 * w + 5)
            nc.gpsimd.tensor_tensor(T1[w][:, :], T1[w][:, :], T2[w][:, :], ALU.add).then_inc(parts_done, 1)
            pool.wait_ge(parts_done, pair * 4 + 2 * w + 1)
            hold(pool, held)
            nc.gpsimd.tensor_copy(rh[w][:, :], T1[w][:, :]).then_inc(parts_done, 1)
            pool.wait_ge(parts_done, pair * 4 + 2 * w + 2)
            nc.gpsimd.tensor_tensor(rl[w][:, :], T1[w][:, :], rh[w][:, :], ALU.subtract).then_inc(parts_ready, 1)

        @block.gpsimd
        def _(pool):
            pool.wait_ge(ld, 64)
            stage_weights(pool, 0)
            nc.gpsimd.tensor_copy(flat(Wo32[:, :, :]), flat(Wo[:, :, :])).then_inc(wo_ready, 1)
            make_parts(pool, 0, 0)
            make_parts(pool, 1, 0)

            def body(it, first, last):
                if last:
                    return
                pool.wait_ge(r_free, it * 8 + 9)
                hold(pool, held)
                stage_weights(pool, it + 1)
                for j in range(2):
                    pool.wait_ge(qk_ld[j], 96 * (it + 1))
                make_parts(pool, 0, it + 1)
                make_parts(pool, 1, it + 1)
            each_pair(pool, body)

        def round_table(r):
            return 2 * (r // 4) + r % 2, (r // 2) % 2

        @block.tensor
        def _(pe):
            def project(pair, r):
                kind, h = round_table(r)
                if r == 0:
                    pe.wait_ge(wst_ready, 2 * pair + 2)
                    if not (isinstance(pair, int) and pair == 0):
                        pe.wait_ge(proj_add, 2 * pair - 1)
                pe.wait_ge(r_free, pair * 8 + r + 1)
                x = bass.ds((pair // HPB) * S + h * C, C)
                nc.tensor.matmul(PS[:, 7, :], Wst[:, kind, :], xl[:, x], start=True, stop=False)
                nc.tensor.matmul(PS[:, 7, :], Wst[:, kind, :], xh[:, x], start=False, stop=True).then_inc(r_full, 1)

            def out_project(it, j):
                pe.wait_ge(A.o_ready, it * 4 + 2 * j + 2 + O0)
                h = (it * 2 + j) % HB
                for qt in range(QT):
                    ins = nc.tensor.matmul(PS[:, 7 - qt // 4, (qt % 4) * P:(qt % 4 + 1) * P],
                                           A.OT[j][:, qt * P:(qt + 1) * P], Wo32[:, h, :], start=True, stop=True)
                ins.then_inc(proj_ready, 1)

            def loaded(it, k):
                j = (k // QT) % 2
                pe.wait_ge(qk_ld[j], 96 * (it + k // 16 + 1))

            for r in range(8):
                project(0, r)
            pe.wait_ge(wo_ready, 1)
            def values(it, k):
                if k % 8 == 3:
                    j = k // QT
                    pe.wait_ge(v_ld[j], 16 * (it + 1))
                    pe.wait_ge(proj_add, it * 2 + j + 1)
                A.values(pe, it, k)

            sc = lambda it, k: A.scores(it, k, loaded=loaded)
            sc(0, 0)
            sc(0, 1)

            def body(it, first, last):
                for k in range(16):
                    if not last or k < 14:
                        pe.wait_ge(A.p_ready, it * 16 + k + 1)
                        sc(it, k + 2)
                    if k % 4 == 0 and not (first and k == 0):
                        values(*before(it, k))
                    if k == 1 and not first:
                        out_project(it - 1, 1)
                    if k == 10:
                        if not last:
                            pe.wait_ge(r_free, it * 8 + 8 + 8 + 1)
                        out_project(it, 0)
                    A.transposes(pe, it, k)
                    if not last and 1 <= k <= 8:
                        project(it + 1, k - 1)
            each_pair(pe, body)
            values(NP - 1, 15)
            out_project(NP - 1, 1)

        @block.scalar
        def _(act):
            A.exponent(act, 0, 0)

            def body(it, first, last):
                for k in range(16):
                    if not last or k < 15:
                        A.exponent(act, it, k + 1)
                    if k % 4 == 0 and not (first and k == 0):
                        A.output(act, *before(it, k))
                    A.high_parts(act, it, k)
            each_pair(act, body)
            A.output(act, NP - 1, 15)

        @block.vector
        def _(dve):
            def rotate(pair, r):
                kind, h = round_table(r)
                w = kind // 2
                dve.wait_ge(r_full, pair * 8 + r + 1)
                if r % 4 == 0 and not (isinstance(pair, int) and pair == 0):
                    dve.wait_ge(parts_ready, 2 * pair)
                T = (T1, T2)[kind % 2][w]
                cs = slice(h * C, (h + 1) * C)
                nc.vector.scalar_tensor_tensor(T[:, cs], PS[:, 7, :], bst[:, kind:kind + 1], tab[:, kind, cs],
                                               ALU.add, ALU.mult).then_inc(r_free, 1)

            def add_head(it, j):
                dve.wait_ge(A.p_ready, it * 16 + 8 * j + 8)
                nc.vector.reciprocal(rden[:, j, :], A.rsum[:, j, :]).then_inc(den_ready, 1)
                dve.wait_ge(den_ready, it * 2 + j + 1)
                dve.wait_ge(proj_ready, it * 2 + j + 1)
                b = ((it * 2 + j) // HB)
                for qt in range(QT):
                    x = X[:, b * QT + qt, :]
                    ins = nc.vector.scalar_tensor_tensor(x, PS[:, 7 - qt // 4, (qt % 4) * P:(qt % 4 + 1) * P],
                                                         rden[:, j, qt:qt + 1], x, ALU.mult, ALU.add)
                ins.then_inc(proj_add, 1)

            nc.vector.memset(A.rsum[:, 0, 0:1], 0.0).then_inc(A.pl_ready, PL0)
            nc.vector.memset(A.rsum[:, 0, 1:2], 0.0).then_inc(A.o_ready, O0)
            nc.vector.memset(A.rsum[:, 0, 2:3], 0.0).then_inc(r_free, 1)
            nc.vector.memset(A.rsum[:, 0, 3:4], 0.0).then_inc(proj_add, 1)
            for r in range(8):
                rotate(0, r)
            A.maximum(dve, 0, 0)
            A.maximum(dve, 0, 1)

            def body(it, first, last):
                for k in range(16):
                    if not last or k < 14:
                        A.maximum(dve, it, k + 2)
                    if k == 1 and not first:
                        add_head(it - 1, 1)
                    if k == 10:
                        add_head(it, 0)
                    A.low_parts(dve, it, k)
                    if not last and 1 <= k <= 8:
                        rotate(it + 1, k - 1)
            each_pair(dve, body)
            add_head(NP - 1, 1)


def program(nc, d, out):
    with ExitStack() as c:
        sb = lambda n, s, t: c.enter_context(nc.sbuf_tensor(n, s, t))
        sem = lambda n: c.enter_context(nc.semaphore(n))
        X = sb("X", [P, NT, E], f32)
        xh = sb("xh", [P, N], f32r)
        xl = sb("xl", [P, N], f32r)
        ident = sb("ident", [P, P], f32)
        identr = sb("identr", [P, P], f32r)
        mask = sb("mask", [P, P], f32)
        maskr = sb("maskr", [P, P], f32r)
        PS = c.enter_context(nc.psum_tensor("PS", [P, 8, C], f32))
        cw_dram = [nc.dram_tensor(f"cw{i}", [NX, N], f32, kind="Internal").ap() for i in range(2)]
        ld, made, st = sem("x_ld"), sem("const_made"), sem("out_st")
        x_dram = d["x"].rearrange("b (t p) e -> p (b t) e", p=P)
        with nc.Block() as block:
            @block.sync
            def _(sp):
                sp.dma_start(X[:, :, :], x_dram).then_inc(ld, 16)
                sp.wait_ge(ld, 16)

            @block.gpsimd
            def _(pool):
                nc.gpsimd.memset(ident[:, :], 0.0).then_inc(made, 1)
                nc.gpsimd.memset(mask[:, :], 0.0).then_inc(made, 1)
                pool.wait_ge(made, 2)
                nc.gpsimd.affine_select(out=ident[:, :], in_=ident[:, :], compare_op=ALU.not_equal, fill=1.0,
                                        base=0, pattern=[[-1, P]], channel_multiplier=1).then_inc(made, 1)
                nc.gpsimd.affine_select(out=mask[:, :], in_=mask[:, :], compare_op=ALU.is_ge, fill=MASKED,
                                        base=0, pattern=[[-1, P]], channel_multiplier=1).then_inc(made, 1)
                pool.wait_ge(made, 4)
                nc.gpsimd.tensor_copy(identr[:, :], ident[:, :])
                nc.gpsimd.tensor_copy(maskr[:, :], mask[:, :])

        layernorm_transposed(nc, "ln1", X, xh, xl, ident, PS)
        attention_a(nc, X, xh, xl, ident, identr, maskr, PS, d)
        layernorm_transposed(nc, "ln2", X, xh, xl, ident, PS)
        router(nc, "r1", xh, xl, PS, d, ident, cw_dram[0])
        experts(nc, "e1", X, xh, xl, PS, d, ident, cw_dram[0])
        layernorm_transposed(nc, "ln3", X, xh, xl, ident, PS)
        attention_b(nc, X, xh, xl, ident, PS, d)
        layernorm_transposed(nc, "ln4", X, xh, xl, ident, PS)
        router(nc, "r2", xh, xl, PS, d, ident, cw_dram[1])
        experts(nc, "e2", X, xh, xl, PS, d, ident, cw_dram[1])
        with nc.Block() as block:
            @block.sync
            def _(sp):
                sp.dma_start(out.rearrange("b (t p) e -> p (b t) e", p=P), X[:, :, :]).then_inc(st, 16)
                sp.wait_ge(st, 16)


def lay_out(np, i):
    g = lambda n: np.ascontiguousarray(i[n])
    a = {"x": g("L0_attn_a_x")}
    swap = np.arange(E) ^ 1
    wq, wk = g("L0_attn_a_W_q"), g("L0_attn_a_W_k")
    a["a_w"] = np.stack([wq, wq[:, swap], wk, wk[:, swap], g("L0_attn_a_W_v")])
    a["a_wo"] = g("L0_attn_a_W_o")

    def table(dim, freq, sign, scale):
        inv = np.float32(1.0) / np.float32(10000.0) ** (np.arange(0, dim, 2, dtype=np.float32) / np.float32(dim))
        ang = np.arange(S, dtype=np.float32)[:, None] * inv[None, :].astype(np.float32)
        cos, sin = np.cos(ang).astype(np.float32).T[freq], np.sin(ang).astype(np.float32).T[freq]
        sin = sin * sign[:, None]
        return np.stack([cos * scale, sin * scale, cos, sin]).astype(np.float32)

    f = np.arange(P)
    a["a_tab"] = table(DA, (f % DA) // 2, np.where(f % 2 == 0, -1.0, 1.0).astype(np.float32),
                       np.float32(1.0 / np.sqrt(E)))
    a["b_tab"] = table(DB, f % (DB // 2), np.where(f % DB < DB // 2, -1.0, 1.0).astype(np.float32),
                       np.float32(DB ** -0.5))
    HF = HB * DB
    ff = np.arange(HF)
    turn = (ff // DB) * DB + (ff + DB // 2) % DB
    kinds = [g("L0_attn_b_Wq"), g("L0_attn_b_Wq")[turn], g("L0_attn_b_Wk"), g("L0_attn_b_Wk")[turn]]
    a["b_wqk"] = np.stack([w.reshape(HB // 2, P, E) for w in kinds]).transpose(3, 1, 0, 2)
    bias = [g("L0_attn_b_bq"), g("L0_attn_b_bq")[turn], g("L0_attn_b_bk"), g("L0_attn_b_bk")[turn]]
    a["b_bqk"] = np.stack([w.reshape(HB // 2, P) for w in bias]).transpose(2, 1, 0)
    a["b_wv"] = g("L0_attn_b_Wv").T
    a["b_bv"] = g("L0_attn_b_bv").reshape(1, HF)
    wo = g("L0_attn_b_Wo").reshape(E, HB, DB).transpose(2, 1, 0)
    a["b_wo"] = np.concatenate([wo, wo])
    a["b_bo"] = g("L0_attn_b_bo").reshape(1, E)
    w1 = np.concatenate([g("L0_ffn_w1"), g("L0_ffn_sw1")]).transpose(0, 2, 1)
    w3 = np.concatenate([g("L0_ffn_w3"), g("L0_ffn_sw3")]).transpose(0, 2, 1)
    w2 = np.concatenate([g("L0_ffn_w2"), g("L0_ffn_sw2")]).transpose(0, 2, 1)
    a["f_w"] = np.concatenate([w1, w3, w2[:, 0:P], w2[:, P:HID]], axis=2)
    a["router"] = g("L0_ffn_router_w").T
    a["ebias"] = g("L0_ffn_expert_bias").reshape(1, NE)
    a["rank"] = np.arange(NE, 0, -1, dtype=np.float32).reshape(1, NE)
    return {n: np.ascontiguousarray(v) for n, v in a.items()}


def kernel(**inputs):
    import numpy as _np
    import concourse.bacc as _bacc
    from concourse import mybir as _mybir
    from concourse.bass_utils import run_bass_kernel_spmd as _run

    nc = _bacc.Bacc("TRN2", target_bir_lowering=False, num_devices=1)
    arrays = {f"in_{n}": v for n, v in lay_out(_np, {k: _np.asarray(v) for k, v in inputs.items()}).items()}
    d = {n[3:]: nc.dram_tensor(n, v.shape, _mybir.dt.from_np(v.dtype), kind="ExternalInput").ap()
         for n, v in arrays.items()}
    out = nc.dram_tensor("out", (B, S, E), _mybir.dt.float32, kind="ExternalOutput").ap()
    program(nc, d, out)
    r = _run(nc, [arrays], core_ids=[0])
    return r.results[0]["out"]
```

```python
import concourse.bass as bass
from concourse import mybir
from contextlib import ExitStack

P = 128
B, S, E = 2, 1024, 128
N = B * S
NT = N // P
QT = S // P
EPS = 1e-5
HA, DA = 16, 8
HB, DB = 16, 64
U = B * HA
VA = 2 * DA + 1
NE, NX, HID = 8, 10, 256
MASKED = -1.0e30
BIG = 3.0e38
C = 512

f32 = mybir.dt.float32
f32r = mybir.dt.float32r
bf16 = mybir.dt.bfloat16
ALU = mybir.AluOpType
ACT = mybir.ActivationFunctionType
AX = mybir.AxisListType


def group_of(it, k):
    end = 4 * ((k - 1) // 4) - 1
    return (it, end, (k - 1) % 4) if end >= 0 else (it - 1, end + 16, (k - 1) % 4)


def words(ap):
    return ap.bitcast(f32)


def hold(eng, tally):
    eng.sem_inc(tally, 1)


def flat(ap):
    return ap.rearrange("p a b -> p (a b)")


class Chain:

    def __init__(self, eng, sem):
        self.eng, self.sem, self.n = eng, sem, 0

    def step(self, ins):
        self.n += 1
        ins.then_inc(self.sem, 1)

    def wait(self):
        self.eng.wait_ge(self.sem, self.n)

    def then(self, ins):
        self.step(ins)
        self.wait()


def layernorm_transposed(nc, tag, X, xh, xl, ident, PS):
    with ExitStack() as c:
        sb = lambda n, s, d: c.enter_context(nc.sbuf_tensor(f"{tag}_{n}", s, d))
        sem = lambda n: c.enter_context(nc.semaphore(f"{tag}_{n}"))
        nrm = sb("nrm", [P, NT, E], f32)
        bn = sb("bn", [P, NT, 6], f32)
        st = sb("st", [P, 8, NT], f32)
        dve_done, var_ready, root_ready, norm_ready, tr_ready, hi_ready = (
            sem(n) for n in ("dve_done", "var_ready", "root_ready", "norm_ready", "tr_ready", "hi_ready"))
        block = c.enter_context(nc.Block())

        def low(dve, g):
            dve.wait_ge(hi_ready, g + 1)
            nc.vector.tensor_tensor(xl[:, g * C:(g + 1) * C], PS[:, g, :], xh[:, g * C:(g + 1) * C], ALU.subtract)

        @block.vector
        def _(dve):
            ch = Chain(dve, dve_done)
            dif, mean, var, root, half, rstd, t = (st[:, i, :] for i in range(7))
            tt, ts = nc.vector.tensor_tensor, nc.vector.tensor_scalar
            for a in range(NT):
                ch.step(nc.vector.bn_stats(bn[:, a, :], X[:, a, :]))
            ch.wait()
            me, ve, mo, vo = (bn[:, :, i] for i in (1, 2, 4, 5))
            ch.step(tt(mean, me, mo, ALU.add))
            ch.step(tt(dif, me, mo, ALU.subtract))
            ch.then(tt(var, ve, vo, ALU.add))
            ch.then(tt(t, dif, dif, ALU.mult))
            ch.step(ts(mean, mean, 0.5, None, ALU.mult))
            ch.step(ts(t, t, 0.25, EPS, ALU.mult, ALU.add))
            ch.then(ts(var, var, 1.0 / E, None, ALU.mult))
            tt(var, var, t, ALU.add).then_inc(var_ready, 1)
            dve.wait_ge(root_ready, 1)
            ch.then(nc.vector.reciprocal(rstd, root))
            ch.then(tt(t, rstd, rstd, ALU.mult))
            ch.then(tt(half, t, var, ALU.mult))
            ch.then(ts(t, half, -0.5, 1.5, ALU.mult, ALU.add))
            ch.then(tt(half, t, rstd, ALU.mult))
            for a in range(NT):
                ts(nrm[:, a, :], X[:, a, :], mean[:, a:a + 1], half[:, a:a + 1],
                   ALU.subtract, ALU.mult).then_inc(norm_ready, 1)
                if a % 4 == 3 and a > 4:
                    low(dve, a // 4 - 1)
            low(dve, 3)

        @block.scalar
        def _(act):
            act.wait_ge(var_ready, 1)
            nc.scalar.activation(st[:, 3, :], st[:, 2, :], ACT.Sqrt).then_inc(root_ready, 1)
            for g in range(4):
                act.wait_ge(tr_ready, g + 1)
                nc.scalar.activation(xh[:, g * C:(g + 1) * C], PS[:, g, :], ACT.Copy).then_inc(hi_ready, 1)

        @block.tensor
        def _(pe):
            for g in range(4):
                for a in range(4):
                    pe.wait_ge(norm_ready, 4 * g + a + 1)
                    ins = nc.tensor.transpose(PS[:, g, a * P:(a + 1) * P], nrm[:, g * 4 + a, :], ident[:, :])
                ins.then_inc(tr_ready, 1)


def attention_core(nc, tag, c, PS, ident, causal, DQK):
    class A: pass
    A = A()
    sb = lambda n, s, d: c.enter_context(nc.sbuf_tensor(f"{tag}_{n}", s, d))
    sem = lambda n: c.enter_context(nc.semaphore(f"{tag}_{n}"))
    vm = VA if causal else P
    QS = A.QS = [sb(f"QS{j}", [P, S], f32r) for j in range(2)]
    K1 = A.K1 = [sb(f"K1{j}", [P, S], f32r) for j in range(2)]
    K2 = A.K2 = None if causal else [sb(f"K2{j}", [P, S], f32r) for j in range(2)]
    V = A.V = [sb(f"V{j}", [P, QT, vm], f32r) for j in range(2)]
    prob = [sb(f"prob{j}", [P, S], f32) for j in range(2)]
    PTh = [sb(f"PTh{i}", [P, QT, C], f32r) for i in range(2)]
    PTl = [sb(f"PTl{i}", [P, QT, C], f32r) for i in range(2)]
    nmax = sb("nmax", [P, 4], f32)
    A.rsum = sb("rsum", [P, 2, QT], f32)
    A.OT = [sb(f"OT{j}", [vm, S], f32) for j in range(2)]
    A.s_ready, A.max_ready, A.p_ready, A.t_ready, A.ph_ready, A.pl_ready, A.pv_ready, A.o_ready = (
        sem(n) for n in ("s_ready", "max_ready", "p_ready", "t_ready", "ph_ready", "pl_ready", "pv_ready", "o_ready"))
    TB = (4, 5, 7) if causal else (4, 5)
    PL0, O0 = len(TB), 1
    halves = [[(4 * h, min(4 * h + 4, qt + 1 if causal else QT)) for h in range(2) if not causal or 4 * h <= qt]
              for qt in range(QT)]
    halves_before = [sum(len(halves[k % QT]) for k in range(n)) for n in range(2 * QT + 1)]
    HP = halves_before[2 * QT]
    width = lambda qt: (qt + 1) * P if causal else S
    bank = lambda k: PS[:, 2 * (k % 2):2 * (k % 2) + 2, :]
    A.credits = (PL0, O0)

    def scores(it, k, maskr=None, identr=None, loaded=None):
        if k % QT == 0 and loaded:
            loaded(it, k)
        j, qt = (k // QT) % 2, k % QT
        q = QS[j][:, qt * P:(qt + 1) * P]
        w = width(qt)
        for h in range((w + C - 1) // C):
            n = min(C, w - h * C)
            out = PS[:, 2 * (k % 2) + h, 0:n]
            last = h == (w + C - 1) // C - 1
            ins = nc.tensor.matmul(out, q, K1[j][:, h * C:h * C + n], start=True, stop=causal and not last)
            if not causal:
                ins = nc.tensor.matmul(out, q, K2[j][:, h * C:h * C + n], start=False, stop=True)
            elif last:
                ins = nc.tensor.matmul(PS[:, 2 * (k % 2) + h, n - P:n], identr[:, :], maskr[:, :], start=False, stop=True)
        ins.then_inc(A.s_ready, 1)

    def transposes(pe, it, k):
        pe.wait_ge(A.p_ready, it * 16 + k + 1)
        for i, (a, b) in enumerate(halves[k % QT]):
            m = halves_before[k] + i
            pe.wait_ge(A.pl_ready, it * HP + m + 1)
            for kt in range(a, b):
                ins = nc.tensor.transpose(PS[:, TB[m % PL0], (kt - a) * P:(kt - a + 1) * P],
                                          prob[k % 2][:, kt * P:(kt + 1) * P], ident[:, :])
            ins.then_inc(A.t_ready, 1)

    def values(pe, it, k, v_ld):
        it, end, quarter = group_of(it, k)
        j, g = end // QT, (end % QT) // 4
        if quarter == 0:
            pe.wait_ge(A.pl_ready, it * HP + halves_before[end + 1] + PL0)
            pe.wait_ge(A.o_ready, it * 4 + 2 * j + g + O0)
            if g == 0:
                pe.wait_ge(v_ld[j], 16 * (it + 1))
        nk = 4 * g + 4 if causal else QT
        for kt in range(nk * quarter // 4, nk * (quarter + 1) // 4):
            q0 = max(0, kt - 4 * g) * P if causal else 0
            for part in (PTh[g], PTl[g]):
                ins = nc.tensor.matmul(PS[0:vm, 6, q0:C], V[j][:, kt, :], part[:, kt, q0:C],
                                       start=kt == 0 and part is PTh[g], stop=kt == nk - 1 and part is PTl[g])
        if quarter == 3:
            ins.then_inc(A.pv_ready, 1)

    def maximum(dve, it, k):
        dve.wait_ge(A.s_ready, it * 16 + k + 1)
        w = width(k % QT)
        src = flat(bank(k))[:, 0:w]
        nc.vector.tensor_reduce(nmax[:, k % 4:k % 4 + 1], src, AX.X, ALU.max, negate=True).then_inc(A.max_ready, 1)

    def exponent(act, it, k):
        act.wait_ge(A.max_ready, it * 16 + k + 1)
        w = width(k % QT)
        kw = {} if causal else {"accum_out": A.rsum[:, (k // QT) % 2, k % QT:k % QT + 1]}
        nc.scalar.activation(prob[k % 2][:, 0:w], flat(bank(k))[:, 0:w], ACT.Exp,
                             bias=nmax[:, k % 4:k % 4 + 1], scale=1.0, **kw).then_inc(A.p_ready, 1)

    def part(k, buf, a, b):
        return buf[(k // 4) % 2][:, a:b, (k % 4) * P:(k % 4 + 1) * P]

    def src(m, a, b):
        return PS[:, TB[m % PL0], 0:(b - a) * P].rearrange("p (a q) -> p a q", q=P)

    def high_parts(act, it, k):
        for i, (a, b) in enumerate(halves[k % QT]):
            m = halves_before[k] + i
            act.wait_ge(A.t_ready, it * HP + m + 1)
            nc.scalar.activation(part(k, PTh, a, b), src(m, a, b), ACT.Copy).then_inc(A.ph_ready, 1)

    def low_parts(dve, it, k):
        for i, (a, b) in enumerate(halves[k % QT]):
            m = halves_before[k] + i
            dve.wait_ge(A.ph_ready, it * HP + m + 1)
            nc.vector.tensor_tensor(part(k, PTl, a, b), src(m, a, b), part(k, PTh, a, b),
                                    ALU.subtract).then_inc(A.pl_ready, 1)

    def output(act, it, k, free=None):
        it, end, _ = group_of(it, k)
        j, g = end // QT, (end % QT) // 4
        act.wait_ge(A.pv_ready, it * 4 + 2 * j + g + 1)
        if free and g == 0:
            free(it, j)
        nc.scalar.activation(A.OT[j][:, g * C:(g + 1) * C], PS[0:vm, 6, :], ACT.Copy).then_inc(A.o_ready, 1)

    A.scores, A.transposes, A.values, A.maximum, A.exponent = scores, transposes, values, maximum, exponent
    A.high_parts, A.low_parts, A.output = high_parts, low_parts, output
    return A


def attention_a(nc, X, xh, xl, ident, identr, maskr, PS, d):
    qk_dram = nc.dram_tensor("qk_a", [2, U, 2, DA, S], f32r, kind="Internal").ap()
    o_dram = nc.dram_tensor("o_a", [U, 2 * DA, S], f32, kind="Internal").ap()
    den_dram = nc.dram_tensor("den_a", [U, S], f32, kind="Internal").ap()
    outer = ExitStack()
    with outer:
        Va = outer.enter_context(nc.sbuf_tensor("Va", [P, U, QT, VA], f32r))
        with ExitStack() as c:
            sb = lambda n, s, t: c.enter_context(nc.sbuf_tensor(f"pa_{n}", s, t))
            sem = lambda n: c.enter_context(nc.semaphore(f"pa_{n}"))
            W = sb("W", [P, 5, P], f32)
            Wh = sb("Wh", [P, 5, P], f32r)
            Wl = sb("Wl", [P, 5, P], f32r)
            tab = sb("tab", [P, 4, S], f32)
            T = [sb(f"T{i}", [P, C], f32) for i in range(2)]
            rot = [sb(f"rot{i}", [P, C], f32) for i in range(2)]
            qkh = sb("qkh", [P, 2, N], f32r)
            qkl = sb("qkl", [P, 2, N], f32r)
            ld, split, mm, dve_done, mid, va_hi, qk_done, st = (
                sem(n) for n in ("ld", "split", "mm", "dve_done", "mid", "va_hi", "qk_done", "st"))
            block = c.enter_context(nc.Block())

            @block.sync
            def _(sp):
                sp.dma_start(W[:, :, :], d["a_w"].rearrange("k e f -> e k f")).then_inc(ld, 16)
                sp.dma_start(tab[:, :, :], d["a_tab"].rearrange("k f s -> f k s")).then_inc(ld, 16)
                for w in range(2):
                    sp.wait_ge(qk_done, 4 * (w + 1))
                    for prt, src in enumerate((qkh, qkl)):
                        for b in range(B):
                            sp.dma_start(words(qk_dram[w, b * HA:(b + 1) * HA, prt]),
                                         words(src[:, w, b * S:(b + 1) * S])).then_inc(st, 16)
                sp.wait_ge(st, 16 * 8)

            @block.tensor
            def _(pe):
                pe.wait_ge(split, 2)
                n = 0
                for w in range(2):
                    for t in range(4):
                        for r in range(2):
                            if n >= 4:
                                pe.wait_ge(mid, n // 2 - 1)
                            bk = PS[:, (n % 4), :]
                            i = 2 * w + r
                            x = slice(t * C, (t + 1) * C)
                            nc.tensor.matmul(bk, Wh[:, i, :], xl[:, x], start=True, stop=False)
                            nc.tensor.matmul(bk, Wl[:, i, :], xh[:, x], start=False, stop=False)
                            nc.tensor.matmul(bk, Wh[:, i, :], xh[:, x], start=False, stop=True).then_inc(mm, 1)
                            n += 1
                for t in range(NT):
                    bk = PS[:, 4 + t // 4, (t % 4) * P:(t % 4 + 1) * P]
                    x = slice(t * P, (t + 1) * P)
                    nc.tensor.matmul(bk, xl[:, x], Wh[:, 4, :], start=True, stop=False)
                    nc.tensor.matmul(bk, xh[:, x], Wl[:, 4, :], start=False, stop=False)
                    ins = nc.tensor.matmul(bk, xh[:, x], Wh[:, 4, :], start=False, stop=True)
                    if t % 4 == 3:
                        ins.then_inc(mm, 1)

            @block.vector
            def _(dve):
                ch = Chain(dve, dve_done)
                dve.wait_ge(ld, 32)
                nc.vector.tensor_copy(Wh[:, :, :], W[:, :, :]).then_inc(split, 1)
                dve.wait_ge(split, 1)
                nc.vector.tensor_tensor(Wl[:, :, :], W[:, :, :], Wh[:, :, :], ALU.subtract).then_inc(split, 1)
                ch.step(nc.vector.memset(Va[:, :, :, 2 * DA:VA].bitcast(f32), 1.0))
                for w in range(2):
                    for t in range(4):
                        n = 8 * w + 2 * t
                        dve.wait_ge(mm, n + 2)
                        s0 = (t % 2) * C
                        ch.step(nc.vector.tensor_tensor(T[0][:, :], PS[:, n % 4, :], tab[:, 2 * w, s0:s0 + C], ALU.mult))
                        nc.vector.tensor_tensor(T[1][:, :], PS[:, n % 4 + 1, :], tab[:, 2 * w + 1, s0:s0 + C],
                                                ALU.mult).then_inc(mid, 1)
                        ch.wait()
                        dve.wait_ge(mid, 4 * w + t + 1)
                        x = slice(t * C, (t + 1) * C)
                        ch.then(nc.vector.tensor_tensor(rot[0][:, :], T[0][:, :], T[1][:, :], ALU.add))
                        ch.then(nc.vector.tensor_copy(qkh[:, w, x], rot[0][:, :]))
                        nc.vector.tensor_tensor(qkl[:, w, x], rot[0][:, :], qkh[:, w, x], ALU.subtract).then_inc(qk_done, 1)
                        dve.wait_ge(qk_done, 4 * w + t + 1)
                for g in range(4):
                    dve.wait_ge(va_hi, 4 * (g + 1))
                    for a in range(4):
                        t = 4 * g + a
                        b, kt = t // QT, t % QT
                        v = Va[:, b * HA:(b + 1) * HA, kt, :]
                        nc.vector.tensor_tensor(v[:, :, DA:2 * DA],
                                                PS[:, 4 + g, a * P:(a + 1) * P].rearrange("p (h d) -> p h d", d=DA),
                                                v[:, :, 0:DA], ALU.subtract)

            @block.scalar
            def _(act):
                for g in range(4):
                    act.wait_ge(mm, 16 + g + 1)
                    for a in range(4):
                        t = 4 * g + a
                        b, kt = t // QT, t % QT
                        nc.scalar.activation(Va[:, b * HA:(b + 1) * HA, kt, 0:DA],
                                             PS[:, 4 + g, a * P:(a + 1) * P].rearrange("p (h d) -> p h d", d=DA),
                                             ACT.Copy).then_inc(va_hi, 1)

        with ExitStack() as c:
            sem = lambda n: c.enter_context(nc.semaphore(f"aa_{n}"))
            A = attention_core(nc, "aa", c, PS, ident, True, DA)
            PL0, O0 = A.credits
            zero_ready, st = sem("zero_ready"), sem("st")
            qk_ld = [sem(f"qk_ld{j}") for j in range(2)]
            v_ld = [sem(f"v_ld{j}") for j in range(2)]
            o_st = [sem(f"o_st{j}") for j in range(2)]
            NP = U // 2

            def load_qk(sp, u, j):
                for r in range(2):
                    sp.dma_start(words(A.QS[j][16 * r:16 * r + 16, :]),
                                 words(qk_dram[0, u].rearrange("r d s -> (r d) s"))).then_inc(qk_ld[j], 16)
                for r in range(4):
                    sp.dma_start(words(A.K1[j][8 * r:8 * r + 8, :]), words(qk_dram[1, u, r // 2])).then_inc(qk_ld[j], 16)

            def load_v(sp, u, j):
                sp.dma_start(words(A.V[j][:, :, :]), words(Va[:, u, :, :])).then_inc(v_ld[j], 16)

            block = c.enter_context(nc.Block())

            def each_pair(eng, body):
                body(0, True, False)
                with eng.Fori(1, NP - 1) as it:
                    body(it, False, False)
                body(NP - 1, False, True)

            @block.sync
            def _(sp):
                sp.wait_ge(zero_ready, 4)
                for j in range(2):
                    load_qk(sp, j, j)
                    load_v(sp, j, j)

                def body(it, first, last):
                    for j in range(2):
                        u = it * 2 + j
                        if not last:
                            sp.wait_ge(A.s_ready, it * 16 + 8 * j + 8)
                            load_qk(sp, u + 2, j)
                            sp.wait_ge(A.pv_ready, it * 4 + 2 * j + 2)
                            load_v(sp, u + 2, j)
                        sp.wait_ge(A.o_ready, it * 4 + 2 * j + 2 + O0)
                        sp.dma_start(o_dram[u], A.OT[j][0:2 * DA, :]).then_inc(o_st[j], 16)
                        sp.dma_start(den_dram[u].unsqueeze(0), A.OT[j][2 * DA:VA, :]).then_inc(o_st[j], 16)
                each_pair(sp, body)
                for j in range(2):
                    sp.wait_ge(o_st[j], 32 * (NP + 1))

            @block.gpsimd
            def _(pool):
                for j in range(2):
                    nc.gpsimd.memset(A.QS[j][:, :].bitcast(f32), 0.0).then_inc(zero_ready, 1)
                    nc.gpsimd.memset(A.K1[j][:, :].bitcast(f32), 0.0).then_inc(zero_ready, 1)

            @block.tensor
            def _(pe):
                def loaded(it, k):
                    j = (k // QT) % 2
                    pe.wait_ge(qk_ld[j], 96 * (it + k // 16 + 1))

                sc = lambda it, k: A.scores(it, k, maskr, identr, loaded)
                sc(0, 0)
                sc(0, 1)

                def body(it, first, last):
                    for k in range(16):
                        if not last or k < 14:
                            pe.wait_ge(A.p_ready, it * 16 + k + 1)
                            sc(it, k + 2)
                        if not first or k > 4:
                            A.values(pe, it, k, v_ld)
                        A.transposes(pe, it, k)
                each_pair(pe, body)
                for k in range(5):
                    A.values(pe, NP, k, v_ld)

            @block.scalar
            def _(act):
                def free(it, j):
                    act.wait_ge(o_st[j], 32 * (it + 1))

                A.exponent(act, 0, 0)

                def body(it, first, last):
                    for k in range(16):
                        if not last or k < 15:
                            A.exponent(act, it, k + 1)
                        if k % 4 == 0 and not (first and k <= 4):
                            A.output(act, it, k, free)
                        A.high_parts(act, it, k)
                each_pair(act, body)
                A.output(act, NP, 0, free)
                A.output(act, NP, 4, free)

            @block.vector
            def _(dve):
                nc.vector.memset(A.rsum[:, 0, 0:1], 0.0).then_inc(A.pl_ready, PL0)
                nc.vector.memset(A.rsum[:, 0, 1:2], 0.0).then_inc(A.o_ready, O0)
                for j in range(2):
                    nc.vector.memset(A.rsum[:, 1, j:j + 1], 0.0).then_inc(o_st[j], 32)
                A.maximum(dve, 0, 0)
                A.maximum(dve, 0, 1)

                def body(it, first, last):
                    for k in range(16):
                        if not last or k < 14:
                            A.maximum(dve, it, k + 2)
                        A.low_parts(dve, it, k)
                each_pair(dve, body)

    with ExitStack() as c:
        sb = lambda n, s, t: c.enter_context(nc.sbuf_tensor(f"oa_{n}", s, t))
        sem = lambda n: c.enter_context(nc.semaphore(f"oa_{n}"))
        oh = sb("oh", [P, B, S], f32)
        ol = sb("ol", [P, B, S], f32)
        rec = sb("rec", [P, B, S], f32)
        CH = P // U
        den = sb("den", [P, S // CH], f32)
        rden = sb("rden", [P, S // CH], f32)
        r_dram = nc.dram_tensor("rden_a", [U, S], f32, kind="Internal").ap()
        Wo = sb("Wo", [P, P], f32)
        den_ld, ld, rden_ready, rden_st, rec_ld, summed, o_norm, mm = (
            sem(n) for n in ("den_ld", "ld", "rden_ready", "rden_st", "rec_ld", "summed", "o_norm", "mm"))
        block = c.enter_context(nc.Block())

        @block.sync
        def _(sp):
            sp.dma_start(den[:, :], den_dram.rearrange("u (c s) -> (u c) s", c=CH)).then_inc(den_ld, 16)
            sp.wait_ge(rden_ready, 1)
            sp.dma_start(r_dram.rearrange("u (c s) -> (u c) s", c=CH), rden[:, :]).then_inc(rden_st, 16)
            sp.wait_ge(rden_st, 16)
            for b in range(B):
                sp.dma_start(rec[:, b, :], r_dram[b * HA:(b + 1) * HA].unsqueeze(1).broadcast_to([HA, DA, S])
                             ).then_inc(rec_ld, 16)

        @block.scalar
        def _(act):
            act.dma_start(Wo[:, :], d["a_wo"]).then_inc(ld, 16)
            for b in range(B):
                us = slice(b * HA, (b + 1) * HA)
                act.dma_start(oh[:, b, :], o_dram[us, 0:DA]).then_inc(ld, 16)
                act.dma_start(ol[:, b, :], o_dram[us, DA:2 * DA]).then_inc(ld, 16)

        @block.vector
        def _(dve):
            dve.wait_ge(den_ld, 16)
            nc.vector.reciprocal(rden[:, :], den[:, :]).then_inc(rden_ready, 1)
            dve.wait_ge(ld, 16 * (1 + 2 * B))
            nc.vector.tensor_tensor(flat(oh[:, :, :]), flat(oh[:, :, :]), flat(ol[:, :, :]), ALU.add).then_inc(summed, 1)
            dve.wait_ge(rec_ld, 16 * B)
            dve.wait_ge(summed, 1)
            nc.vector.tensor_tensor(flat(ol[:, :, :]), flat(oh[:, :, :]), flat(rec[:, :, :]), ALU.mult).then_inc(o_norm, 1)
            for g in range(4):
                dve.wait_ge(mm, g + 1)
                x = flat(X[:, 4 * g:4 * g + 4, :])
                nc.vector.tensor_tensor(x, x, PS[:, g, :], ALU.add)

        @block.tensor
        def _(pe):
            pe.wait_ge(o_norm, 1)
            for t in range(NT):
                ins = nc.tensor.matmul(PS[:, t // 4, (t % 4) * P:(t % 4 + 1) * P],
                                       flat(ol[:, :, :])[:, t * P:(t + 1) * P], Wo[:, :], start=True, stop=True)
                if t % 4 == 3:
                    ins.then_inc(mm, 1)


def router(nc, tag, xh, xl, PS, d, ident, cw_dram):
    with ExitStack() as c:
        sb = lambda n, s, t: c.enter_context(nc.sbuf_tensor(f"{tag}_{n}", s, t))
        sem = lambda n: c.enter_context(nc.semaphore(f"{tag}_{n}"))
        rw = sb("rw", [P, NE], f32)
        rwh = sb("rwh", [P, NE], f32r)
        rwl = sb("rwl", [P, NE], f32r)
        bias = sb("bias", [P, NE], f32)
        rank = sb("rank", [P, NE], f32)
        W = {n: sb(n, [P, NT, NE], f32) for n in ("lg", "lg2", "eq", "cand", "one1", "one2", "cmb")}
        v = sb("v", [P, 8, NT], f32)
        cT = sb("cT", [P, P], f32)
        ones = sb("ones", [NX - NE, N], f32)
        ld, split, mm, dve_done, dif_ready, exp_ready, cmb_ready, tr, cT_ready, ones_ready, st = (
            sem(n) for n in ("ld", "split", "mm", "dve_done", "dif_ready", "exp_ready", "cmb_ready", "tr", "cT_ready", "ones_ready", "st"))
        block = c.enter_context(nc.Block())
        wide = lambda a: a.unsqueeze(2).broadcast_to([P, NT, NE])
        rows = lambda a: a.unsqueeze(1).broadcast_to([P, NT, NE])

        @block.sync
        def _(sp):
            sp.dma_start(rw[:, :], d["router"]).then_inc(ld, 16)
            sp.dma_start(bias[:, :], d["ebias"].broadcast_to([P, NE])).then_inc(ld, 16)
            sp.dma_start(rank[:, :], d["rank"].broadcast_to([P, NE])).then_inc(ld, 16)
            sp.wait_ge(ones_ready, 1)
            sp.dma_start(cw_dram[NE:NX, :], ones[:, :]).then_inc(st, 16)
            sp.wait_ge(cT_ready, 1)
            for t in range(NT):
                sp.dma_start(cw_dram[0:NE, t * P:(t + 1) * P], cT[t * NE:(t + 1) * NE, :]).then_inc(st, 16)
            sp.wait_ge(st, 16 * (NT + 1))

        @block.gpsimd
        def _(pool):
            nc.gpsimd.memset(ones[:, :], 1.0).then_inc(ones_ready, 1)

        @block.tensor
        def _(pe):
            pe.wait_ge(split, 2)
            for t in range(NT):
                o = PS[:, 0, t * NE:(t + 1) * NE]
                x = slice(t * P, (t + 1) * P)
                nc.tensor.matmul(o, xl[:, x], rwl[:, :], start=True, stop=False)
                nc.tensor.matmul(o, xl[:, x], rwh[:, :], start=False, stop=False)
                nc.tensor.matmul(o, xh[:, x], rwl[:, :], start=False, stop=False)
                ins = nc.tensor.matmul(o, xh[:, x], rwh[:, :], start=False, stop=True)
            ins.then_inc(mm, 1)
            pe.wait_ge(cmb_ready, 1)
            nc.tensor.transpose(PS[:, 1, 0:P], flat(W["cmb"][:, :, :]), ident[:, :]).then_inc(tr, 1)

        @block.scalar
        def _(act):
            act.wait_ge(dif_ready, 1)
            nc.scalar.activation(v[:, 3, :], v[:, 2, :], ACT.Exp).then_inc(exp_ready, 1)

        @block.vector
        def _(dve):
            ch = Chain(dve, dve_done)
            lg, lg2, eq, cand, one1, one2, cmb = (W[n][:, :, :] for n in ("lg", "lg2", "eq", "cand", "one1", "one2", "cmb"))
            m1, m2, dif, e, den, w1, w2, top = (v[:, i, :] for i in range(8))
            tt = nc.vector.tensor_tensor
            dve.wait_ge(ld, 48)
            nc.vector.tensor_copy(rwh[:, :], rw[:, :]).then_inc(split, 1)
            dve.wait_ge(split, 1)
            tt(rwl[:, :], rw[:, :], rwh[:, :], ALU.subtract).then_inc(split, 1)
            dve.wait_ge(mm, 1)
            ch.then(tt(lg, PS[:, 0, 0:NT * NE].rearrange("p (t e) -> p t e", e=NE), rows(bias[:, :]), ALU.add))

            def pick(scores, mx, one):
                ch.then(nc.vector.tensor_reduce(mx, scores, AX.X, ALU.max))
                ch.then(tt(eq, scores, wide(mx), ALU.is_equal))
                ch.then(tt(cand, eq, rows(rank[:, :]), ALU.mult))
                ch.then(nc.vector.tensor_reduce(top, cand, AX.X, ALU.max))
                ch.then(tt(one, rows(rank[:, :]), wide(top), ALU.is_equal))

            pick(lg, m1, one1)
            ch.then(nc.vector.scalar_tensor_tensor(lg2, one1, -BIG, lg, ALU.mult, ALU.add))
            pick(lg2, m2, one2)
            tt(dif, m2, m1, ALU.subtract).then_inc(dif_ready, 1)
            dve.wait_ge(exp_ready, 1)
            ch.then(nc.vector.tensor_scalar(den, e, 1.0, None, ALU.add))
            ch.then(nc.vector.reciprocal(w1, den))
            ch.then(tt(w2, e, w1, ALU.mult))
            ch.then(tt(cand, one1, wide(w1), ALU.mult))
            ch.then(tt(eq, one2, wide(w2), ALU.mult))
            tt(cmb, cand, eq, ALU.add).then_inc(cmb_ready, 1)
            dve.wait_ge(tr, 1)
            nc.vector.tensor_copy(cT[:, :], PS[:, 1, 0:P]).then_inc(cT_ready, 1)


def experts(nc, tag, X, xh, xl, PS, d, ident, cw_dram):
    WC = 3 * HID
    with ExitStack() as c:
        sb = lambda n, s, t: c.enter_context(nc.sbuf_tensor(f"{tag}_{n}", s, t))
        sem = lambda n: c.enter_context(nc.semaphore(f"{tag}_{n}"))
        raw = [sb(f"raw{j}", [P, WC], f32) for j in range(2)]
        wh = [sb(f"wh{j}", [P, WC], f32r) for j in range(2)]
        wl = [sb(f"wl{j}", [P, WC], f32r) for j in range(2)]
        cw = [sb(f"cw{j}", [P, N], f32) for j in range(2)]
        sl = [sb(f"sl{i}", [P, C], f32) for i in range(4)]
        G = [sb(f"G{i}", [P, C], f32) for i in range(4)]
        Gh = [sb(f"Gh{i}", [P, C], f32r) for i in range(4)]
        Gl = [sb(f"Gl{i}", [P, C], f32r) for i in range(4)]
        tmp = [sb(f"tmp{i}", [P, C], f32) for i in range(2)]
        acc = sb("acc", [P, N], f32)
        h_ready, silu_ready, g_ready, gh_ready, gl_ready, y_ready, tmp_ready, acc_ready, w_hi, w_ready, tr, held = (
            sem(n) for n in ("h_ready", "silu_ready", "g_ready", "gh_ready", "gl_ready", "y_ready", "tmp_ready",
                             "acc_ready", "w_hi", "w_ready", "tr", "held"))
        w_ld = [sem(f"w_ld{j}") for j in range(2)]
        cw_ld = [sem(f"cw_ld{j}") for j in range(2)]
        block = c.enter_context(nc.Block())
        NI = NX // 2

        def each_pair(eng, body):
            body(0, True, False)
            with eng.Fori(1, NI - 1) as i:
                body(i, False, False)
            body(NI - 1, False, True)

        @block.sync
        def _(sp):
            for j in range(2):
                sp.dma_start(raw[j][:, :], d["f_w"][j]).then_inc(w_ld[j], 16)
                sp.dma_start(cw[j][:, :], cw_dram[j:j + 1, :].broadcast_to([P, N])).then_inc(cw_ld[j], 16)

            def body(i, first, last):
                for j in range(2):
                    if not last:
                        e = i * 2 + j
                        sp.wait_ge(w_ready, e + 1)
                        sp.dma_start(raw[j][:, :], d["f_w"][e + 2]).then_inc(w_ld[j], 16)
                        sp.wait_ge(tmp_ready, e * 4 + 4)
                        sp.dma_start(cw[j][:, :], cw_dram[e + 2].unsqueeze(0).broadcast_to([P, N])).then_inc(cw_ld[j], 16)
            each_pair(sp, body)

        @block.gpsimd
        def _(pool):
            def split(e, i, j):
                pool.wait_ge(w_ld[j], 16 * (i + 1))
                hold(pool, held)
                nc.gpsimd.tensor_copy(wh[j][:, :], raw[j][:, :]).then_inc(w_hi, 1)
                pool.wait_ge(w_hi, e + 1)
                nc.gpsimd.tensor_tensor(wl[j][:, :], raw[j][:, :], wh[j][:, :], ALU.subtract).then_inc(w_ready, 1)

            split(0, 0, 0)
            split(1, 0, 1)

            def body(i, first, last):
                for j in range(2):
                    for t in range(4):
                        n = i * 8 + j * 4 + t
                        a = acc[:, t * C:(t + 1) * C]
                        pool.wait_ge(tmp_ready, n + 1)
                        if first and j == 0:
                            nc.gpsimd.tensor_copy(a, tmp[t % 2][:, :]).then_inc(acc_ready, 1)
                        else:
                            pool.wait_ge(acc_ready, n - 3)
                            nc.gpsimd.tensor_tensor(a, a, tmp[t % 2][:, :], ALU.add).then_inc(acc_ready, 1)
                    if not last:
                        split(i * 2 + j + 2, i + 1, j)
            each_pair(pool, body)

        @block.tensor
        def _(pe):
            def up(i, w):
                j, t, hh = (w // 8) % 2, (w // 2) % 4, w % 2
                if w % 8 == 0:
                    pe.wait_ge(w_ready, i * 2 + w // 8 + 1)
                if not (isinstance(i, int) and i == 0 and w < 2):
                    pe.wait_ge(g_ready, i * 16 + w - 1)
                x = slice(t * C, (t + 1) * C)
                for bk, col in ((hh, hh * P), (2 + hh, HID + hh * P)):
                    cs = slice(col, col + P)
                    nc.tensor.matmul(PS[:, bk, :], wh[j][:, cs], xl[:, x], start=True, stop=False)
                    nc.tensor.matmul(PS[:, bk, :], wl[j][:, cs], xh[:, x], start=False, stop=False)
                    ins = nc.tensor.matmul(PS[:, bk, :], wh[j][:, cs], xh[:, x], start=False, stop=True)
                ins.then_inc(h_ready, 1)

            def down(i, first, n):
                j, t = n // 4, n % 4
                pe.wait_ge(gl_ready, i * 16 + 2 * n + 2)
                if not first or n >= 2:
                    pe.wait_ge(tmp_ready, i * 8 + n - 1)
                for hh in range(2):
                    cs = slice(2 * HID + hh * P, 2 * HID + hh * P + P)
                    s = (2 * n + hh) % 4
                    nc.tensor.matmul(PS[:, 4 + n % 2, :], wh[j][:, cs], Gl[s][:, :], start=hh == 0, stop=False)
                    nc.tensor.matmul(PS[:, 4 + n % 2, :], wl[j][:, cs], Gh[s][:, :], start=False, stop=False)
                    ins = nc.tensor.matmul(PS[:, 4 + n % 2, :], wh[j][:, cs], Gh[s][:, :], start=False, stop=hh == 1)
                ins.then_inc(y_ready, 1)

            for w in range(3):
                up(0, w)

            def body(i, first, last):
                for n in range(8):
                    for w in (2 * n + 3, 2 * n + 4):
                        if not last or w < 16:
                            up(i, w)
                    down(i, first, n)
            each_pair(pe, body)
            pe.wait_ge(acc_ready, 4 * NX)
            for t in range(NT):
                ins = nc.tensor.transpose(PS[:, t // 4, (t % 4) * P:(t % 4 + 1) * P], acc[:, t * P:(t + 1) * P], ident[:, :])
                if t % 4 == 3:
                    ins.then_inc(tr, 1)

        @block.scalar
        def _(act):
            def silu(i, w):
                act.wait_ge(h_ready, i * 16 + w + 1)
                nc.scalar.activation(sl[w % 4][:, :], PS[:, w % 2, :], ACT.Silu).then_inc(silu_ready, 1)

            def high(i, w):
                act.wait_ge(g_ready, i * 16 + w + 1)
                nc.scalar.activation(Gh[w % 4][:, :], G[w % 4][:, :], ACT.Copy).then_inc(gh_ready, 1)

            silu(0, 0)

            def body(i, first, last):
                for w in range(16):
                    if not last or w < 15:
                        silu(i, w + 1)
                    high(i, w)
            each_pair(act, body)

        @block.vector
        def _(dve):
            def gate(i, w):
                dve.wait_ge(silu_ready, i * 16 + w + 1)
                nc.vector.tensor_tensor(G[w % 4][:, :], sl[w % 4][:, :], PS[:, 2 + w % 2, :], ALU.mult).then_inc(g_ready, 1)

            def low(i, w):
                dve.wait_ge(gh_ready, i * 16 + w + 1)
                nc.vector.tensor_tensor(Gl[w % 4][:, :], G[w % 4][:, :], Gh[w % 4][:, :], ALU.subtract).then_inc(gl_ready, 1)

            def weigh(i, n, skip_free):
                j, t = (n // 4) % 2, n % 4
                if t == 0:
                    dve.wait_ge(cw_ld[j], 16 * (i + 1))
                dve.wait_ge(y_ready, i * 8 + n + 1)
                if not skip_free:
                    dve.wait_ge(acc_ready, i * 8 + n - 1)
                nc.vector.tensor_tensor(tmp[n % 2][:, :], PS[:, 4 + n % 2, :], cw[j][:, t * C:(t + 1) * C],
                                        ALU.mult).then_inc(tmp_ready, 1)

            gate(0, 0)

            def body(i, first, last):
                for w in range(16):
                    if not last or w < 15:
                        gate(i, w + 1)
                    low(i, w)
                    if w % 2 == 0 and w >= 2:
                        weigh(i, w // 2 - 1, first and w <= 4)
                    elif w == 0 and not first:
                        weigh(i - 1, 7, False)
                if last:
                    weigh(i, 7, False)
            each_pair(dve, body)
            for g in range(4):
                dve.wait_ge(tr, g + 1)
                x = flat(X[:, 4 * g:4 * g + 4, :])
                nc.vector.tensor_tensor(x, x, PS[:, g, :], ALU.add)


def attention_b(nc, X, xh, xl, ident, PS, d):
    v_dram = nc.dram_tensor("v_b", [U, P, QT, 2 * DB], f32r, kind="Internal").ap()
    with ExitStack() as c:
        sb = lambda n, s, t: c.enter_context(nc.sbuf_tensor(f"vb_{n}", s, t))
        sem = lambda n: c.enter_context(nc.semaphore(f"vb_{n}"))
        HF = HB * DB
        Wb = sb("Wb", [P, HF], bf16)
        W = sb("W", [P, HF], f32r)
        bb = sb("bb", [1, HF], bf16)
        bob = sb("bob", [P, E], bf16)
        brow = sb("brow", [P, HF], f32r)
        one = sb("one", [P, P], f32r)
        NS = 4
        vp = [sb(f"vp{i}", [P, HB, 2 * DB], f32r) for i in range(NS)]
        ld, zero, w_ready, mm, hi, lo = (sem(n) for n in ("ld", "zero", "w_ready", "mm", "hi", "lo"))
        st = [sem(f"st{i}") for i in range(NS)]
        block = c.enter_context(nc.Block())

        @block.sync
        def _(sp):
            sp.dma_start(Wb[:, :], d["b_wv"]).then_inc(ld, 16)
            sp.dma_start(bb[:, :], d["b_bv"]).then_inc(ld, 16)
            sp.dma_start(bob[:, :], d["b_bo"].broadcast_to([P, E])).then_inc(ld, 16)
            for t in range(NT):
                b, kt = t // QT, t % QT
                sp.wait_ge(lo, t + 1)
                sp.dma_start(words(v_dram[b * HB:(b + 1) * HB, :, kt, :].rearrange("h p c -> p h c")),
                             words(vp[t % NS][:, :, :])).then_inc(st[t % NS], 16)
            for i in range(NS):
                sp.wait_ge(st[i], 16 * (NT // NS))

        @block.gpsimd
        def _(pool):
            nc.gpsimd.memset(brow[:, :].bitcast(f32), 0.0).then_inc(zero, 1)
            nc.gpsimd.memset(one[:, :].bitcast(f32), 0.0).then_inc(zero, 1)
            pool.wait_ge(zero, 2)
            nc.gpsimd.memset(one[0:1, :].bitcast(f32), 1.0).then_inc(w_ready, 1)
            pool.wait_ge(ld, 48)
            nc.gpsimd.tensor_copy(brow[0:1, :], bb[:, :]).then_inc(w_ready, 1)
            nc.gpsimd.tensor_copy(W[:, :], Wb[:, :]).then_inc(w_ready, 1)

        @block.tensor
        def _(pe):
            pe.wait_ge(w_ready, 3)
            for t in range(NT):
                if t >= NS:
                    pe.wait_ge(lo, t - NS + 1)
                x = slice(t * P, (t + 1) * P)
                for h in range(2):
                    o, cs = PS[:, 2 * (t % NS) + h, :], slice(h * C, (h + 1) * C)
                    nc.tensor.matmul(o, one[:, :], brow[:, cs], start=True, stop=False)
                    nc.tensor.matmul(o, xl[:, x], W[:, cs], start=False, stop=False)
                    ins = nc.tensor.matmul(o, xh[:, x], W[:, cs], start=False, stop=True)
                ins.then_inc(mm, 1)

        @block.scalar
        def _(act):
            for t in range(NT):
                act.wait_ge(mm, t + 1)
                if t >= NS:
                    act.wait_ge(st[t % NS], 16 * (t // NS))
                src = flat(PS[:, 2 * (t % NS):2 * (t % NS) + 2, :]).rearrange("p (h d) -> p h d", d=DB)
                nc.scalar.activation(vp[t % NS][:, :, 0:DB], src, ACT.Copy).then_inc(hi, 1)

        @block.vector
        def _(dve):
            dve.wait_ge(ld, 48)
            for t in range(NT):
                dve.wait_ge(hi, t + 1)
                v = vp[t % NS]
                src = flat(PS[:, 2 * (t % NS):2 * (t % NS) + 2, :]).rearrange("p (h d) -> p h d", d=DB)
                nc.vector.tensor_tensor(v[:, :, DB:2 * DB], src, v[:, :, 0:DB], ALU.subtract).then_inc(lo, 1)
            nc.vector.tensor_tensor(X[:, :, :], X[:, :, :], bob[:, :].unsqueeze(1).broadcast_to([P, NT, E]), ALU.add)

    with ExitStack() as c:
        sb = lambda n, s, t: c.enter_context(nc.sbuf_tensor(f"ab_{n}", s, t))
        sem = lambda n: c.enter_context(nc.semaphore(f"ab_{n}"))
        A = attention_core(nc, "ab", c, PS, ident, False, DB)
        PL0, O0 = A.credits
        NP = U // 2
        HPB = HB // 2
        tab = sb("tab", [P, 4, S], f32)
        Wall = sb("Wall", [P, HPB, 4, P], bf16)
        ball = sb("ball", [P, HPB, 4], bf16)
        Wst = sb("Wst", [P, 4, P], f32r)
        bst = sb("bst", [P, 4], f32)
        Wo32 = sb("Wo32", [P, HB, E], f32)
        T1 = [sb(f"T1{w}", [P, S], f32) for w in range(2)]
        T2 = [sb(f"T2{w}", [P, S], f32) for w in range(2)]
        rh = [sb(f"rh{w}", [P, S], f32r) for w in range(2)]
        rl = [sb(f"rl{w}", [P, S], f32r) for w in range(2)]
        rden = sb("rden", [P, 2, QT], f32)
        Wo = T2[1][:, :].bitcast(bf16).rearrange("p (h e) -> p h e", h=HB)
        ld, wst_ready, r_full, r_free, parts_done, parts_ready, den_ready, proj_ready, proj_add, wo_ready, held = (
            sem(n) for n in ("ld", "wst_ready", "r_full", "r_free", "parts_done", "parts_ready", "den_ready",
                             "proj_ready", "proj_add", "wo_ready", "held"))
        qk_ld = [sem(f"qk_ld{j}") for j in range(2)]
        v_ld = [sem(f"v_ld{j}") for j in range(2)]
        block = c.enter_context(nc.Block())

        def each_pair(eng, body):
            body(0, True, False)
            with eng.Fori(1, NP - 1) as it:
                body(it, False, False)
            body(NP - 1, False, True)

        def load_qk(sp, j, pair):
            rows = slice(j * DB, (j + 1) * DB)
            sp.wait_ge(parts_ready, 2 * pair + 2)
            for dst, top, bot in ((A.QS[j], rh[0], rl[0]), (A.K1[j], rh[1], rh[1]), (A.K2[j], rl[1], rl[1])):
                sp.dma_start(words(dst[0:DB, :]), words(top[rows, :])).then_inc(qk_ld[j], 16)
                sp.dma_start(words(dst[DB:P, :]), words(bot[rows, :])).then_inc(qk_ld[j], 16)

        @block.sync
        def _(sp):
            sp.dma_start(tab[:, :, :], d["b_tab"].rearrange("k f s -> f k s")).then_inc(ld, 16)
            sp.dma_start(Wall[:, :, :, :], d["b_wqk"]).then_inc(ld, 16)
            sp.dma_start(ball[:, :, :], d["b_bqk"]).then_inc(ld, 16)
            sp.dma_start(Wo, d["b_wo"]).then_inc(ld, 16)
            for j in range(2):
                sp.dma_start(words(A.V[j][:, :, :]), words(v_dram[j])).then_inc(v_ld[j], 16)
                load_qk(sp, j, 0)

            def body(it, first, last):
                if last:
                    return
                sp.wait_ge(A.s_ready, it * 16 + 8)
                load_qk(sp, 0, it + 1)
                sp.wait_ge(A.pv_ready, it * 4 + 2)
                sp.dma_start(words(A.V[0][:, :, :]), words(v_dram[it * 2 + 2])).then_inc(v_ld[0], 16)
                sp.wait_ge(A.s_ready, it * 16 + 16)
                load_qk(sp, 1, it + 1)
                sp.wait_ge(A.pv_ready, it * 4 + 4)
                sp.dma_start(words(A.V[1][:, :, :]), words(v_dram[it * 2 + 3])).then_inc(v_ld[1], 16)
            each_pair(sp, body)

        def stage_weights(pool, pair):
            p = pair % HPB
            nc.gpsimd.tensor_copy(Wst[:, :, :], Wall[:, p, :, :]).then_inc(wst_ready, 1)
            nc.gpsimd.tensor_copy(bst[:, :], ball[:, p, :]).then_inc(wst_ready, 1)

        def make_parts(pool, w, pair):
            pool.wait_ge(r_free, pair * 8 + 4 * w + 5)
            nc.gpsimd.tensor_tensor(T1[w][:, :], T1[w][:, :], T2[w][:, :], ALU.add).then_inc(parts_done, 1)
            pool.wait_ge(parts_done, pair * 4 + 2 * w + 1)
            hold(pool, held)
            nc.gpsimd.tensor_copy(rh[w][:, :], T1[w][:, :]).then_inc(parts_done, 1)
            pool.wait_ge(parts_done, pair * 4 + 2 * w + 2)
            nc.gpsimd.tensor_tensor(rl[w][:, :], T1[w][:, :], rh[w][:, :], ALU.subtract).then_inc(parts_ready, 1)

        @block.gpsimd
        def _(pool):
            pool.wait_ge(ld, 64)
            stage_weights(pool, 0)
            nc.gpsimd.tensor_copy(Wo32[:, :, :], Wo).then_inc(wo_ready, 1)
            make_parts(pool, 0, 0)
            make_parts(pool, 1, 0)

            def body(it, first, last):
                if last:
                    return
                pool.wait_ge(r_free, it * 8 + 9)
                hold(pool, held)
                stage_weights(pool, it + 1)
                for j in range(2):
                    pool.wait_ge(qk_ld[j], 96 * (it + 1))
                make_parts(pool, 0, it + 1)
                make_parts(pool, 1, it + 1)
            each_pair(pool, body)

        def round_table(r):
            return 2 * (r // 4) + r % 2, (r // 2) % 2

        @block.tensor
        def _(pe):
            def project(pair, r):
                kind, h = round_table(r)
                if r == 0:
                    pe.wait_ge(wst_ready, 2 * pair + 2)
                    if not (isinstance(pair, int) and pair <= 1):
                        pe.wait_ge(proj_add, 4 * pair - 5)
                pe.wait_ge(r_free, pair * 8 + r + 1)
                x = bass.ds((pair // HPB) * S + h * C, C)
                nc.tensor.matmul(PS[:, 7, :], Wst[:, kind, :], xl[:, x], start=True, stop=False)
                nc.tensor.matmul(PS[:, 7, :], Wst[:, kind, :], xh[:, x], start=False, stop=True).then_inc(r_full, 1)

            def out_project(it, j, half, rounds):
                pe.wait_ge(A.o_ready, it * 4 + 2 * j + 2 + O0)
                pe.wait_ge(proj_add, it * 4 + 2 * j + half + 1)
                if rounds is not None and half == 0:
                    pe.wait_ge(r_free, rounds + 1)
                h = (it * 2 + j) % HB
                for a in range(4):
                    qt = 4 * half + a
                    ins = nc.tensor.matmul(PS[:, 7, a * P:(a + 1) * P],
                                           A.OT[j][:, qt * P:(qt + 1) * P], Wo32[:, h, :], start=True, stop=True)
                ins.then_inc(proj_ready, 1)

            def loaded(it, k):
                j = (k // QT) % 2
                pe.wait_ge(qk_ld[j], 96 * (it + k // 16 + 1))

            for r in range(8):
                project(0, r)
            pe.wait_ge(wo_ready, 1)
            sc = lambda it, k: A.scores(it, k, loaded=loaded)
            sc(0, 0)
            sc(0, 1)

            def body(it, first, last):
                for k in range(16):
                    if not last or k < 14:
                        pe.wait_ge(A.p_ready, it * 16 + k + 1)
                        sc(it, k + 2)
                    if not first or k > 4:
                        A.values(pe, it, k, v_ld)
                    if k < 8 and not last:
                        project(it + 1, k)
                    if k in (8, 9) and not first:
                        out_project(it - 1, 1, k - 8, None if last else it * 8 + 16)
                    if k in (13, 14):
                        out_project(it, 0, k - 13, None if last else it * 8 + 16)
                    A.transposes(pe, it, k)
            each_pair(pe, body)
            for k in range(5):
                A.values(pe, NP, k, v_ld)
            for h in range(2):
                out_project(NP - 1, 1, h, None)

        @block.scalar
        def _(act):
            A.exponent(act, 0, 0)

            def body(it, first, last):
                for k in range(16):
                    if not last or k < 15:
                        A.exponent(act, it, k + 1)
                    if k % 4 == 0 and not (first and k <= 4):
                        A.output(act, it, k)
                    A.high_parts(act, it, k)
            each_pair(act, body)
            A.output(act, NP, 0)
            A.output(act, NP, 4)

        @block.vector
        def _(dve):
            def rotate(pair, r):
                kind, h = round_table(r)
                w = kind // 2
                dve.wait_ge(r_full, pair * 8 + r + 1)
                if r == 4 and isinstance(pair, int) and pair == 0:
                    dve.wait_ge(wo_ready, 1)
                if r % 4 == 0 and not (isinstance(pair, int) and pair == 0):
                    dve.wait_ge(parts_ready, 2 * pair)
                T = (T1, T2)[kind % 2][w]
                cs = slice(h * C, (h + 1) * C)
                nc.vector.scalar_tensor_tensor(T[:, cs], PS[:, 7, :], bst[:, kind:kind + 1], tab[:, kind, cs],
                                               ALU.add, ALU.mult).then_inc(r_free, 1)

            def invert(it, j):
                dve.wait_ge(A.p_ready, it * 16 + 8 * j + 8)
                nc.vector.reciprocal(rden[:, j, :], A.rsum[:, j, :]).then_inc(den_ready, 1)

            def add_head(it, j, half):
                if half == 0:
                    dve.wait_ge(den_ready, it * 2 + j + 1)
                dve.wait_ge(proj_ready, it * 4 + 2 * j + half + 1)
                b = ((it * 2 + j) // HB)
                for a in range(4):
                    qt = 4 * half + a
                    x = X[:, b * QT + qt, :]
                    ins = nc.vector.scalar_tensor_tensor(x, PS[:, 7, a * P:(a + 1) * P],
                                                         rden[:, j, qt:qt + 1], x, ALU.mult, ALU.add)
                ins.then_inc(proj_add, 1)

            nc.vector.memset(A.rsum[:, 0, 0:1], 0.0).then_inc(A.pl_ready, PL0)
            nc.vector.memset(A.rsum[:, 0, 1:2], 0.0).then_inc(A.o_ready, O0)
            nc.vector.memset(A.rsum[:, 0, 2:3], 0.0).then_inc(r_free, 1)
            nc.vector.memset(A.rsum[:, 0, 3:4], 0.0).then_inc(proj_add, 1)
            for r in range(8):
                rotate(0, r)
            A.maximum(dve, 0, 0)
            A.maximum(dve, 0, 1)

            def body(it, first, last):
                for k in range(16):
                    if not last or k < 14:
                        A.maximum(dve, it, k + 2)
                    if k < 8 and not last:
                        rotate(it + 1, k)
                    if k == 3 and not first:
                        invert(it - 1, 1)
                    if k in (8, 9) and not first:
                        add_head(it - 1, 1, k - 8)
                    if k == 11:
                        invert(it, 0)
                    if k in (13, 14):
                        add_head(it, 0, k - 13)
                    A.low_parts(dve, it, k)
            each_pair(dve, body)
            invert(NP - 1, 1)
            for h in range(2):
                add_head(NP - 1, 1, h)


def program(nc, d, out):
    with ExitStack() as c:
        sb = lambda n, s, t: c.enter_context(nc.sbuf_tensor(n, s, t))
        sem = lambda n: c.enter_context(nc.semaphore(n))
        X = sb("X", [P, NT, E], f32)
        xh = sb("xh", [P, N], f32r)
        xl = sb("xl", [P, N], f32r)
        ident = sb("ident", [P, P], f32)
        identr = sb("identr", [P, P], f32r)
        mask = sb("mask", [P, P], f32)
        maskr = sb("maskr", [P, P], f32r)
        PS = c.enter_context(nc.psum_tensor("PS", [P, 8, C], f32))
        cw_dram = [nc.dram_tensor(f"cw{i}", [NX, N], f32, kind="Internal").ap() for i in range(2)]
        ld, made, st = sem("x_ld"), sem("const_made"), sem("out_st")
        x_dram = d["x"].rearrange("b (t p) e -> p (b t) e", p=P)
        with nc.Block() as block:
            @block.sync
            def _(sp):
                sp.dma_start(X[:, :, :], x_dram).then_inc(ld, 16)
                sp.wait_ge(ld, 16)

            @block.gpsimd
            def _(pool):
                nc.gpsimd.memset(ident[:, :], 0.0).then_inc(made, 1)
                nc.gpsimd.memset(mask[:, :], 0.0).then_inc(made, 1)
                pool.wait_ge(made, 2)
                nc.gpsimd.affine_select(out=ident[:, :], in_=ident[:, :], compare_op=ALU.not_equal, fill=1.0,
                                        base=0, pattern=[[-1, P]], channel_multiplier=1).then_inc(made, 1)
                nc.gpsimd.affine_select(out=mask[:, :], in_=mask[:, :], compare_op=ALU.is_ge, fill=MASKED,
                                        base=0, pattern=[[-1, P]], channel_multiplier=1).then_inc(made, 1)
                pool.wait_ge(made, 4)
                nc.gpsimd.tensor_copy(identr[:, :], ident[:, :])
                nc.gpsimd.tensor_copy(maskr[:, :], mask[:, :])

        layernorm_transposed(nc, "ln1", X, xh, xl, ident, PS)
        attention_a(nc, X, xh, xl, ident, identr, maskr, PS, d)
        layernorm_transposed(nc, "ln2", X, xh, xl, ident, PS)
        router(nc, "r1", xh, xl, PS, d, ident, cw_dram[0])
        experts(nc, "e1", X, xh, xl, PS, d, ident, cw_dram[0])
        layernorm_transposed(nc, "ln3", X, xh, xl, ident, PS)
        attention_b(nc, X, xh, xl, ident, PS, d)
        layernorm_transposed(nc, "ln4", X, xh, xl, ident, PS)
        router(nc, "r2", xh, xl, PS, d, ident, cw_dram[1])
        experts(nc, "e2", X, xh, xl, PS, d, ident, cw_dram[1])
        with nc.Block() as block:
            @block.sync
            def _(sp):
                sp.dma_start(out.rearrange("b (t p) e -> p (b t) e", p=P), X[:, :, :]).then_inc(st, 16)
                sp.wait_ge(st, 16)


def lay_out(np, i):
    g = lambda n: np.ascontiguousarray(i[n])
    a = {"x": g("L0_attn_a_x")}
    swap = np.arange(E) ^ 1
    wq, wk = g("L0_attn_a_W_q"), g("L0_attn_a_W_k")
    a["a_w"] = np.stack([wq, wq[:, swap], wk, wk[:, swap], g("L0_attn_a_W_v")])
    a["a_wo"] = g("L0_attn_a_W_o")

    def table(dim, freq, sign, scale):
        inv = np.float32(1.0) / np.float32(10000.0) ** (np.arange(0, dim, 2, dtype=np.float32) / np.float32(dim))
        ang = np.arange(S, dtype=np.float32)[:, None] * inv[None, :].astype(np.float32)
        cos, sin = np.cos(ang).astype(np.float32).T[freq], np.sin(ang).astype(np.float32).T[freq]
        sin = sin * sign[:, None]
        return np.stack([cos * scale, sin * scale, cos, sin]).astype(np.float32)

    f = np.arange(P)
    a["a_tab"] = table(DA, (f % DA) // 2, np.where(f % 2 == 0, -1.0, 1.0).astype(np.float32),
                       np.float32(1.0 / np.sqrt(E)))
    a["b_tab"] = table(DB, f % (DB // 2), np.where(f % DB < DB // 2, -1.0, 1.0).astype(np.float32),
                       np.float32(DB ** -0.5))
    HF = HB * DB
    ff = np.arange(HF)
    turn = (ff // DB) * DB + (ff + DB // 2) % DB
    kinds = [g("L0_attn_b_Wq"), g("L0_attn_b_Wq")[turn], g("L0_attn_b_Wk"), g("L0_attn_b_Wk")[turn]]
    a["b_wqk"] = np.stack([w.reshape(HB // 2, P, E) for w in kinds]).transpose(3, 1, 0, 2)
    bias = [g("L0_attn_b_bq"), g("L0_attn_b_bq")[turn], g("L0_attn_b_bk"), g("L0_attn_b_bk")[turn]]
    a["b_bqk"] = np.stack([w.reshape(HB // 2, P) for w in bias]).transpose(2, 1, 0)
    a["b_wv"] = g("L0_attn_b_Wv").T
    a["b_bv"] = g("L0_attn_b_bv").reshape(1, HF)
    wo = g("L0_attn_b_Wo").reshape(E, HB, DB).transpose(2, 1, 0)
    a["b_wo"] = np.concatenate([wo, wo])
    a["b_bo"] = g("L0_attn_b_bo").reshape(1, E)
    w1 = np.concatenate([g("L0_ffn_w1"), g("L0_ffn_sw1")]).transpose(0, 2, 1)
    w3 = np.concatenate([g("L0_ffn_w3"), g("L0_ffn_sw3")]).transpose(0, 2, 1)
    w2 = np.concatenate([g("L0_ffn_w2"), g("L0_ffn_sw2")]).transpose(0, 2, 1)
    a["f_w"] = np.concatenate([w1, w3, w2[:, 0:P], w2[:, P:HID]], axis=2)
    a["router"] = g("L0_ffn_router_w").T
    a["ebias"] = g("L0_ffn_expert_bias").reshape(1, NE)
    a["rank"] = np.arange(NE, 0, -1, dtype=np.float32).reshape(1, NE)
    return {n: np.ascontiguousarray(v) for n, v in a.items()}


def kernel(**inputs):
    import numpy as _np
    import concourse.bacc as _bacc
    from concourse import mybir as _mybir
    from concourse.bass_utils import run_bass_kernel_spmd as _run

    nc = _bacc.Bacc("TRN2", target_bir_lowering=False, num_devices=1)
    arrays = {f"in_{n}": v for n, v in lay_out(_np, {k: _np.asarray(v) for k, v in inputs.items()}).items()}
    d = {n[3:]: nc.dram_tensor(n, v.shape, _mybir.dt.from_np(v.dtype), kind="ExternalInput").ap()
         for n, v in arrays.items()}
    out = nc.dram_tensor("out", (B, S, E), _mybir.dt.float32, kind="ExternalOutput").ap()
    program(nc, d, out)
    r = _run(nc, [arrays], core_ids=[0])
    return r.results[0]["out"]
```

```python
import concourse.bass as bass
from concourse import mybir
from contextlib import ExitStack

P = 128
B, S, E = 2, 1024, 128
N = B * S
NT = N // P
QT = S // P
EPS = 1e-5
HA, DA = 16, 8
HB, DB = 16, 64
U = B * HA
VA = 2 * DA + 1
NE, NX, HID = 8, 10, 256
MASKED = -1.0e30
BIG = 3.0e38
C = 512

f32 = mybir.dt.float32
f32r = mybir.dt.float32r
bf16 = mybir.dt.bfloat16
ALU = mybir.AluOpType
ACT = mybir.ActivationFunctionType
AX = mybir.AxisListType


def group_of(it, k):
    end = 4 * ((k - 1) // 4) - 1
    return (it, end, (k - 1) % 4) if end >= 0 else (it - 1, end + 16, (k - 1) % 4)


def words(ap):
    return ap.bitcast(f32)


def hold(eng, tally):
    eng.sem_inc(tally, 1)


def flat(ap):
    return ap.rearrange("p a b -> p (a b)")


class Chain:

    def __init__(self, eng, sem):
        self.eng, self.sem, self.n = eng, sem, 0

    def step(self, ins):
        self.n += 1
        ins.then_inc(self.sem, 1)

    def wait(self):
        self.eng.wait_ge(self.sem, self.n)

    def then(self, ins):
        self.step(ins)
        self.wait()


def layernorm_transposed(nc, tag, X, xh, xl, ident, PS, meanwhile=None, nrm=None):
    with ExitStack() as c:
        sb = lambda n, s, d: c.enter_context(nc.sbuf_tensor(f"{tag}_{n}", s, d))
        sem = lambda n: c.enter_context(nc.semaphore(f"{tag}_{n}"))
        nrm = sb("nrm", [P, NT, E], f32) if nrm is None else nrm
        bn = sb("bn", [P, NT, 6], f32)
        st = sb("st", [P, 8, NT], f32)
        dve_done, var_ready, root_ready, norm_ready, tr_ready, hi_ready = (
            sem(n) for n in ("dve_done", "var_ready", "root_ready", "norm_ready", "tr_ready", "hi_ready"))
        block = c.enter_context(nc.Block())
        if meanwhile:
            meanwhile(block)

        def low(dve, g):
            dve.wait_ge(hi_ready, g + 1)
            nc.vector.tensor_tensor(xl[:, g * C:(g + 1) * C], PS[:, g, :], xh[:, g * C:(g + 1) * C], ALU.subtract)

        @block.vector
        def _(dve):
            ch = Chain(dve, dve_done)
            dif, mean, var, root, half, rstd, t = (st[:, i, :] for i in range(7))
            tt, ts = nc.vector.tensor_tensor, nc.vector.tensor_scalar
            for a in range(NT):
                ch.step(nc.vector.bn_stats(bn[:, a, :], X[:, a, :]))
            ch.wait()
            me, ve, mo, vo = (bn[:, :, i] for i in (1, 2, 4, 5))
            ch.step(tt(mean, me, mo, ALU.add))
            ch.step(tt(dif, me, mo, ALU.subtract))
            ch.then(tt(var, ve, vo, ALU.add))
            ch.then(tt(t, dif, dif, ALU.mult))
            ch.step(ts(mean, mean, 0.5, None, ALU.mult))
            ch.step(ts(t, t, 0.25, EPS, ALU.mult, ALU.add))
            ch.then(ts(var, var, 1.0 / E, None, ALU.mult))
            tt(var, var, t, ALU.add).then_inc(var_ready, 1)
            dve.wait_ge(root_ready, 1)
            ch.then(nc.vector.reciprocal(rstd, root))
            ch.then(tt(t, rstd, rstd, ALU.mult))
            ch.then(tt(half, t, var, ALU.mult))
            ch.then(ts(t, half, -0.5, 1.5, ALU.mult, ALU.add))
            ch.then(tt(half, t, rstd, ALU.mult))
            for a in range(NT):
                ts(nrm[:, a, :], X[:, a, :], mean[:, a:a + 1], half[:, a:a + 1],
                   ALU.subtract, ALU.mult).then_inc(norm_ready, 1)
                if a % 4 == 3 and a > 4:
                    low(dve, a // 4 - 1)
            low(dve, 3)

        @block.scalar
        def _(act):
            act.wait_ge(var_ready, 1)
            nc.scalar.activation(st[:, 3, :], st[:, 2, :], ACT.Sqrt).then_inc(root_ready, 1)
            for g in range(4):
                act.wait_ge(tr_ready, g + 1)
                nc.scalar.activation(xh[:, g * C:(g + 1) * C], PS[:, g, :], ACT.Copy).then_inc(hi_ready, 1)

        @block.tensor
        def _(pe):
            for g in range(4):
                for a in range(4):
                    pe.wait_ge(norm_ready, 4 * g + a + 1)
                    ins = nc.tensor.transpose(PS[:, g, a * P:(a + 1) * P], nrm[:, g * 4 + a, :], ident[:, :])
                ins.then_inc(tr_ready, 1)


def attention_core(nc, tag, c, PS, ident, causal, DQK):
    class A: pass
    A = A()
    sb = lambda n, s, d: c.enter_context(nc.sbuf_tensor(f"{tag}_{n}", s, d))
    sem = lambda n: c.enter_context(nc.semaphore(f"{tag}_{n}"))
    vm = VA if causal else P
    QS = A.QS = [sb(f"QS{j}", [P, S], f32r) for j in range(2)]
    K1 = A.K1 = [sb(f"K1{j}", [P, S], f32r) for j in range(2)]
    K2 = A.K2 = None if causal else [sb(f"K2{j}", [P, S], f32r) for j in range(2)]
    V = A.V = [sb(f"V{j}", [P, QT, vm], f32r) for j in range(2)]
    probs = A.probs = sb("probs", [P, 2, S], f32)
    prob = A.prob = [probs[:, j, :] for j in range(2)]
    PTh = [sb(f"PTh{i}", [P, QT, C], f32r) for i in range(2)]
    PTl = [sb(f"PTl{i}", [P, QT, C], f32r) for i in range(2)]
    nmax = sb("nmax", [P, 4], f32)
    A.rsum = sb("rsum", [P, 2, QT], f32)
    A.OT = [sb(f"OT{j}", [vm, S], f32) for j in range(2)]
    A.s_ready, A.max_ready, A.p_ready, A.t_ready, A.ph_ready, A.pl_ready, A.pv_ready, A.o_ready = (
        sem(n) for n in ("s_ready", "max_ready", "p_ready", "t_ready", "ph_ready", "pl_ready", "pv_ready", "o_ready"))
    TB = (4, 5, 7) if causal else (4, 5)
    PL0, O0 = len(TB), 1
    halves = [[(4 * h, min(4 * h + 4, qt + 1 if causal else QT)) for h in range(2) if not causal or 4 * h <= qt]
              for qt in range(QT)]
    halves_before = [sum(len(halves[k % QT]) for k in range(n)) for n in range(2 * QT + 1)]
    HP = halves_before[2 * QT]
    width = lambda qt: (qt + 1) * P if causal else S
    bank = lambda k: PS[:, 2 * (k % 2):2 * (k % 2) + 2, :]
    A.credits = (PL0, O0)

    def scores(it, k, maskr=None, identr=None, loaded=None):
        if k % QT == 0 and loaded:
            loaded(it, k)
        j, qt = (k // QT) % 2, k % QT
        q = QS[j][:, qt * P:(qt + 1) * P]
        w = width(qt)
        for h in range((w + C - 1) // C):
            n = min(C, w - h * C)
            out = PS[:, 2 * (k % 2) + h, 0:n]
            last = h == (w + C - 1) // C - 1
            ins = nc.tensor.matmul(out, q, K1[j][:, h * C:h * C + n], start=True, stop=causal and not last)
            if not causal:
                ins = nc.tensor.matmul(out, q, K2[j][:, h * C:h * C + n], start=False, stop=True)
            elif last:
                ins = nc.tensor.matmul(PS[:, 2 * (k % 2) + h, n - P:n], identr[:, :], maskr[:, :], start=False, stop=True)
        ins.then_inc(A.s_ready, 1)

    def transposes(pe, it, k):
        pe.wait_ge(A.p_ready, it * 16 + k + 1)
        for i, (a, b) in enumerate(halves[k % QT]):
            m = halves_before[k] + i
            pe.wait_ge(A.pl_ready, it * HP + m + 1)
            for kt in range(a, b):
                ins = nc.tensor.transpose(PS[:, TB[m % PL0], (kt - a) * P:(kt - a + 1) * P],
                                          prob[k % 2][:, kt * P:(kt + 1) * P], ident[:, :])
            ins.then_inc(A.t_ready, 1)

    def values(pe, it, k, v_in, unit=16):
        it, end, quarter = group_of(it, k)
        j, g = end // QT, (end % QT) // 4
        if quarter == 0:
            pe.wait_ge(A.pl_ready, it * HP + halves_before[end + 1] + PL0)
            pe.wait_ge(A.o_ready, it * 4 + 2 * j + g + O0)
            if g == 0:
                pe.wait_ge(v_in[j], unit * (it + 1))
        nk = 4 * g + 4 if causal else QT
        for kt in range(nk * quarter // 4, nk * (quarter + 1) // 4):
            q0 = max(0, kt - 4 * g) * P if causal else 0
            for part in (PTh[g], PTl[g]):
                ins = nc.tensor.matmul(PS[0:vm, 6, q0:C], V[j][:, kt, :], part[:, kt, q0:C],
                                       start=kt == 0 and part is PTh[g], stop=kt == nk - 1 and part is PTl[g])
        if quarter == 3:
            ins.then_inc(A.pv_ready, 1)

    def maximum(dve, it, k):
        dve.wait_ge(A.s_ready, it * 16 + k + 1)
        w = width(k % QT)
        src = flat(bank(k))[:, 0:w]
        nc.vector.tensor_reduce(nmax[:, k % 4:k % 4 + 1], src, AX.X, ALU.max, negate=True).then_inc(A.max_ready, 1)

    def exponent(act, it, k):
        act.wait_ge(A.max_ready, it * 16 + k + 1)
        w = width(k % QT)
        kw = {} if causal else {"accum_out": A.rsum[:, (k // QT) % 2, k % QT:k % QT + 1]}
        nc.scalar.activation(prob[k % 2][:, 0:w], flat(bank(k))[:, 0:w], ACT.Exp,
                             bias=nmax[:, k % 4:k % 4 + 1], scale=1.0, **kw).then_inc(A.p_ready, 1)

    def part(k, buf, a, b):
        return buf[(k // 4) % 2][:, a:b, (k % 4) * P:(k % 4 + 1) * P]

    def src(m, a, b):
        return PS[:, TB[m % PL0], 0:(b - a) * P].rearrange("p (a q) -> p a q", q=P)

    def high_parts(act, it, k):
        for i, (a, b) in enumerate(halves[k % QT]):
            m = halves_before[k] + i
            act.wait_ge(A.t_ready, it * HP + m + 1)
            nc.scalar.activation(part(k, PTh, a, b), src(m, a, b), ACT.Copy).then_inc(A.ph_ready, 1)

    def low_parts(dve, it, k):
        for i, (a, b) in enumerate(halves[k % QT]):
            m = halves_before[k] + i
            dve.wait_ge(A.ph_ready, it * HP + m + 1)
            nc.vector.tensor_tensor(part(k, PTl, a, b), src(m, a, b), part(k, PTh, a, b),
                                    ALU.subtract).then_inc(A.pl_ready, 1)

    def output(act, it, k, free=None):
        it, end, _ = group_of(it, k)
        j, g = end // QT, (end % QT) // 4
        act.wait_ge(A.pv_ready, it * 4 + 2 * j + g + 1)
        if free and g == 0:
            free(it, j)
        nc.scalar.activation(A.OT[j][:, g * C:(g + 1) * C], PS[0:vm, 6, :], ACT.Copy).then_inc(A.o_ready, 1)

    A.PTh = PTh
    A.scores, A.transposes, A.values, A.maximum, A.exponent = scores, transposes, values, maximum, exponent
    A.high_parts, A.low_parts, A.output = high_parts, low_parts, output
    return A


def attention_a(nc, X, xh, xl, ident, identr, maskr, PS, d):
    qk_dram = nc.dram_tensor("qk_a", [2, U, 2, DA, S], f32r, kind="Internal").ap()
    o_dram = nc.dram_tensor("o_a", [U, 2 * DA, S], f32, kind="Internal").ap()
    den_dram = nc.dram_tensor("den_a", [U, S], f32, kind="Internal").ap()
    with ExitStack() as outer:
        sb = lambda n, s, t: outer.enter_context(nc.sbuf_tensor(f"pa_{n}", s, t))
        sem = lambda n: outer.enter_context(nc.semaphore(f"aa_{n}"))
        A = attention_core(nc, "aa", outer, PS, ident, True, DA)
        PL0, O0 = A.credits
        Va = sb("Va", [P, U, QT, VA], f32r)
        wide_ld, split, zero_ready = sem("wide_ld"), sem("split"), sem("zero_ready")
        qk_st = [sem(f"qk_st{b}") for b in range(B)]
        qk_ld = [sem(f"qk_ld{j}") for j in range(2)]
        v_ld = [sem(f"v_ld{j}") for j in range(2)]
        o_st = [sem(f"o_st{j}") for j in range(2)]
        NP = U // 2

        def load_qk(sp, u, j):
            for r in range(2):
                sp.dma_start(words(A.QS[j][16 * r:16 * r + 16, :]),
                             words(qk_dram[0, u].rearrange("r d s -> (r d) s"))).then_inc(qk_ld[j], 16)
            for r in range(4):
                sp.dma_start(words(A.K1[j][8 * r:8 * r + 8, :]), words(qk_dram[1, u, r // 2])).then_inc(qk_ld[j], 16)

        def load_v(sp, u, j):
            sp.dma_start(words(A.V[j][:, :, :]), words(Va[:, u, :, :])).then_inc(v_ld[j], 16)

        with ExitStack() as c:
            sb = lambda n, s, t: c.enter_context(nc.sbuf_tensor(f"pa_{n}", s, t))
            sem = lambda n: c.enter_context(nc.semaphore(f"pa_{n}"))
            W = sb("W", [P, 5, P], f32)
            Wh = sb("Wh", [P, 5, P], f32r)
            Wl = sb("Wl", [P, 5, P], f32r)
            tab = sb("tab", [P, 4, S], f32)

            def prepare(block):
                @block.sync
                def _(sp):
                    sp.dma_start(W[:, :, :], d["a_w"].rearrange("k e f -> e k f")).then_inc(wide_ld, 16)
                    sp.dma_start(tab[:, :, :], d["a_tab"].rearrange("k f s -> f k s")).then_inc(wide_ld, 16)

                @block.gpsimd
                def _(pool):
                    pool.wait_ge(wide_ld, 32)
                    nc.gpsimd.tensor_copy(Wh[:, :, :], W[:, :, :]).then_inc(split, 1)
                    pool.wait_ge(split, 1)
                    nc.gpsimd.tensor_tensor(Wl[:, :, :], W[:, :, :], Wh[:, :, :], ALU.subtract).then_inc(split, 1)

            layernorm_transposed(nc, "ln1", X, xh, xl, ident, PS, prepare)

            qkh = sb("qkh", [P, 2, N], f32r)
            qkl = sb("qkl", [P, 2, N], f32r)
            more = sb("more", [P, 2, C], f32)
            T = [(A.prob[i][:, 0:C], A.prob[i][:, C:S]) for i in range(2)] + [(more[:, 0, :], more[:, 1, :])]
            rot = [sb(f"rot{i}", [P, C], f32)[:, :] for i in range(3)]
            mm, v_mm, v_hi, v_lo, mid, rot_ready, qk_hi, qk_done = (
                sem(n) for n in ("mm", "v_mm", "v_hi", "v_lo", "mid", "rot_ready", "qk_hi", "qk_done"))
            block = c.enter_context(nc.Block())
            rounds = [(b, w, t) for b in range(B) for w in range(2) for t in range(2)]
            NR = len(rounds)

            def store(eng, b, w):
                for prt, src in enumerate((qkh, qkl)):
                    eng.dma_start(words(qk_dram[w, b * HA:(b + 1) * HA, prt]),
                                  words(src[:, w, b * S:(b + 1) * S])).then_inc(qk_st[b], 16)

            @block.sync
            def _(sp):
                for w in range(2):
                    sp.wait_ge(qk_done, 2 * (w + 1))
                    store(sp, 0, w)
                sp.wait_ge(v_lo, NT)
                sp.wait_ge(zero_ready, 5)
                sp.wait_ge(qk_st[0], 64)
                load_qk(sp, 0, 0)
                load_v(sp, 0, 0)

            @block.tensor
            def _(pe):
                def rotary_rounds(first):
                    for n in range(first, first + 4):
                        b, w, t = rounds[n]
                        if n >= 2:
                            pe.wait_ge(mid, n - 1)
                        for r in range(2):
                            bk, i = PS[:, 2 * (n % 2) + r, :], 2 * w + r
                            x = slice(b * S + t * C, b * S + (t + 1) * C)
                            nc.tensor.matmul(bk, Wh[:, i, :], xl[:, x], start=True, stop=False)
                            nc.tensor.matmul(bk, Wl[:, i, :], xh[:, x], start=False, stop=False)
                            ins = nc.tensor.matmul(bk, Wh[:, i, :], xh[:, x], start=False, stop=True)
                        ins.then_inc(mm, 1)

                rotary_rounds(0)
                for t in range(NT):
                    bk = PS[:, 4 + t // 4, (t % 4) * P:(t % 4 + 1) * P]
                    x = slice(t * P, (t + 1) * P)
                    nc.tensor.matmul(bk, xl[:, x], Wh[:, 4, :], start=True, stop=False)
                    nc.tensor.matmul(bk, xh[:, x], Wl[:, 4, :], start=False, stop=False)
                    ins = nc.tensor.matmul(bk, xh[:, x], Wh[:, 4, :], start=False, stop=True)
                    if t % 4 == 3:
                        ins.then_inc(v_mm, 1)
                rotary_rounds(4)

            @block.vector
            def _(dve):
                def products(n):
                    b, w, t = rounds[n]
                    cs = slice(t * C, (t + 1) * C)
                    dve.wait_ge(mm, n + 1)
                    if n >= 3:
                        dve.wait_ge(rot_ready, n - 2)
                    nc.vector.tensor_tensor(T[n % 3][0], PS[:, 2 * (n % 2), :], tab[:, 2 * w, cs], ALU.mult)
                    nc.vector.tensor_tensor(T[n % 3][1], PS[:, 2 * (n % 2) + 1, :], tab[:, 2 * w + 1, cs],
                                            ALU.mult).then_inc(mid, 1)

                def low_parts(n):
                    b, w, t = rounds[n]
                    x = slice(b * S + t * C, b * S + (t + 1) * C)
                    dve.wait_ge(qk_hi, n + 1)
                    nc.vector.tensor_tensor(qkl[:, w, x], rot[n % 3], qkh[:, w, x], ALU.subtract).then_inc(qk_done, 1)

                for first in (0, 4):
                    products(first)
                    products(first + 1)
                    for n in range(first, first + 4):
                        if n + 2 < first + 4:
                            products(n + 2)
                        low_parts(n)
                    if first == 0:
                        for t in range(NT):
                            g, a = t // 4, t % 4
                            dve.wait_ge(v_hi, 4 * (g + 1))
                            v = Va[:, (t // QT) * HA:(t // QT + 1) * HA, t % QT, :]
                            nc.vector.tensor_tensor(v[:, :, DA:2 * DA],
                                                    PS[:, 4 + g, a * P:(a + 1) * P].rearrange("p (h d) -> p h d", d=DA),
                                                    v[:, :, 0:DA], ALU.subtract).then_inc(v_lo, 1)

            @block.gpsimd
            def _(pool):
                for n in range(NR):
                    if n == 4:
                        nc.gpsimd.memset(Va[:, :, :, 2 * DA:VA].bitcast(f32), 1.0).then_inc(zero_ready, 1)
                        for j in range(2):
                            nc.gpsimd.memset(A.QS[j][:, :].bitcast(f32), 0.0).then_inc(zero_ready, 1)
                            nc.gpsimd.memset(A.K1[j][:, :].bitcast(f32), 0.0).then_inc(zero_ready, 1)
                    pool.wait_ge(mid, n + 1)
                    if n >= 3:
                        pool.wait_ge(qk_done, n - 2)
                    nc.gpsimd.tensor_tensor(rot[n % 3], T[n % 3][0], T[n % 3][1], ALU.add).then_inc(rot_ready, 1)

            @block.scalar
            def _(act):
                for n, (b, w, t) in enumerate(rounds):
                    act.wait_ge(rot_ready, n + 1)
                    x = slice(b * S + t * C, b * S + (t + 1) * C)
                    nc.scalar.activation(qkh[:, w, x], rot[n % 3], ACT.Copy).then_inc(qk_hi, 1)
                    if n == 3:
                        for tile in range(NT):
                            g, a = tile // 4, tile % 4
                            act.wait_ge(v_mm, g + 1)
                            nc.scalar.activation(Va[:, (tile // QT) * HA:(tile // QT + 1) * HA, tile % QT, 0:DA],
                                                 PS[:, 4 + g, a * P:(a + 1) * P].rearrange("p (h d) -> p h d", d=DA),
                                                 ACT.Copy).then_inc(v_hi, 1)
                for w in range(2):
                    act.wait_ge(qk_done, 4 + 2 * (w + 1))
                    store(act, 1, w)

        with ExitStack() as c:
            block = c.enter_context(nc.Block())

            def each_pair(eng, body):
                body(0, True, False)
                with eng.Fori(1, NP - 1) as it:
                    body(it, False, False)
                body(NP - 1, False, True)

            @block.sync
            def _(sp):
                load_qk(sp, 1, 1)
                load_v(sp, 1, 1)

                def body(it, first, last):
                    for j in range(2):
                        u = it * 2 + j
                        if not last:
                            sp.wait_ge(A.s_ready, it * 16 + 8 * j + 8)
                            load_qk(sp, u + 2, j)
                            sp.wait_ge(A.pv_ready, it * 4 + 2 * j + 2)
                            load_v(sp, u + 2, j)
                        sp.wait_ge(A.o_ready, it * 4 + 2 * j + 2 + O0)
                        sp.dma_start(o_dram[u], A.OT[j][0:2 * DA, :]).then_inc(o_st[j], 16)
                        sp.dma_start(den_dram[u].unsqueeze(0), A.OT[j][2 * DA:VA, :]).then_inc(o_st[j], 16)
                    if first:
                        sp.wait_ge(qk_st[1], 64)
                each_pair(sp, body)
                for j in range(2):
                    sp.wait_ge(o_st[j], 32 * (NP + 1))

            @block.tensor
            def _(pe):
                def loaded(it, k):
                    j = (k // QT) % 2
                    pe.wait_ge(qk_ld[j], 96 * (it + k // 16 + 1))

                sc = lambda it, k: A.scores(it, k, maskr, identr, loaded)
                sc(0, 0)
                sc(0, 1)

                def body(it, first, last):
                    for k in range(16):
                        if not last or k < 14:
                            pe.wait_ge(A.p_ready, it * 16 + k + 1)
                            sc(it, k + 2)
                        if k % 4 != 0:
                            A.transposes(pe, it, k)
                        if not first or k > 4:
                            A.values(pe, it, k, v_ld)
                        if k % 4 == 0:
                            A.transposes(pe, it, k)
                each_pair(pe, body)
                for k in range(5):
                    A.values(pe, NP, k, v_ld)

            @block.scalar
            def _(act):
                def free(it, j):
                    act.wait_ge(o_st[j], 32 * (it + 1))

                A.exponent(act, 0, 0)

                def body(it, first, last):
                    for k in range(16):
                        if not last or k < 15:
                            A.exponent(act, it, k + 1)
                        if k % 4 == 0 and not (first and k <= 4):
                            A.output(act, it, k, free)
                        A.high_parts(act, it, k)
                each_pair(act, body)
                A.output(act, NP, 0, free)
                A.output(act, NP, 4, free)

            @block.vector
            def _(dve):
                nc.vector.memset(A.rsum[:, 0, 0:1], 0.0).then_inc(A.pl_ready, PL0)
                nc.vector.memset(A.rsum[:, 0, 1:2], 0.0).then_inc(A.o_ready, O0)
                for j in range(2):
                    nc.vector.memset(A.rsum[:, 1, j:j + 1], 0.0).then_inc(o_st[j], 32)
                A.maximum(dve, 0, 0)
                A.maximum(dve, 0, 1)

                def body(it, first, last):
                    for k in range(16):
                        if not last or k < 14:
                            A.maximum(dve, it, k + 2)
                        A.low_parts(dve, it, k)
                each_pair(dve, body)

    with ExitStack() as c:
        sb = lambda n, s, t: c.enter_context(nc.sbuf_tensor(f"oa_{n}", s, t))
        sem = lambda n: c.enter_context(nc.semaphore(f"oa_{n}"))
        oh = sb("oh", [P, B, S], f32)
        ol = sb("ol", [P, B, S], f32)
        rec = sb("rec", [P, B, S], f32)
        CH = P // U
        den = sb("den", [P, S // CH], f32)
        rden = sb("rden", [P, S // CH], f32)
        r_dram = nc.dram_tensor("rden_a", [U, S], f32, kind="Internal").ap()
        Wo = sb("Wo", [P, P], f32)
        den_ld, ld, rden_ready, rden_st, summed, o_norm, mm = (
            sem(n) for n in ("den_ld", "ld", "rden_ready", "rden_st", "summed", "o_norm", "mm"))
        rec_ld = [sem(f"rec_ld{b}") for b in range(B)]
        block = c.enter_context(nc.Block())

        @block.sync
        def _(sp):
            sp.dma_start(den[:, :], den_dram.rearrange("u (c s) -> (u c) s", c=CH)).then_inc(den_ld, 16)
            sp.wait_ge(rden_ready, 1)
            sp.dma_start(r_dram.rearrange("u (c s) -> (u c) s", c=CH), rden[:, :]).then_inc(rden_st, 16)
            sp.wait_ge(rden_st, 16)
            for b in range(B):
                sp.dma_start(rec[:, b, :], r_dram[b * HA:(b + 1) * HA].unsqueeze(1).broadcast_to([HA, DA, S])
                             ).then_inc(rec_ld[b], 16)

        @block.scalar
        def _(act):
            act.dma_start(Wo[:, :], d["a_wo"]).then_inc(ld, 16)
            for b in range(B):
                us = slice(b * HA, (b + 1) * HA)
                act.dma_start(oh[:, b, :], o_dram[us, 0:DA]).then_inc(ld, 16)
                act.dma_start(ol[:, b, :], o_dram[us, DA:2 * DA]).then_inc(ld, 16)

        @block.vector
        def _(dve):
            dve.wait_ge(den_ld, 16)
            nc.vector.reciprocal(rden[:, :], den[:, :]).then_inc(rden_ready, 1)
            dve.wait_ge(ld, 16 * (1 + 2 * B))
            nc.vector.tensor_tensor(flat(oh[:, :, :]), flat(oh[:, :, :]), flat(ol[:, :, :]), ALU.add).then_inc(summed, 1)
            dve.wait_ge(summed, 1)
            for b in range(B):
                dve.wait_ge(rec_ld[b], 16)
                nc.vector.tensor_tensor(ol[:, b, :], oh[:, b, :], rec[:, b, :], ALU.mult).then_inc(o_norm, 1)
            for g in range(4):
                dve.wait_ge(mm, g + 1)
                x = flat(X[:, 4 * g:4 * g + 4, :])
                nc.vector.tensor_tensor(x, x, PS[:, g, :], ALU.add)

        @block.tensor
        def _(pe):
            for t in range(NT):
                if t % QT == 0:
                    pe.wait_ge(o_norm, t // QT + 1)
                ins = nc.tensor.matmul(PS[:, t // 4, (t % 4) * P:(t % 4 + 1) * P],
                                       flat(ol[:, :, :])[:, t * P:(t + 1) * P], Wo[:, :], start=True, stop=True)
                if t % 4 == 3:
                    ins.then_inc(mm, 1)


def experts(nc, tag, X, xh, xl, PS, d, ident, cw_dram):
    WC = 3 * HID
    with ExitStack() as c:
        sb = lambda n, s, t: c.enter_context(nc.sbuf_tensor(f"{tag}_{n}", s, t))
        sem = lambda n: c.enter_context(nc.semaphore(f"{tag}_{n}"))
        raw = [sb(f"raw{j}", [P, WC], f32) for j in range(2)]
        wh = [sb(f"wh{j}", [P, WC], f32r) for j in range(2)]
        wl = [sb(f"wl{j}", [P, WC], f32r) for j in range(2)]
        cw = [sb(f"cw{j}", [P, N], f32) for j in range(2)]
        sl = [sb(f"sl{i}", [P, C], f32) for i in range(4)]
        G = [sb(f"G{i}", [P, C], f32) for i in range(4)]
        Gh = [sb(f"Gh{i}", [P, C], f32r) for i in range(4)]
        Gl = [sb(f"Gl{i}", [P, C], f32r) for i in range(4)]
        tmp = [sb(f"tmp{i}", [P, C], f32) for i in range(2)]
        acc = sb("acc", [P, N], f32)
        h_ready, silu_ready, g_ready, gh_ready, gl_ready, y_ready, tmp_ready, acc_ready, w_hi, w_ready, tr, held = (
            sem(n) for n in ("h_ready", "silu_ready", "g_ready", "gh_ready", "gl_ready", "y_ready", "tmp_ready",
                             "acc_ready", "w_hi", "w_ready", "tr", "held"))
        w_ld = [sem(f"w_ld{j}") for j in range(2)]
        cw_ld = [sem(f"cw_ld{j}") for j in range(2)]
        NI = NX // 2
        rw = sb("rw", [P, NE], f32)
        rwp = sb("rwp", [P, 2 * NE], f32r)
        rwh, rwl = rwp[:, 0:NE], rwp[:, NE:2 * NE]
        bias = sb("bias", [P, NE], f32)
        rank = sb("rank", [P, NE], f32)
        lg, lg2, eq, cand, one1, one2, cmb = (
            sb(n, [P, NT, NE], f32)[:, :, :] for n in ("lg", "lg2", "eq", "cand", "one1", "one2", "cmb"))
        v = sb("v", [P, 8, NT], f32)
        m1, m2, dif, e, den, w1, w2, top = (v[:, i, :] for i in range(8))
        cT = sb("cT", [P, P], f32)
        r_ld, r_split, logits, low_logits, routed, exp_ready, cmb_tr, cT_ready, cw_st = (
            sem(n) for n in ("r_ld", "r_split", "logits", "low_logits", "routed", "exp_ready", "cmb_tr", "cT_ready", "cw_st"))
        wide = lambda a: a.unsqueeze(2).broadcast_to([P, NT, NE])
        rows = lambda a: a.unsqueeze(1).broadcast_to([P, NT, NE])
        DIF, CMB = 12, 18

        def split(pool, e, i, j):
            pool.wait_ge(w_ld[j], 16 * (i + 1))
            hold(pool, held)
            nc.gpsimd.tensor_copy(wh[j][:, :], raw[j][:, :]).then_inc(w_hi, 1)
            pool.wait_ge(w_hi, e + 1)
            nc.gpsimd.tensor_tensor(wl[j][:, :], raw[j][:, :], wh[j][:, :], ALU.subtract).then_inc(w_ready, 1)

        def prepare(block):
            @block.sync
            def _(sp):
                for j in range(2):
                    sp.dma_start(raw[j][:, :], d["f_w"][j]).then_inc(w_ld[j], 16)
                sp.dma_start(rw[:, :], d["router"]).then_inc(r_ld, 16)
                sp.dma_start(bias[:, :], d["ebias"].broadcast_to([P, NE])).then_inc(r_ld, 16)
                sp.dma_start(rank[:, :], d["rank"].broadcast_to([P, NE])).then_inc(r_ld, 16)

            @block.gpsimd
            def _(pool):
                split(pool, 0, 0, 0)
                pool.wait_ge(r_ld, 48)
                nc.gpsimd.tensor_copy(rwh, rw[:, :]).then_inc(r_split, 1)
                pool.wait_ge(r_split, 1)
                nc.gpsimd.tensor_tensor(rwl, rw[:, :], rwh, ALU.subtract).then_inc(r_split, 1)
                split(pool, 1, 0, 1)

        layernorm_transposed(nc, f"{tag}_ln", X, xh, xl, ident, PS, prepare)
        block = c.enter_context(nc.Block())

        def each_pair(eng, body):
            body(0, True, False)
            with eng.Fori(1, NI - 1) as i:
                body(i, False, False)
            body(NI - 1, False, True)

        @block.sync
        def _(sp):
            def body(i, first, last):
                if last:
                    return
                for j in range(2):
                    e = i * 2 + j
                    sp.wait_ge(w_ready, e + 1)
                    sp.dma_start(raw[j][:, :], d["f_w"][e + 2]).then_inc(w_ld[j], 16)
                    if first and j == 0:
                        sp.wait_ge(cT_ready, 1)
                        sp.dma_start(cw_dram.rearrange("t e p -> (t e) p"), cT[:, :]).then_inc(cw_st, 16)
                        sp.wait_ge(cw_st, 16)
                    sp.wait_ge(tmp_ready, e * 4 + 4)
                    sp.dma_start(cw[j][:, :].rearrange("p (t q) -> p t q", q=P),
                                 cw_dram[:, e, :].unsqueeze(0).broadcast_to([P, NT, P])).then_inc(cw_ld[j], 16)
            each_pair(sp, body)

        @block.gpsimd
        def _(pool):
            for j in range(2):
                nc.gpsimd.memset(cw[j][:, :], 1.0).then_inc(cw_ld[j], 16)

            def body(i, first, last):
                for j in range(2):
                    for t in range(4):
                        n = i * 8 + j * 4 + t
                        a = acc[:, t * C:(t + 1) * C]
                        pool.wait_ge(tmp_ready, n + 1)
                        if first and j == 0:
                            nc.gpsimd.tensor_copy(a, tmp[t % 2][:, :]).then_inc(acc_ready, 1)
                        else:
                            pool.wait_ge(acc_ready, n - 3)
                            nc.gpsimd.tensor_tensor(a, a, tmp[t % 2][:, :], ALU.add).then_inc(acc_ready, 1)
                    if not last:
                        split(pool, i * 2 + j + 2, i + 1, j)
            each_pair(pool, body)

        @block.tensor
        def _(pe):
            def up(i, w):
                j, t, hh = (w // 8) % 2, (w // 2) % 4, w % 2
                if w % 8 == 0:
                    pe.wait_ge(w_ready, i * 2 + w // 8 + 1)
                if not (isinstance(i, int) and i == 0 and w < 2):
                    pe.wait_ge(g_ready, i * 16 + w - 1)
                x = slice(t * C, (t + 1) * C)
                for bk, col in ((hh, hh * P), (2 + hh, HID + hh * P)):
                    cs = slice(col, col + P)
                    nc.tensor.matmul(PS[:, bk, :], wh[j][:, cs], xl[:, x], start=True, stop=False)
                    nc.tensor.matmul(PS[:, bk, :], wl[j][:, cs], xh[:, x], start=False, stop=False)
                    ins = nc.tensor.matmul(PS[:, bk, :], wh[j][:, cs], xh[:, x], start=False, stop=True)
                ins.then_inc(h_ready, 1)

            def down(i, first, n):
                j, t = n // 4, n % 4
                pe.wait_ge(gl_ready, i * 16 + 2 * n + 2)
                if not first or n >= 2:
                    pe.wait_ge(tmp_ready, i * 8 + n - 1)
                for hh in range(2):
                    cs = slice(2 * HID + hh * P, 2 * HID + hh * P + P)
                    s = (2 * n + hh) % 4
                    nc.tensor.matmul(PS[:, 4 + n % 2, :], wh[j][:, cs], Gl[s][:, :], start=hh == 0, stop=False)
                    nc.tensor.matmul(PS[:, 4 + n % 2, :], wl[j][:, cs], Gh[s][:, :], start=False, stop=False)
                    ins = nc.tensor.matmul(PS[:, 4 + n % 2, :], wh[j][:, cs], Gh[s][:, :], start=False, stop=hh == 1)
                ins.then_inc(y_ready, 1)

            for w in range(3):
                up(0, w)
            for t in range(NT):
                o = PS[:, 6, t * 2 * NE:(t + 1) * 2 * NE]
                x = slice(t * P, (t + 1) * P)
                nc.tensor.matmul(o, xl[:, x], rwp[:, :], start=True, stop=False)
                ins = nc.tensor.matmul(o, xh[:, x], rwp[:, :], start=False, stop=True)
            ins.then_inc(logits, 1)

            def body(i, first, last):
                for n in range(8):
                    if first and n == 6:
                        pe.wait_ge(routed, CMB + 1)
                        nc.tensor.transpose(PS[:, 7, 0:P], flat(cmb), ident[:, :]).then_inc(cmb_tr, 1)
                    for w in (2 * n + 3, 2 * n + 4):
                        if not last or w < 16:
                            up(i, w)
                    down(i, first, n)
            each_pair(pe, body)
            pe.wait_ge(acc_ready, 4 * NX)
            for t in range(NT):
                ins = nc.tensor.transpose(PS[:, t // 4, (t % 4) * P:(t % 4 + 1) * P], acc[:, t * P:(t + 1) * P], ident[:, :])
                if t % 4 == 3:
                    ins.then_inc(tr, 1)

        @block.scalar
        def _(act):
            def silu(i, w):
                act.wait_ge(h_ready, i * 16 + w + 1)
                nc.scalar.activation(sl[w % 4][:, :], PS[:, w % 2, :], ACT.Silu).then_inc(silu_ready, 1)

            def high(i, w):
                act.wait_ge(g_ready, i * 16 + w + 1)
                nc.scalar.activation(Gh[w % 4][:, :], G[w % 4][:, :], ACT.Copy).then_inc(gh_ready, 1)

            silu(0, 0)

            def body(i, first, last):
                for w in range(16):
                    if not last or w < 15:
                        silu(i, w + 1)
                    high(i, w)
                    if first and w == 8:
                        act.wait_ge(routed, DIF + 1)
                        nc.scalar.activation(e, dif, ACT.Exp).then_inc(exp_ready, 1)
            each_pair(act, body)

        @block.vector
        def _(dve):
            tt = nc.vector.tensor_tensor

            def gate(i, w):
                dve.wait_ge(silu_ready, i * 16 + w + 1)
                nc.vector.tensor_tensor(G[w % 4][:, :], sl[w % 4][:, :], PS[:, 2 + w % 2, :], ALU.mult).then_inc(g_ready, 1)

            def low(i, w):
                dve.wait_ge(gh_ready, i * 16 + w + 1)
                nc.vector.tensor_tensor(Gl[w % 4][:, :], G[w % 4][:, :], Gh[w % 4][:, :], ALU.subtract).then_inc(gl_ready, 1)

            def weigh(i, n, skip_free):
                j, t = (n // 4) % 2, n % 4
                if t == 0:
                    dve.wait_ge(cw_ld[j], 16 * (i + 1))
                dve.wait_ge(y_ready, i * 8 + n + 1)
                if not skip_free:
                    dve.wait_ge(acc_ready, i * 8 + n - 1)
                nc.vector.tensor_tensor(tmp[n % 2][:, :], PS[:, 4 + n % 2, :], cw[j][:, t * C:(t + 1) * C],
                                        ALU.mult).then_inc(tmp_ready, 1)

            def pick(p, scores, mx, one):
                if p == 0:
                    return nc.vector.tensor_reduce(mx, scores, AX.X, ALU.max)
                if p == 1:
                    return tt(eq, scores, wide(mx), ALU.is_equal)
                if p == 2:
                    return tt(cand, eq, rows(rank[:, :]), ALU.mult)
                if p == 3:
                    return nc.vector.tensor_reduce(top, cand, AX.X, ALU.max)
                return tt(one, rows(rank[:, :]), wide(top), ALU.is_equal)

            def route(s):
                if s == 0:
                    dve.wait_ge(logits, 1)
                    both = PS[:, 6, 0:NT * 2 * NE].rearrange("p (t e) -> p t e", e=2 * NE)
                    tt(lg2, both[:, :, NE:2 * NE], rows(bias[:, :]), ALU.add).then_inc(low_logits, 1)
                    dve.wait_ge(low_logits, 1)
                    ins = tt(lg, both[:, :, 0:NE], lg2, ALU.add)
                else:
                    dve.wait_ge(routed, s)
                if 1 <= s <= 5:
                    ins = pick(s - 1, lg, m1, one1)
                if s == 6:
                    ins = nc.vector.scalar_tensor_tensor(lg2, one1, -BIG, lg, ALU.mult, ALU.add)
                if 7 <= s <= 11:
                    ins = pick(s - 7, lg2, m2, one2)
                if s == DIF:
                    ins = tt(dif, m2, m1, ALU.subtract)
                if s == 13:
                    dve.wait_ge(exp_ready, 1)
                    ins = nc.vector.tensor_scalar(den, e, 1.0, None, ALU.add)
                if s == 14:
                    ins = nc.vector.reciprocal(w1, den)
                if s == 15:
                    ins = tt(w2, e, w1, ALU.mult)
                if s == 16:
                    ins = tt(cand, one1, wide(w1), ALU.mult)
                if s == 17:
                    ins = tt(eq, one2, wide(w2), ALU.mult)
                if s == CMB:
                    ins = tt(cmb, cand, eq, ALU.add)
                ins.then_inc(routed, 1)

            gate(0, 0)

            def body(i, first, last):
                for w in range(16):
                    if not last or w < 15:
                        gate(i, w + 1)
                    low(i, w)
                    if first and 1 <= w <= 7:
                        for s in range(2 * w - 2, min(2 * w, DIF + 1)):
                            route(s)
                    if first and 9 <= w <= 11:
                        for s in range(2 * w - 5, 2 * w - 3):
                            route(s)
                    if first and w == 15:
                        dve.wait_ge(cmb_tr, 1)
                        nc.vector.tensor_copy(cT[:, :], PS[:, 7, 0:P]).then_inc(cT_ready, 1)
                    if w % 2 == 1 and w >= 3:
                        weigh(i, w // 2 - 1, first and w <= 5)
                    elif w == 1 and not first:
                        weigh(i - 1, 7, False)
                if last:
                    weigh(i, 7, False)
            each_pair(dve, body)
            for g in range(4):
                dve.wait_ge(tr, g + 1)
                x = flat(X[:, 4 * g:4 * g + 4, :])
                nc.vector.tensor_tensor(x, x, PS[:, g, :], ALU.add)


def attention_b(nc, X, xh, xl, ident, PS, d):
    v_dram = nc.dram_tensor("v_b", [B, QT, P, HB // 2, 2 * DB], f32, kind="Internal").ap()
    with ExitStack() as c:
        sb = lambda n, s, t: c.enter_context(nc.sbuf_tensor(f"ab_{n}", s, t))
        sem = lambda n: c.enter_context(nc.semaphore(f"ab_{n}"))
        A = attention_core(nc, "ab", c, PS, ident, False, DB)
        PL0, O0 = A.credits
        NP = U // 2
        HPB = HB // 2
        tab = sb("tab", [P, 4, S], f32)
        Wall = sb("Wall", [P, HPB, 4, P], bf16)
        ball = sb("ball", [P, HPB, 4], bf16)
        Wst = sb("Wst", [P, 4, P], f32r)
        bst = sb("bst", [P, 4], f32)
        Wo = sb("Wo", [P, HB, E], bf16)
        Wo32 = sb("Wo32", [P, HB, E], f32)
        bob = sb("bob", [P, E], bf16)
        VS = sb("VS", [P, QT, 2 * DB], f32)
        T1 = [sb(f"T1{w}", [P, S], f32) for w in range(2)]
        T2 = [sb(f"T2{w}", [P, S], f32) for w in range(2)]
        rh = [sb(f"rh{w}", [P, S], f32r) for w in range(2)]
        rl = [T2[w][:, :].bitcast(f32r) for w in range(2)]
        rden = sb("rden", [P, 2, QT], f32)
        ld, wst_ready, r_full, r_free, parts_done, parts_ready, den_ready, proj_ready, proj_add, wo_ready, held = (
            sem(n) for n in ("ld", "wst_ready", "r_full", "r_free", "parts_done", "parts_ready", "den_ready",
                             "proj_ready", "proj_add", "wo_ready", "held"))
        qk_ld = [sem(f"qk_ld{j}") for j in range(2)]
        v_ld = sem("v_ld")
        v_hi = [sem(f"v_hi{j}") for j in range(2)]
        v_in = [sem(f"v_in{j}") for j in range(2)]
        all_ld, w_ld, filled, w_ready = (sem(n) for n in ("all_ld", "w_ld", "filled", "w_ready"))

        Wb = rh[0][:, 0:C].bitcast(bf16)
        bb = rh[0][0:1, C:S].bitcast(bf16)
        W = flat(A.PTh[0][:, 0:2, :])
        brow = flat(A.PTh[0][:, 2:4, :])
        one = A.PTh[0][:, 4, 0:P]

        def load_qk(sp, j, pair):
            rows = slice(j * DB, (j + 1) * DB)
            sp.wait_ge(parts_ready, 2 * pair + 2)
            for dst, top, bot in ((A.QS[j], rh[0], rl[0]), (A.K1[j], rh[1], rh[1]), (A.K2[j], rl[1], rl[1])):
                sp.dma_start(words(dst[0:DB, :]), words(top[rows, :])).then_inc(qk_ld[j], 16)
                sp.dma_start(words(dst[DB:P, :]), words(bot[rows, :])).then_inc(qk_ld[j], 16)

        def load_v(sp, pair):
            sp.dma_start(VS[:, :, :], v_dram[pair // HPB, :, :, pair % HPB, :].rearrange("t p c -> p t c")).then_inc(v_ld, 16)

        def split_v(pool, j, pair):
            v = VS[:, :, j * DB:(j + 1) * DB]
            pool.wait_ge(v_ld, 16 * (pair + 1))
            hold(pool, held)
            nc.gpsimd.tensor_copy(A.V[j][:, :, 0:DB], v).then_inc(v_hi[j], 1)
            pool.wait_ge(v_hi[j], pair + 1)
            nc.gpsimd.tensor_tensor(A.V[j][:, :, DB:2 * DB], v, A.V[j][:, :, 0:DB],
                                    ALU.subtract).then_inc(v_in[j], 1)

        def round_table(r):
            return 2 * (r // 4) + r % 2, (r // 2) % 2

        def project(pe, pair, r):
            kind, h = round_table(r)
            if r == 0:
                pe.wait_ge(wst_ready, 2 * pair + 2)
                if not (isinstance(pair, int) and pair <= 1):
                    pe.wait_ge(proj_add, 4 * pair - 5)
            pe.wait_ge(r_free, pair * 8 + r + 1)
            x = bass.ds((pair // HPB) * S + h * C, C)
            nc.tensor.matmul(PS[:, 7, :], Wst[:, kind, :], xl[:, x], start=True, stop=False)
            nc.tensor.matmul(PS[:, 7, :], Wst[:, kind, :], xh[:, x], start=False, stop=True).then_inc(r_full, 1)

        def rotate(dve, pair, r):
            kind, h = round_table(r)
            w = kind // 2
            dve.wait_ge(r_full, pair * 8 + r + 1)
            if r % 4 == 0 and not (isinstance(pair, int) and pair == 0):
                dve.wait_ge(parts_ready, 2 * pair)
            if r == 1 and not (isinstance(pair, int) and pair == 0):
                for j in range(2):
                    dve.wait_ge(qk_ld[j], 96 * pair)
            T = (T1, T2)[kind % 2][w]
            cs = slice(h * C, (h + 1) * C)
            nc.vector.scalar_tensor_tensor(T[:, cs], PS[:, 7, :], bst[:, kind:kind + 1], tab[:, kind, cs],
                                           ALU.add, ALU.mult).then_inc(r_free, 1)

        def stage_weights(pool, pair):
            p = pair % HPB
            nc.gpsimd.tensor_copy(Wst[:, :, :], Wall[:, p, :, :]).then_inc(wst_ready, 1)
            nc.gpsimd.tensor_copy(bst[:, :], ball[:, p, :]).then_inc(wst_ready, 1)

        def make_parts(pool, w, pair):
            pool.wait_ge(r_free, pair * 8 + 4 * w + 5)
            nc.gpsimd.tensor_tensor(T1[w][:, :], T1[w][:, :], T2[w][:, :], ALU.add).then_inc(parts_done, 1)
            pool.wait_ge(parts_done, pair * 4 + 2 * w + 1)
            hold(pool, held)
            nc.gpsimd.tensor_copy(rh[w][:, :], T1[w][:, :]).then_inc(parts_done, 1)
            pool.wait_ge(parts_done, pair * 4 + 2 * w + 2)
            nc.gpsimd.tensor_tensor(rl[w][:, :], T1[w][:, :], rh[w][:, :], ALU.subtract).then_inc(parts_ready, 1)

        def prepare(block):
            @block.sync
            def _(sp):
                sp.dma_start(Wall[:, :, :, :], d["b_wqk"]).then_inc(all_ld, 16)
                sp.dma_start(ball[:, :, :], d["b_bqk"]).then_inc(all_ld, 16)
                sp.dma_start(Wb, d["b_wv"]).then_inc(w_ld, 16)
                sp.dma_start(bb, d["b_bv"]).then_inc(w_ld, 16)
                sp.dma_start(tab[:, :, :], d["b_tab"].rearrange("k f s -> f k s")).then_inc(ld, 16)
                sp.dma_start(Wo[:, :, :], d["b_wo"]).then_inc(ld, 16)
                sp.dma_start(bob[:, :], d["b_bo"].broadcast_to([P, E])).then_inc(ld, 16)

            @block.gpsimd
            def _(pool):
                nc.gpsimd.memset(brow.bitcast(f32), 0.0).then_inc(filled, 1)
                nc.gpsimd.memset(one.bitcast(f32), 0.0).then_inc(filled, 1)
                pool.wait_ge(filled, 2)
                nc.gpsimd.memset(one[0:1, :].bitcast(f32), 1.0).then_inc(w_ready, 1)
                pool.wait_ge(all_ld, 32)
                stage_weights(pool, 0)
                pool.wait_ge(w_ld, 32)
                nc.gpsimd.tensor_copy(W, Wb).then_inc(w_ready, 1)

        layernorm_transposed(nc, "ln3", X, xh, xl, ident, PS, prepare,
                             flat(A.probs[:, :, :]).rearrange("p (t e) -> p t e", e=E))

        with ExitStack() as cv:
            sem = lambda n: cv.enter_context(nc.semaphore(f"vb_{n}"))
            NS, NB = 4, 3
            vp = [A.prob[0], A.prob[1], A.OT[0][:, :], A.OT[1][:, :]]
            mm, out = sem("mm"), sem("out")
            st = [sem(f"st{i}") for i in range(NS)]
            block = cv.enter_context(nc.Block())

            @block.sync
            def _(sp):
                for t in range(NT):
                    b, kt = t // QT, t % QT
                    sp.wait_ge(out, t + 1)
                    sp.dma_start(v_dram[b, kt].rearrange("p h c -> p (h c)"), vp[t % NS]).then_inc(st[t % NS], 16)
                    if t == 13:
                        load_qk(sp, 0, 0)
                for i in range(NS):
                    sp.wait_ge(st[i], 16 * (NT // NS))

            @block.gpsimd
            def _(pool):
                pool.wait_ge(w_ready, 3)
                make_parts(pool, 0, 0)
                make_parts(pool, 1, 0)

            @block.tensor
            def _(pe):
                for t in range(NT):
                    if t < 4:
                        project(pe, 0, 2 * t)
                    if t == 0:
                        pe.wait_ge(w_ready, 3)
                    if t >= NB:
                        pe.wait_ge(out, t - NB + 1)
                    x = slice(t * P, (t + 1) * P)
                    for h in range(2):
                        if h == 1 and t < 4:
                            project(pe, 0, 2 * t + 1)
                        o, cs = PS[:, 2 * (t % NB) + h, :], slice(h * C, (h + 1) * C)
                        nc.tensor.matmul(o, one, brow[:, cs], start=True, stop=False)
                        nc.tensor.matmul(o, xl[:, x], W[:, cs], start=False, stop=False)
                        ins = nc.tensor.matmul(o, xh[:, x], W[:, cs], start=False, stop=True)
                    ins.then_inc(mm, 1)

            @block.scalar
            def _(act):
                for t in range(NT):
                    act.wait_ge(mm, t + 1)
                    if t >= NS:
                        act.wait_ge(st[t % NS], 16 * (t // NS))
                    nc.scalar.activation(vp[t % NS], flat(PS[:, 2 * (t % NB):2 * (t % NB) + 2, :]),
                                         ACT.Copy).then_inc(out, 1)

            @block.vector
            def _(dve):
                nc.vector.memset(A.rsum[:, 0, 0:1], 0.0).then_inc(A.pl_ready, PL0)
                nc.vector.memset(A.rsum[:, 0, 1:2], 0.0).then_inc(A.o_ready, O0)
                nc.vector.memset(A.rsum[:, 0, 2:3], 0.0).then_inc(r_free, 1)
                nc.vector.memset(A.rsum[:, 0, 3:4], 0.0).then_inc(proj_add, 1)
                dve.wait_ge(ld, 48)
                dve.wait_ge(w_ld, 32)
                dve.wait_ge(filled, 2)
                nc.vector.tensor_copy(brow[0:1, :], bb).then_inc(w_ready, 1)
                for r in range(8):
                    rotate(dve, 0, r)
                nc.vector.tensor_tensor(X[:, :, :], X[:, :, :], bob[:, :].unsqueeze(1).broadcast_to([P, NT, E]), ALU.add)

        block = c.enter_context(nc.Block())

        def each_pair(eng, body):
            body(0, True, False)
            with eng.Fori(1, NP - 1) as it:
                body(it, False, False)
            body(NP - 1, False, True)

        @block.sync
        def _(sp):
            load_v(sp, 0)
            load_qk(sp, 1, 0)

            def body(it, first, last):
                if last:
                    return
                for j in range(2):
                    sp.wait_ge(v_in[j], it + 1)
                load_v(sp, it + 1)
                sp.wait_ge(A.s_ready, it * 16 + 8)
                load_qk(sp, 0, it + 1)
                sp.wait_ge(A.s_ready, it * 16 + 16)
                load_qk(sp, 1, it + 1)
            each_pair(sp, body)

        @block.gpsimd
        def _(pool):
            for j in range(2):
                split_v(pool, j, 0)
            pool.wait_ge(ld, 48)
            nc.gpsimd.tensor_copy(Wo32[:, :, :], Wo[:, :, :]).then_inc(wo_ready, 1)

            def body(it, first, last):
                if not last:
                    pool.wait_ge(r_free, it * 8 + 9)
                    hold(pool, held)
                    stage_weights(pool, it + 1)
                    for j in range(2):
                        pool.wait_ge(qk_ld[j], 96 * (it + 1))
                    make_parts(pool, 0, it + 1)
                if not first:
                    pool.wait_ge(A.pv_ready, it * 4)
                    split_v(pool, 1, it)
                if not last:
                    make_parts(pool, 1, it + 1)
                    pool.wait_ge(A.pv_ready, it * 4 + 2)
                    split_v(pool, 0, it + 1)
            each_pair(pool, body)

        @block.tensor
        def _(pe):
            def out_project(it, j, half, rounds):
                pe.wait_ge(A.o_ready, it * 4 + 2 * j + 2 + O0)
                pe.wait_ge(proj_add, it * 4 + 2 * j + half + 1)
                if rounds is not None and half == 0:
                    pe.wait_ge(r_free, rounds + 1)
                h = (it * 2 + j) % HB
                for a in range(4):
                    qt = 4 * half + a
                    ins = nc.tensor.matmul(PS[:, 7, a * P:(a + 1) * P],
                                           A.OT[j][:, qt * P:(qt + 1) * P], Wo32[:, h, :], start=True, stop=True)
                ins.then_inc(proj_ready, 1)

            def loaded(it, k):
                j = (k // QT) % 2
                pe.wait_ge(qk_ld[j], 96 * (it + k // 16 + 1))

            sc = lambda it, k: A.scores(it, k, loaded=loaded)
            sc(0, 0)
            sc(0, 1)

            def body(it, first, last):
                for k in range(16):
                    if not last or k < 14:
                        pe.wait_ge(A.p_ready, it * 16 + k + 1)
                        sc(it, k + 2)
                    if not first or k > 4:
                        A.values(pe, it, k, v_in, 1)
                    if k < 8 and not last:
                        project(pe, it + 1, k)
                    if k in (8, 9) and not first:
                        out_project(it - 1, 1, k - 8, None if last else it * 8 + 16)
                    if first and k == 13:
                        pe.wait_ge(wo_ready, 1)
                    if k in (13, 14):
                        out_project(it, 0, k - 13, None if last else it * 8 + 16)
                    A.transposes(pe, it, k)
            each_pair(pe, body)
            for k in range(5):
                A.values(pe, NP, k, v_in, 1)
            for h in range(2):
                out_project(NP - 1, 1, h, None)

        @block.scalar
        def _(act):
            A.exponent(act, 0, 0)

            def body(it, first, last):
                for k in range(16):
                    if not last or k < 15:
                        A.exponent(act, it, k + 1)
                    if k % 4 == 0 and not (first and k <= 4):
                        A.output(act, it, k)
                    A.high_parts(act, it, k)
            each_pair(act, body)
            A.output(act, NP, 0)
            A.output(act, NP, 4)

        @block.vector
        def _(dve):
            def invert(it, j):
                dve.wait_ge(A.p_ready, it * 16 + 8 * j + 8)
                nc.vector.reciprocal(rden[:, j, :], A.rsum[:, j, :]).then_inc(den_ready, 1)

            def add_head(it, j, half):
                if half == 0:
                    dve.wait_ge(den_ready, it * 2 + j + 1)
                dve.wait_ge(proj_ready, it * 4 + 2 * j + half + 1)
                b = ((it * 2 + j) // HB)
                for a in range(4):
                    qt = 4 * half + a
                    x = X[:, b * QT + qt, :]
                    ins = nc.vector.scalar_tensor_tensor(x, PS[:, 7, a * P:(a + 1) * P],
                                                         rden[:, j, qt:qt + 1], x, ALU.mult, ALU.add)
                ins.then_inc(proj_add, 1)

            A.maximum(dve, 0, 0)
            A.maximum(dve, 0, 1)

            def body(it, first, last):
                for k in range(16):
                    if not last or k < 14:
                        A.maximum(dve, it, k + 2)
                    if k < 8 and not last:
                        rotate(dve, it + 1, k)
                    if k == 3 and not first:
                        invert(it - 1, 1)
                    if k in (8, 9) and not first:
                        add_head(it - 1, 1, k - 8)
                    if k == 11:
                        invert(it, 0)
                    if k in (13, 14):
                        add_head(it, 0, k - 13)
                    A.low_parts(dve, it, k)
            each_pair(dve, body)
            invert(NP - 1, 1)
            for h in range(2):
                add_head(NP - 1, 1, h)


def program(nc, d, out):
    with ExitStack() as c:
        sb = lambda n, s, t: c.enter_context(nc.sbuf_tensor(n, s, t))
        sem = lambda n: c.enter_context(nc.semaphore(n))
        X = sb("X", [P, NT, E], f32)
        xh = sb("xh", [P, N], f32r)
        xl = sb("xl", [P, N], f32r)
        ident = sb("ident", [P, P], f32)
        identr = sb("identr", [P, P], f32r)
        mask = sb("mask", [P, P], f32)
        maskr = sb("maskr", [P, P], f32r)
        PS = c.enter_context(nc.psum_tensor("PS", [P, 8, C], f32))
        cw_dram = [nc.dram_tensor(f"cw{i}", [NT, NE, P], f32, kind="Internal").ap() for i in range(2)]
        ld, made, st = sem("x_ld"), sem("const_made"), sem("out_st")
        x_dram = d["x"].rearrange("b (t p) e -> p (b t) e", p=P)
        with nc.Block() as block:
            @block.sync
            def _(sp):
                sp.dma_start(X[:, :, :], x_dram).then_inc(ld, 16)
                sp.wait_ge(ld, 16)

            @block.gpsimd
            def _(pool):
                nc.gpsimd.memset(ident[:, :], 0.0).then_inc(made, 1)
                nc.gpsimd.memset(mask[:, :], 0.0).then_inc(made, 1)
                pool.wait_ge(made, 2)
                nc.gpsimd.affine_select(out=ident[:, :], in_=ident[:, :], compare_op=ALU.not_equal, fill=1.0,
                                        base=0, pattern=[[-1, P]], channel_multiplier=1).then_inc(made, 1)
                nc.gpsimd.affine_select(out=mask[:, :], in_=mask[:, :], compare_op=ALU.is_ge, fill=MASKED,
                                        base=0, pattern=[[-1, P]], channel_multiplier=1).then_inc(made, 1)
                pool.wait_ge(made, 4)
                nc.gpsimd.tensor_copy(identr[:, :], ident[:, :])
                nc.gpsimd.tensor_copy(maskr[:, :], mask[:, :])

        attention_a(nc, X, xh, xl, ident, identr, maskr, PS, d)
        experts(nc, "e1", X, xh, xl, PS, d, ident, cw_dram[0])
        attention_b(nc, X, xh, xl, ident, PS, d)
        experts(nc, "e2", X, xh, xl, PS, d, ident, cw_dram[1])
        with nc.Block() as block:
            @block.sync
            def _(sp):
                sp.dma_start(out.rearrange("b (t p) e -> p (b t) e", p=P), X[:, :, :]).then_inc(st, 16)
                sp.wait_ge(st, 16)


def lay_out(np, i):
    g = lambda n: np.ascontiguousarray(i[n])
    a = {"x": g("L0_attn_a_x")}
    swap = np.arange(E) ^ 1
    wq, wk = g("L0_attn_a_W_q"), g("L0_attn_a_W_k")
    a["a_w"] = np.stack([wq, wq[:, swap], wk, wk[:, swap], g("L0_attn_a_W_v")])
    a["a_wo"] = g("L0_attn_a_W_o")

    def table(dim, freq, sign, scale):
        inv = np.float32(1.0) / np.float32(10000.0) ** (np.arange(0, dim, 2, dtype=np.float32) / np.float32(dim))
        ang = np.arange(S, dtype=np.float32)[:, None] * inv[None, :].astype(np.float32)
        cos, sin = np.cos(ang).astype(np.float32).T[freq], np.sin(ang).astype(np.float32).T[freq]
        sin = sin * sign[:, None]
        return np.stack([cos * scale, sin * scale, cos, sin]).astype(np.float32)

    f = np.arange(P)
    a["a_tab"] = table(DA, (f % DA) // 2, np.where(f % 2 == 0, -1.0, 1.0).astype(np.float32),
                       np.float32(1.0 / np.sqrt(E)))
    a["b_tab"] = table(DB, f % (DB // 2), np.where(f % DB < DB // 2, -1.0, 1.0).astype(np.float32),
                       np.float32(DB ** -0.5))
    HF = HB * DB
    ff = np.arange(HF)
    turn = (ff // DB) * DB + (ff + DB // 2) % DB
    kinds = [g("L0_attn_b_Wq"), g("L0_attn_b_Wq")[turn], g("L0_attn_b_Wk"), g("L0_attn_b_Wk")[turn]]
    a["b_wqk"] = np.stack([w.reshape(HB // 2, P, E) for w in kinds]).transpose(3, 1, 0, 2)
    bias = [g("L0_attn_b_bq"), g("L0_attn_b_bq")[turn], g("L0_attn_b_bk"), g("L0_attn_b_bk")[turn]]
    a["b_bqk"] = np.stack([w.reshape(HB // 2, P) for w in bias]).transpose(2, 1, 0)
    a["b_wv"] = g("L0_attn_b_Wv").T
    a["b_bv"] = g("L0_attn_b_bv").reshape(1, HF)
    wo = g("L0_attn_b_Wo").reshape(E, HB, DB).transpose(2, 1, 0)
    a["b_wo"] = np.concatenate([wo, wo])
    a["b_bo"] = g("L0_attn_b_bo").reshape(1, E)
    w1 = np.concatenate([g("L0_ffn_sw1"), g("L0_ffn_w1")]).transpose(0, 2, 1)
    w3 = np.concatenate([g("L0_ffn_sw3"), g("L0_ffn_w3")]).transpose(0, 2, 1)
    w2 = np.concatenate([g("L0_ffn_sw2"), g("L0_ffn_w2")]).transpose(0, 2, 1)
    a["f_w"] = np.concatenate([w1, w3, w2[:, 0:P], w2[:, P:HID]], axis=2)
    a["router"] = g("L0_ffn_router_w").T
    a["ebias"] = g("L0_ffn_expert_bias").reshape(1, NE)
    a["rank"] = np.arange(NE, 0, -1, dtype=np.float32).reshape(1, NE)
    return {n: np.ascontiguousarray(v) for n, v in a.items()}


def kernel(**inputs):
    import numpy as _np
    import concourse.bacc as _bacc
    from concourse import mybir as _mybir
    from concourse.bass_utils import run_bass_kernel_spmd as _run

    nc = _bacc.Bacc("TRN2", target_bir_lowering=False, num_devices=1)
    arrays = {f"in_{n}": v for n, v in lay_out(_np, {k: _np.asarray(v) for k, v in inputs.items()}).items()}
    d = {n[3:]: nc.dram_tensor(n, v.shape, _mybir.dt.from_np(v.dtype), kind="ExternalInput").ap()
         for n, v in arrays.items()}
    out = nc.dram_tensor("out", (B, S, E), _mybir.dt.float32, kind="ExternalOutput").ap()
    program(nc, d, out)
    r = _run(nc, [arrays], core_ids=[0])
    return r.results[0]["out"]
```
